# Optimizing a Trainium2 kernel written in Bass

```python
import numpy as np
import jax
import jax.numpy as jnp

def _softmax(x, axis=-1):
    return jax.nn.softmax(x, axis=axis)

def _gelu(x):
    return jax.nn.gelu(x, approximate=True)

def _silu(x):
    return jax.nn.silu(x)

def _sigmoid(x):
    return jax.nn.sigmoid(x)

def _layernorm(x, axis=-1, eps=1e-05):
    m = jnp.mean(x, axis=axis, keepdims=True)
    v = jnp.var(x, axis=axis, keepdims=True)
    return (x - m) / jnp.sqrt(v + eps)

def _scatter_add(tgt, idx, src, axis=0):
    return tgt.at[idx].add(src)

def _segment_sum(src, seg, n):
    return jax.ops.segment_sum(src, seg, n)
kernel_name = 'mk_vit_tower_postln_d1_tok_img768_r4_9994be'

def setup_inputs(seed: int=0):
    np.random.seed(seed)
    _w = jnp.asarray

    def _rec_inputs():
        import jax
        import jax.numpy as jnp
        _rk = jax.random.key(seed)
        x = -0.00040386 + 0.999972 * jax.random.normal(jax.random.fold_in(_rk, 1), (64, 3, 128, 128), jnp.float32)
        return x
    x = _rec_inputs()

    def _L0_tok_setup():
        import jax, jax.numpy as jnp
        import numpy as np
        P = 16
        WIN = 64
        NH = 12

        def _layernorm(x, g, b, eps=1e-05):
            m = x.mean(-1, keepdims=True)
            v = ((x - m) ** 2).mean(-1, keepdims=True)
            return (x - m) * jax.lax.rsqrt(v + eps) * g + b

        def _sinusoidal_pe(n, d):
            pos = jnp.arange(n, dtype=jnp.float32)[:, None]
            i = jnp.arange(d // 2, dtype=jnp.float32)[None, :]
            ang = pos / jnp.power(10000.0, 2.0 * i / d)
            pe = jnp.zeros((n, d), jnp.float32)
            pe = pe.at[:, 0::2].set(jnp.sin(ang)).at[:, 1::2].set(jnp.cos(ang))
            return pe
        key = jax.random.key(seed)
        ks = jax.random.split(key, 8)
        B, C, H, W, D, F = (16, 3, 128, 128, 192, 768)
        s = lambda k, shape: jax.random.normal(k, shape, jnp.float32) * 0.02
        return {'input': jax.random.normal(ks[0], (B, C, H, W), jnp.float32), 'patch_w': s(ks[1], (D, C, P, P)), 'patch_b': jnp.zeros((D,), jnp.float32), 'ln_g': jnp.ones((D,), jnp.float32), 'ln_b': jnp.zeros((D,), jnp.float32), 'qkv_w': s(ks[2], (D, 3 * D)), 'qkv_b': jnp.zeros((3 * D,), jnp.float32), 'proj_w': s(ks[3], (D, D)), 'proj_b': jnp.zeros((D,), jnp.float32), 'ff1_w': s(ks[4], (D, F)), 'ff1_b': jnp.zeros((F,), jnp.float32), 'ff2_w': s(ks[5], (F, D)), 'ff2_b': jnp.zeros((D,), jnp.float32)}
    _L0_tok_all = _L0_tok_setup()
    _L0_tok_in = {k: v for k, v in _L0_tok_all.items() if k in ('patch_w', 'patch_b', 'ln_g', 'ln_b', 'qkv_w', 'qkv_b', 'proj_w', 'proj_b', 'ff1_w', 'ff1_b', 'ff2_w', 'ff2_b')}
    del _L0_tok_all

    def _L0_attn_setup():
        import jax, jax.numpy as jnp
        import numpy as np
        DIM = 192
        GP_NUM = 49
        key = jax.random.key(seed)
        ks = jax.random.split(key, 7)
        b, n, d = (16, 256, DIM)
        s = d ** (-0.5)
        x = jax.random.normal(ks[0], (b, n, d), dtype=jnp.float32)
        W_qkv = jax.random.normal(ks[1], (d, 3 * d), dtype=jnp.float32) * s
        b_qkv = jnp.zeros((3 * d,), dtype=jnp.float32)
        W_proj = jax.random.normal(ks[2], (d, d), dtype=jnp.float32) * s
        b_proj = jnp.zeros((d,), dtype=jnp.float32)
        W_gp = jax.random.normal(ks[3], (d, GP_NUM), dtype=jnp.float32) * s
        alpha = jnp.zeros((1,), dtype=jnp.float32)
        return {'x': x, 'W_qkv': W_qkv, 'b_qkv': b_qkv, 'W_proj': W_proj, 'b_proj': b_proj, 'W_gp': W_gp, 'alpha': alpha}
    _L0_attn_all = _L0_attn_setup()
    _L0_attn_in = {k: v for k, v in _L0_attn_all.items() if k in ('W_qkv', 'b_qkv', 'W_proj', 'b_proj', 'W_gp', 'alpha')}
    del _L0_attn_all

    def _L0_ffn_setup():
        import jax, jax.numpy as jnp
        import numpy as np
        DIM = 192
        MOE_INTER = 512
        N_EXPERTS = 16
        TOP_K = 2
        SHARED_INTER = 2 * 512
        ROUTE_SCALE = 1.0
        B, S = (8, 196)
        key = jax.random.key(seed)
        ks = jax.random.split(key, 8)
        sc = 0.02
        return {'x': jax.random.normal(ks[0], (B, S, DIM), jnp.float32), 'gate_w': jax.random.normal(ks[1], (N_EXPERTS, DIM), jnp.float32) * sc, 'w1': jax.random.normal(ks[2], (N_EXPERTS, MOE_INTER, DIM), jnp.float32) * sc, 'w2': jax.random.normal(ks[3], (N_EXPERTS, DIM, MOE_INTER), jnp.float32) * sc, 'w3': jax.random.normal(ks[4], (N_EXPERTS, MOE_INTER, DIM), jnp.float32) * sc, 'sw1': jax.random.normal(ks[5], (SHARED_INTER, DIM), jnp.float32) * sc, 'sw2': jax.random.normal(ks[6], (DIM, SHARED_INTER), jnp.float32) * sc, 'sw3': jax.random.normal(ks[7], (SHARED_INTER, DIM), jnp.float32) * sc}
    _L0_ffn_all = _L0_ffn_setup()
    _L0_ffn_in = {k: v for k, v in _L0_ffn_all.items() if k in ('gate_w', 'w1', 'w2', 'w3', 'sw1', 'sw2', 'sw3')}
    del _L0_ffn_all
    return {'x': x, 'L0_tok_patch_w': _L0_tok_in['patch_w'], 'L0_tok_patch_b': _L0_tok_in['patch_b'], 'L0_tok_ln_g': _L0_tok_in['ln_g'], 'L0_tok_ln_b': _L0_tok_in['ln_b'], 'L0_tok_qkv_w': _L0_tok_in['qkv_w'], 'L0_tok_qkv_b': _L0_tok_in['qkv_b'], 'L0_tok_proj_w': _L0_tok_in['proj_w'], 'L0_tok_proj_b': _L0_tok_in['proj_b'], 'L0_tok_ff1_w': _L0_tok_in['ff1_w'], 'L0_tok_ff1_b': _L0_tok_in['ff1_b'], 'L0_tok_ff2_w': _L0_tok_in['ff2_w'], 'L0_tok_ff2_b': _L0_tok_in['ff2_b'], 'L0_attn_W_qkv': _L0_attn_in['W_qkv'], 'L0_attn_b_qkv': _L0_attn_in['b_qkv'], 'L0_attn_W_proj': _L0_attn_in['W_proj'], 'L0_attn_b_proj': _L0_attn_in['b_proj'], 'L0_attn_W_gp': _L0_attn_in['W_gp'], 'L0_attn_alpha': _L0_attn_in['alpha'], 'L0_ffn_gate_w': _L0_ffn_in['gate_w'], 'L0_ffn_w1': _L0_ffn_in['w1'], 'L0_ffn_w2': _L0_ffn_in['w2'], 'L0_ffn_w3': _L0_ffn_in['w3'], 'L0_ffn_sw1': _L0_ffn_in['sw1'], 'L0_ffn_sw2': _L0_ffn_in['sw2'], 'L0_ffn_sw3': _L0_ffn_in['sw3']}

def reference(x, L0_tok_patch_w, L0_tok_patch_b, L0_tok_ln_g, L0_tok_ln_b, L0_tok_qkv_w, L0_tok_qkv_b, L0_tok_proj_w, L0_tok_proj_b, L0_tok_ff1_w, L0_tok_ff1_b, L0_tok_ff2_w, L0_tok_ff2_b, L0_attn_W_qkv, L0_attn_b_qkv, L0_attn_W_proj, L0_attn_b_proj, L0_attn_W_gp, L0_attn_alpha, L0_ffn_gate_w, L0_ffn_w1, L0_ffn_w2, L0_ffn_w3, L0_ffn_sw1, L0_ffn_sw2, L0_ffn_sw3):
    import jax
    import jax.numpy as jnp

    def _L0_tok_ref(input, patch_w, patch_b, ln_g, ln_b, qkv_w, qkv_b, proj_w, proj_b, ff1_w, ff1_b, ff2_w, ff2_b):
        import jax, jax.numpy as jnp
        import numpy as np
        P = 16
        WIN = 64
        NH = 12

        def _layernorm(x, g, b, eps=1e-05):
            m = x.mean(-1, keepdims=True)
            v = ((x - m) ** 2).mean(-1, keepdims=True)
            return (x - m) * jax.lax.rsqrt(v + eps) * g + b

        def _sinusoidal_pe(n, d):
            pos = jnp.arange(n, dtype=jnp.float32)[:, None]
            i = jnp.arange(d // 2, dtype=jnp.float32)[None, :]
            ang = pos / jnp.power(10000.0, 2.0 * i / d)
            pe = jnp.zeros((n, d), jnp.float32)
            pe = pe.at[:, 0::2].set(jnp.sin(ang)).at[:, 1::2].set(jnp.cos(ang))
            return pe
        B, C, H, W = input.shape
        D = patch_w.shape[0]
        dh = D // NH
        xp = input.reshape(B, C, H // P, P, W // P, P)
        x = jnp.einsum('bchpwq,dcpq->bhwd', xp, patch_w) + patch_b
        x = x.reshape(B, -1, D)
        x = _layernorm(x, ln_g, ln_b)
        N = x.shape[1]
        x = x + _sinusoidal_pe(N, D)

        def ff(y):
            return jax.nn.gelu(y @ ff1_w + ff1_b) @ ff2_w + ff2_b

        def sparse_attn(y):
            nW = N // WIN
            qkv = (y @ qkv_w + qkv_b).reshape(B, nW, WIN, 3, NH, dh)
            q, k, v = (qkv[:, :, :, 0], qkv[:, :, :, 1], qkv[:, :, :, 2])
            scores = jnp.einsum('bwqhd,bwkhd->bwhqk', q, k) * dh ** (-0.5)
            a = jax.nn.softmax(scores, axis=-1)
            o = jnp.einsum('bwhqk,bwkhd->bwqhd', a, v).reshape(B, N, D)
            return o @ proj_w + proj_b
        identity = x
        x = ff(x)
        x = sparse_attn(x)
        x = x + identity
        identity = x
        x = ff(x)
        x = x + identity
        return x

    def _L0_attn_ref(x, W_qkv, b_qkv, W_proj, b_proj, W_gp, alpha):
        import jax, jax.numpy as jnp
        import numpy as np
        DIM = 192
        GP_NUM = 49
        d = x.shape[-1]
        scale = d ** (-0.5)
        qkv = x @ W_qkv + b_qkv
        q, k, v = jnp.split(qkv, 3, axis=-1)
        scores = jnp.einsum('bnd,bmd->bnm', q, k) * scale
        attn = jax.nn.softmax(scores, axis=-1)
        gw = jax.nn.softmax(q @ W_gp, axis=-1)
        group = jnp.einsum('bng,bmg->bnm', gw, gw)
        a = jax.nn.sigmoid(alpha)
        weights = attn * (a + (1.0 - a) * group)
        out = jnp.einsum('bnm,bmd->bnd', weights, v)
        return out @ W_proj + b_proj

    def _L0_ffn_ref(x, gate_w, w1, w2, w3, sw1, sw2, sw3):
        import jax, jax.numpy as jnp
        import numpy as np
        DIM = 192
        MOE_INTER = 512
        N_EXPERTS = 16
        TOP_K = 2
        SHARED_INTER = 2 * 512
        ROUTE_SCALE = 1.0
        B, S = (8, 196)
        Bb, Ss, D = x.shape
        xf = x.reshape(-1, D)
        T = xf.shape[0]
        scores = jax.nn.softmax(xf @ gate_w.T, axis=-1)
        topw, topi = jax.lax.top_k(scores, TOP_K)
        topw = topw * ROUTE_SCALE
        comb = jnp.zeros((T, N_EXPERTS), xf.dtype).at[jnp.arange(T)[:, None], topi].set(topw)
        h = jax.nn.silu(jnp.einsum('td,eid->tei', xf, w1)) * jnp.einsum('td,eid->tei', xf, w3)
        h = h * comb[:, :, None]
        y = jnp.einsum('tei,edi->td', h, w2)
        z = jax.nn.silu(xf @ sw1.T) * (xf @ sw3.T) @ sw2.T
        return (y + z).reshape(Bb, Ss, D)
    h = _L0_tok_ref(x, L0_tok_patch_w, L0_tok_patch_b, L0_tok_ln_g, L0_tok_ln_b, L0_tok_qkv_w, L0_tok_qkv_b, L0_tok_proj_w, L0_tok_proj_b, L0_tok_ff1_w, L0_tok_ff1_b, L0_tok_ff2_w, L0_tok_ff2_b)
    h = _layernorm(h + _L0_attn_ref(h, L0_attn_W_qkv, L0_attn_b_qkv, L0_attn_W_proj, L0_attn_b_proj, L0_attn_W_gp, L0_attn_alpha), axis=-1)
    h = _layernorm(h + _L0_ffn_ref(h, L0_ffn_gate_w, L0_ffn_w1, L0_ffn_w2, L0_ffn_w3, L0_ffn_sw1, L0_ffn_sw2, L0_ffn_sw3), axis=-1)
    return h

_drawn_inputs = setup_inputs


def setup_inputs(seed=0):
    import zlib

    import numpy as np

    out = dict(_drawn_inputs(seed))
    spreads = {'L0_tok_patch_b': (0.0, 0.1),
     'L0_tok_ln_g': (1.0, 0.2),
     'L0_tok_ln_b': (0.0, 0.1),
     'L0_tok_qkv_b': (0.0, 0.339),
     'L0_tok_proj_b': (0.0, 0.1),
     'L0_tok_ff1_b': (0.0, 0.281),
     'L0_tok_ff2_b': (0.0, 0.1),
     'L0_attn_b_qkv': (0.0, 0.1),
     'L0_attn_b_proj': (0.0, 0.1)}
    factors = {'L0_tok_qkv_w': 6.019,
     'L0_attn_W_gp': 8.0,
     'L0_ffn_gate_w': 8.0,
     'L0_ffn_w1': 8.0,
     'L0_ffn_w2': 8.0,
     'L0_ffn_w3': 8.0,
     'L0_ffn_sw1': 8.0,
     'L0_ffn_sw2': 8.0,
     'L0_ffn_sw3': 8.0}
    for name, (base, spread) in spreads.items():
        noise = np.random.default_rng([zlib.crc32(name.encode()), seed]).standard_normal(out[name].shape)
        drawn = base * np.exp(spread * noise) if base else spread * noise
        out[name] = jnp.asarray(drawn.astype(out[name].dtype))
    for name, factor in factors.items():
        out[name] = (out[name] * factor).astype(out[name].dtype)
    return out
```

```python
from contextlib import ExitStack

import numpy as np

import concourse.bass as bass
from concourse import mybir

F32 = mybir.dt.float32
I32 = mybir.dt.int32
U32 = mybir.dt.uint32
ALU = mybir.AluOpType
ACT = mybir.ActivationFunctionType
AX = mybir.AxisListType.X

P = 128
IMAGES, CH, SIDE, PATCH = 64, 3, 128, 16
GRID = SIDE // PATCH
WIN = GRID * GRID
TOK = IMAGES * WIN
D = 192
DM, DT = P, D - P
PK = CH * PATCH * PATCH // P
TT = 512
NT = TOK // TT
IPT = TT // WIN
BPT = TT // P
NB = TOK // P
FF = 768
FC = FF // P
NH, DH = 12, 16
HM = DM // DH
GP = 49
NE, MI = 16, 512
SI = 1024
SC = SI // P
ROW = D + 4
ET = TOK * 2 // P + NE - 1
EPS = 1e-5
EW = 2 * MI + MI + (MI // P) * D

_C = {}
_at = 0
for _name, _n in (("ident", P), ("before", P), ("ones", P), ("kmask", HM), ("vmask", D), ("pe", D),
                  ("experts", NE), ("tiles", ET), ("padrow", ROW), ("token", NB)):
    _C[_name] = slice(_at, _at + _n)
    _at += _n
CONST = _at
_B = {}
_at = 0
for _name, _n in (("ff1", FC), ("ff2", 2), ("q", 2), ("k", 2), ("v", 2), ("proj", 2), ("q2", 2), ("k2", 2)):
    _B[_name] = slice(_at, _at + _n)
    _at += _n
BCOLS = _at


class Signal:

    def __init__(self, sem, depth, per=1, first=0):
        self.sem, self.depth, self.per, self.first = sem, depth, per, first

    def start(self, engine):
        engine.sem_inc(self.sem, self.depth * self.per)

    def done(self, item, part=None):
        return (item - self.first + self.depth) * self.per + (self.per if part is None else part + 1)

    def recycled(self, item):
        return (item - self.first) * self.per + self.per


class Chain:

    def __init__(self, engine, sem, base):
        self.engine, self.sem, self.base, self.n = engine, sem, base, 0

    def __call__(self, instruction):
        self.n += 1
        instruction.then_inc(self.sem, 1)

    def join(self):
        self.engine.wait_ge(self.sem, self.base + self.n)


NEWTON = 3
RSQRT_STEPS = 3 + 3 * NEWTON


def rsqrt(dve, chain, out, var, tmp):
    chain(dve.tensor_scalar(var, var, EPS, None, ALU.add))
    chain.join()
    chain(dve.tensor_scalar(tmp.bitcast(I32), var.bitcast(I32), 1, None, ALU.logical_shift_right))
    chain.join()
    chain(dve.tensor_scalar(out.bitcast(I32), tmp.bitcast(I32), -1.0, float(0x5F3759DF), ALU.mult, ALU.add))
    chain.join()
    for _ in range(NEWTON):
        chain(dve.tensor_tensor(tmp, out, out, ALU.mult))
        chain.join()
        chain(dve.scalar_tensor_tensor(out=tmp, in0=tmp, scalar=-0.5, in1=var, op0=ALU.mult, op1=ALU.mult))
        chain.join()
        chain(dve.scalar_tensor_tensor(out=out, in0=tmp, scalar=1.5, in1=out, op0=ALU.add, op1=ALU.mult))
        chain.join()


def norm_steps(n):
    return 2 * n + RSQRT_STEPS


def norm_stats(dve, chain, rows, stats, mv, rstd, tmp, met):
    for j, row in enumerate(rows):
        chain(dve.bn_stats(stats[:, j, :], row))
    chain.join()
    dve.sem_inc(met, 1)
    for j in range(len(rows)):
        chain(dve.bn_aggr(mv[:, j, :], stats[:, j, :]))
    chain.join()
    rsqrt(dve, chain, rstd, mv[:, :, 1], tmp)


def build(nc, d, out):
    XS = nc.dram_tensor("sorted_rows", (ET * P, ROW), F32).ap()
    ACC = nc.dram_tensor("acc_rows", (TOK + P, D), F32).ap()

    with ExitStack() as ctx:
        MEM = 53200
        mem = ctx.enter_context(nc.sbuf_tensor("mem", [P, MEM], F32))[:, :]
        PS = ctx.enter_context(nc.psum_tensor("PS", [P, 8, 512], F32))

        def sem(name):
            return ctx.enter_context(nc.semaphore(name))

        def signal(name, depth, per=1, first=0):
            return Signal(sem(name), depth, per, first)

        class Region:
            def __init__(self, lo, hi):
                self.at, self.hi = lo, hi

            def __call__(self, n, **shape):
                a = mem[:, self.at:self.at + n]
                self.at += n
                assert self.at <= self.hi, (self.at, self.hi)
                if not shape:
                    return a
                keys = list(shape)
                return a.rearrange(f"p ({' '.join(keys)} n) -> p {' '.join(keys)} n", **shape)

        EXPERTS = NE * EW
        SHW = (NE - 1) * EW
        H2 = SHW + 3 * SI + SC * D
        SHWORK = H2 + NB * ROW
        CONSTS = MEM - 1500

        early = Region(0, SHW)
        XT = early(2 * TOK, k=2)
        YT = early(2 * TOK, k=2)
        wpatch = early(PK * D, c=PK)
        wff1 = early(2 * FF, k=2)
        wff2 = early(FC * D, c=FC)
        wqkv = early(2 * 3 * D, k=2)
        wproj = early(2 * D, k=2)
        wqkv2 = early(2 * 3 * D, k=2)
        wproj2 = early(2 * D, k=2)
        wgp = early(2 * GP, k=2)
        wgate = early(2 * NE, k=2)
        rows5 = early(5 * D, r=5)
        bias_pe = early(D)
        WORK = early.at
        work = Region(WORK, CONSTS)
        patches = work(2 * PK * TT, b=2, c=PK)
        xw = work(2 * BPT * D, b=2, j=BPT)
        work = Region(WORK, CONSTS)
        hid = work(3 * TT, b=3)
        work = Region(WORK, CONSTS)
        yd = work(2 * IPT * 2 * WIN, k=2, i=IPT, r=2)
        qT = work(2 * TT, k=2)
        kT = work(2 * TT, k=2)
        kbd = work(IPT * NH * WIN, i=IPT, h=NH)
        vbd = work(2 * IPT * D, b=2, i=IPT)
        E = work(2 * NH * WIN, b=2)
        ETb = work(2 * NH * WIN, b=2)
        oT = work(2 * TT, k=2)
        work = Region(WORK, SHW)
        hs = work(2 * 2 * TT, b=2, k=2)
        q2 = work(2 * TT, k=2)
        k2 = work(2 * TT, k=2)
        v2 = work(2 * BPT * D, b=2, j=BPT)
        sE = work(BPT * WIN, j=BPT)
        lE = work(BPT * GP, j=BPT)
        gT = work(TT)
        t1 = work(BPT * WIN, j=BPT)
        wb = work(BPT * P, j=BPT)
        wT = work(TT)
        oT2 = work(2 * TT, k=2)
        work = Region(SHWORK, CONSTS)
        zw = work(BPT * D, j=BPT)
        hT2 = work(2 * TT, k=2)
        LG = work(NB * NE, b=NB)
        work = Region(WORK, SHW)
        R = [work(NB * NE, b=NB) for _ in range(8)]
        r1 = [work(NB) for _ in range(8)]
        re = [work(NE) for _ in range(8)]
        tmap = work(ET * NE, j=ET)
        work = Region(SHW, H2)
        shw13 = work(2 * SI)
        shwt = work(SI)
        shw2 = work(SC * D, c=SC)
        H2X = Region(H2, SHWORK)(NB * ROW, b=NB)
        work = Region(SHWORK, CONSTS)
        sxT = work(4 * TT, b=2, k=2)
        shx = work(BPT * D, j=BPT)
        sil = work(2 * TT, b=2)
        gg = work(2 * TT, b=2)
        zo = work(BPT * D, j=BPT)
        work = Region(H2, SHWORK)
        xg = work(2 * ROW, b=2)
        exT = work(2 * 3 * P, b=2, k=3)
        esil = work(2 * MI, b=2)
        eg = work(2 * MI, b=2)
        egT = work(2 * MI, b=2)
        ey = work(2 * D, b=2)
        egate = work(2 * 4, b=2)
        work = Region(0, SHW)
        fin = work(NT * BPT * D, t=NT, j=BPT)
        fout = work(NT * BPT * D, t=NT, j=BPT)
        work = Region(CONSTS, MEM)
        const = work(CONST)
        bcols = work(BCOLS)
        stats = work(24, j=4)
        mv = work(8, j=4)
        rstd, tmp4 = work(4), work(4)
        mix = work(4)
        alpha = work(1)
        mx12, sm12 = work(2 * NH, b=2), work(2 * NH, b=2)
        mxS, smS, mxL, smL = work(4), work(4), work(4), work(4)
        posi = work(2 * NB, s=2).bitcast(I32)
        emap = work(ET).bitcast(I32)
        emapf = work(ET)
        tokidx = work(2).bitcast(I32)

        def c(name):
            return const[:, _C[name]]

        def bc(name, k, rows=P):
            return bcols[0:rows, _B[name]][:, k:k + 1]

        ident, kmask = c("ident"), c("kmask")
        KROWS = (P, DT)


        early_in, late_in, shared_in, experts_in, lastw_in = (
            sem("early_weights_loaded"), sem("row_constants_loaded"), sem("shared_weights_loaded"),
            sem("expert_weights_loaded"), sem("last_expert_loaded"))
        table_filled, dummies_filled = sem("sorted_rows_filled"), sem("dummy_rows_filled")
        consts_ready, bias_ready = sem("mix_ready"), sem("position_bias_ready")
        exp_alpha = sem("exp_alpha")

        patch_in = [sem("patches_in0"), sem("patches_in1")]
        em_mm, em_raw, em_norm = signal("embed_products", 2), signal("embed_raw", 2, 2), signal("embed_normed", 2, BPT)
        em_mul, em_tok = signal("embed_scaled", 2), signal("embed_tokens", 2)
        em_tr, em_xt = signal("embed_transposed", 2), signal("embed_xt", 2, 2)
        em_chain = sem("embed_chain")

        ffs = []
        for which in "ab":
            ffs.append({n: signal(f"ff_{which}_{n}", depth, per) for n, depth, per in
                        (("up", 3, 1), ("gelu", 3, 1), ("down", 3, 1), ("out", 2, 2))})

        w_yd, w_fill, w_drain = signal("win_y_copied", 1, 4), signal("win_ring_filled", 2, 1, -2), signal("win_ring_drained", 2, 1, -2)
        w_kbd = signal("win_k_spread", 4, 4)
        w_s, w_mx, w_sub, w_exp = (signal(f"win_{n}", 2) for n in ("scores", "max", "shifted", "exp"))
        w_sum, w_rs, w_norm = (signal(f"win_{n}", 2) for n in ("sum", "reciprocal", "weights"))
        w_tr, w_et, w_pv, w_o = (signal("win_transposed", 2), signal("win_turned", 2, 2),
                                 signal("win_values", 2), signal("win_heads_out", 1, 2))

        g_hs, g_fill, g_drain = signal("grp_h_copied", 2, 2), signal("grp_ring_filled", 2), signal("grp_ring_drained", 2)
        g_a = signal("grp_scores", 1, 2)
        g_mx, g_dif = signal("grp_max", 1, 2), signal("grp_shifted", 1, 2)
        g_exp, g_sum, g_gw = signal("grp_exp", 1, 2), signal("grp_sums", 1, 4), signal("grp_group_probs", 1, 2)
        g_gt, g_gtc, g_grp = signal("grp_probs_turned", 1), signal("grp_probs_copied", 1), signal("grp_group", 1)
        g_t1, g_wb = signal("grp_mix", 1), signal("grp_weights", 1, 2)
        g_wt, g_wtc, g_pv = signal("grp_weights_turned", 1), signal("grp_weights_copied", 1), signal("grp_values", 1)
        g_oc, g_z, g_raw = signal("grp_values_copied", 1, 2), signal("grp_rows", 1), signal("grp_rows_raw", 1, 2)
        g_norm, g_h2 = signal("grp_rows_normed", 1, BPT), signal("grp_rows_kept", 1)
        g_tr, g_ht = signal("grp_rows_turned", 1), signal("grp_rows_turned_copied", 1, 2)
        g_lg, g_lgc = signal("grp_logits", 1), signal("grp_logits_copied", 1)
        g_chain, wb_zero = sem("grp_chain"), sem("grp_weights_zeroed")

        r_chain, r_exp, r_pos, r_mask = sem("route_chain"), sem("route_exp"), sem("route_counts"), sem("route_chosen")
        r_done = sem("route_done")
        scat = [sem("scatter0"), sem("scatter1")]
        scattered = sem("scattered_tiles")

        s_x, s_tr, s_xt = signal("sh_rows", 1), signal("sh_turned", 2), signal("sh_x", 2, 3)
        s_up, s_silu, s_gg, s_dn = signal("sh_up", 2, 2), signal("sh_silu", 2), signal("sh_hidden", 2), signal("sh_down", 2)
        s_z, s_acc = signal("sh_out", 1, 2), sem("acc_rows_stored")

        e_in = [sem("ex_rows0"), sem("ex_rows1")]
        e_zero = sem("ex_pads_zeroed")
        e_tr, e_xt, e_h1, e_h3 = signal("ex_turned", 2), signal("ex_x", 2, 3), signal("ex_h1", 2), signal("ex_h3", 2)
        e_silu, e_g, e_gt, e_gtc = signal("ex_silu", 2), signal("ex_hidden", 2), signal("ex_hidden_turned", 2), signal("ex_hidden_copied", 2)
        e_y, e_ys, e_gate = signal("ex_y", 2), signal("ex_rows_out", 2), signal("ex_gates", 2, 5)
        e_acc = [sem("ex_add_landed0"), sem("ex_add_landed1")]
        e_added = signal("ex_added", 2)

        f_in = [sem(f"fin_in{n}") for n in range(NT)]
        f_chain, f_out, f_st = sem("fin_chain"), sem("fin_rows"), sem("fin_stored")

        met_dve, met_pe, met_pool = sem("waits_met_vector"), sem("waits_met_tensor"), sem("waits_met_pool")
        EARLY = 16
        N_EMBED = norm_steps(BPT)
        N_GROUP = norm_steps(BPT)
        N_FIN = norm_steps(BPT)
        last = NT - 1

        def kparts(weights, cols):
            return [weights[0:KROWS[k], k, cols] for k in range(2)]

        def halves(k):
            return slice(0, DM) if k == 0 else slice(DM, D)

        def win_ring_qkv(t):
            return 10 * t - 2

        def win_ring_proj(t, more):
            return 10 * t + (16 if more else 8)

        block = ctx.enter_context(nc.Block())

        @block.sync
        def _(sp):
            sp.sem_inc(s_acc, 16)
            sp.dma_start(const, d["const"]).then_inc(late_in, 16)
            sp.dma_start(rows5, d["rows5"].partition_broadcast(P)).then_inc(late_in, 16)
            sp.dma_start(alpha, d["alpha"].partition_broadcast(P)).then_inc(late_in, 16)
            sp.dma_start(bcols, d["bcols"]).then_inc(late_in, 16)
            sp.dma_start(wpatch, d["patch_w"]).then_inc(early_in, 16)

            with sp.Fori(0, NT // 2) as i:
                for b in range(2):
                    sp.wait_ge(em_mm.sem, em_mm.recycled(2 * i + b))
                    sp.dma_start(patches[:, b, :, :], d["patches"][bass.ds(2 * i + b, 1)]
                                 .rearrange("o p c n -> (o p) c n")).then_inc(patch_in[b], 16)

            sp.wait_ge(late_in, 64)
            sp.dma_start(XS.rearrange("(t p) n -> p t n", p=P),
                         c("padrow").unsqueeze(1).broadcast_to([P, ET, ROW])).then_inc(table_filled, 16)
            sp.dma_start(ACC[TOK:TOK + P, :], c("padrow")[:, 0:D]).then_inc(dummies_filled, 16)

            sp.wait_ge(w_drain.sem, w_drain.done(win_ring_proj(last, False) + 1))
            sp.dma_start(mem[:, SHW:H2], d["shared"]).then_inc(shared_in, 16)
            sp.wait_ge(r_done, 1)
            for e in range(NE - 1):
                sp.dma_start(mem[:, e * EW:(e + 1) * EW], d["experts"][e]).then_inc(experts_in, 16)
            with sp.Fori(0, NT) as t:
                sp.wait_ge(s_z.sem, s_z.done(t))
                sp.dma_start(ACC[bass.ds(t * TT, TT), :].rearrange("(j p) n -> p j n", p=P), zo).then_inc(s_acc, 16)
            sp.dma_start(mem[:, SHW:SHW + EW], d["experts"][NE - 1]).then_inc(lastw_in, 16)
            sp.wait_ge(scattered, NT)

            def rows_in(j, b):
                sp.wait_ge(e_tr.sem, e_tr.recycled(j))
                sp.wait_ge(e_gate.sem, e_gate.recycled(j))
                sp.dma_start(xg[:, b, :], XS[bass.ds(j * P, P), :]).then_inc(e_in[b], 16)

            with sp.Fori(0, ET // 2) as i:
                for b in range(2):
                    rows_in(2 * i + b, b)
            rows_in(ET - 1, (ET - 1) % 2)
            sp.wait_ge(e_added.sem, e_added.done(ET - 1))
            for t in range(NT):
                sp.dma_start(fin[:, t, :, :], ACC[t * TT:(t + 1) * TT, :]
                             .rearrange("(j p) n -> p j n", p=P)).then_inc(f_in[t], 16)
            for t in range(NT):
                sp.wait_ge(f_out, BPT * (t + 1))
                sp.dma_start(out[t * TT:(t + 1) * TT, :].rearrange("(j p) n -> p j n", p=P),
                             fout[:, t, :, :]).then_inc(f_st, 16)
            sp.wait_ge(f_st, 16 * NT)

        @block.tensor
        def _(pe):
            for s in (em_mm, em_tr, ffs[0]["up"], ffs[0]["down"], ffs[1]["up"], ffs[1]["down"], w_fill, w_s, w_tr, w_pv,
                      g_fill, g_a, g_gt, g_grp, g_wt, g_pv, g_z, g_tr, g_lg, s_tr, s_up, s_dn,
                      e_tr, e_h1, e_h3, e_gt, e_y):
                s.start(pe)
            pe.wait_ge(early_in, 16 * EARLY)
            pe.wait_ge(late_in, 64)

            def embed_mm(t, b, i):
                pe.wait_ge(patch_in[b], 16 * (i + 1))
                pe.wait_ge(em_raw.sem, em_raw.recycled(t))
                for j in range(BPT):
                    for k in range(PK):
                        mm = pe.matmul(PS[:, 2 * b + j // 2, D * (j % 2):D * (j % 2) + D],
                                       patches[:, b, k, P * j:P * j + P], wpatch[:, k, :],
                                       start=k == 0, stop=k == PK - 1)
                mm.then_inc(em_mm.sem, 1)

            def embed_tr(t, b):
                pe.wait_ge(em_tok.sem, em_tok.done(t))
                pe.wait_ge(em_xt.sem, em_xt.recycled(t))
                for j in range(BPT):
                    pe.transpose(PS[:, 4 + b, P * j:P * j + P], xw[:, b, j, 0:DM], ident)
                    tr = pe.transpose(PS[0:DT, 6 + b, P * j:P * j + P], xw[:, b, j, DM:D], ident)
                tr.then_inc(em_tr.sem, 1)

            embed_mm(0, 0, 0)
            with pe.Fori(0, NT // 2 - 1) as i:
                embed_mm(2 * i + 1, 1, i)
                embed_tr(2 * i, 0)
                embed_mm(2 * i + 2, 0, i + 1)
                embed_tr(2 * i + 1, 1)
            embed_mm(last, 1, NT // 2 - 1)
            embed_tr(last - 1, 0)
            embed_tr(last, 1)

            def feed_forward(s):
                with pe.Fori(0, NT // 2) as i:
                    for b in range(2):
                        t = 2 * i + b

                        def up(m):
                            pe.wait_ge(s["gelu"].sem, s["gelu"].recycled(FC * t + m))
                            w = kparts(wff1, slice(P * m, P * m + P))
                            for k in range(2):
                                mm = pe.matmul(PS[:, 4 + m % 3, :], w[k], XT[0:KROWS[k], k, bass.ds(t * TT, TT)],
                                               start=k == 0, stop=k == 1)
                            mm.then_inc(s["up"].sem, 1)

                        def down(m):
                            pe.wait_ge(s["gelu"].sem, s["gelu"].done(FC * t + m))
                            if m == 0:
                                pe.wait_ge(s["out"].sem, s["out"].recycled(t))
                            for k in range(2):
                                mm = pe.matmul(PS[0:KROWS[k], 2 * b + k, :], wff2[:, m, halves(k)],
                                               hid[:, m % 3, :], start=m == 0, stop=m == FC - 1)
                            mm.then_inc(s["down"].sem, 1)

                        up(0)
                        for m in range(1, FC):
                            up(m)
                            down(m - 1)
                        down(FC - 1)

            pe.wait_ge(em_raw.sem, em_raw.done(last))
            pe.wait_ge(em_xt.sem, em_xt.done(last))
            feed_forward(ffs[0])

            def win_qkv(t):
                n = win_ring_qkv(t)
                pe.wait_ge(w_yd.sem, w_yd.done(t))
                for u in range(4):
                    pe.wait_ge(w_drain.sem, w_drain.recycled(n + u))
                    lo, m = D * (u // 2) + DM * (u % 2), KROWS[u % 2]
                    w = kparts(wqkv, slice(lo, lo + m))
                    for k in range(2):
                        mm = pe.matmul(PS[0:m, 6 + u % 2, :].rearrange("p (i n) -> p i n", i=IPT), w[k],
                                       yd[0:KROWS[k], k, :, 0, :], start=k == 0, stop=k == 1)
                    mm.then_inc(w_fill.sem, 1)
                w = kparts(wqkv, slice(2 * D, 3 * D))
                for u in range(4, 8):
                    pe.wait_ge(w_drain.sem, w_drain.recycled(n + u))
                    for r in range(2):
                        img = 2 * (u - 4) + r
                        for k in range(2):
                            mm = pe.matmul(PS[:, 6 + u % 2, D * r:D * r + D],
                                           yd[0:KROWS[k], k, img, :, :].rearrange("p r n -> p (r n)"), w[k],
                                           start=k == 0, stop=k == 1)
                    mm.then_inc(w_fill.sem, 1)

            def win_scores(t, p):
                pair = 4 * t + p
                pe.wait_ge(w_drain.sem, w_drain.done(win_ring_qkv(t) + 1))
                pe.wait_ge(w_kbd.sem, w_kbd.done(pair))
                pe.wait_ge(w_sub.sem, w_sub.done(pair - 1))
                for r in range(2):
                    img = 2 * p + r
                    q = slice(WIN * img, WIN * img + WIN)
                    o = slice(WIN * r, WIN * r + WIN)
                    pe.matmul(PS[o, 0, :].rearrange("p (h n) -> p h n", n=WIN), qT[:, 0, q], kbd[:, img, 0:HM, :],
                              start=True, stop=True)
                    mm = pe.matmul(PS[o, 1, 0:(NH - HM) * WIN].rearrange("p (h n) -> p h n", n=WIN),
                                   qT[0:DT, 1, q], kbd[0:DT, img, HM:NH, :], start=True, stop=True)
                mm.then_inc(w_s.sem, 1)

            def win_turn(t, p):
                pair = 4 * t + p
                pe.wait_ge(w_norm.sem, w_norm.done(pair))
                pe.wait_ge(w_et.sem, w_et.done(pair - 1))
                for hp in range(NH // 2):
                    tr = pe.transpose(PS[:, 2 + hp // 4, P * (hp % 4):P * (hp % 4) + P],
                                      E[:, p % 2, P * hp:P * hp + P], ident)
                tr.then_inc(w_tr.sem, 1)

            def win_values(t, b, p):
                pair = 4 * t + p
                pe.wait_ge(w_et.sem, w_et.done(pair))
                pe.wait_ge(w_drain.sem, w_drain.done(win_ring_qkv(t) + 7))
                if p == 0:
                    pe.wait_ge(w_o.sem, w_o.done(t - 1))
                for r in range(2):
                    img = 2 * p + r
                    for hp in range(NH // 2):
                        o = 32 * (hp % 4)
                        mm = pe.matmul(PS[o:o + 32, 4 + hp // 4, WIN * img:WIN * img + WIN],
                                       vbd[:, b, img, 32 * hp:32 * hp + 32],
                                       ETb[:, p % 2, P * hp + WIN * r:P * hp + WIN * r + WIN],
                                       start=True, stop=True)
                mm.then_inc(w_pv.sem, 1)

            def win_proj(t, more):
                pe.wait_ge(w_o.sem, w_o.done(t))
                for u in range(2):
                    pe.wait_ge(w_drain.sem, w_drain.recycled(win_ring_proj(t, more) + u))
                    w = kparts(wproj, halves(u))
                    for k in range(2):
                        mm = pe.matmul(PS[0:KROWS[u], 6 + u, :], w[k], oT[0:KROWS[k], k, :],
                                       start=k == 0, stop=k == 1)
                    mm.then_inc(w_fill.sem, 1)

            def win_tile(t, b, more):
                win_scores(t, 0)
                win_scores(t, 1)
                win_turn(t, 0)
                win_scores(t, 2)
                win_values(t, b, 0)
                win_turn(t, 1)
                win_scores(t, 3)
                win_values(t, b, 1)
                if more:
                    win_qkv(t + 1)
                for p in (2, 3):
                    win_turn(t, p)
                    win_values(t, b, p)
                win_proj(t, more)

            pe.wait_ge(ffs[0]["out"].sem, ffs[0]["out"].done(last))
            pe.wait_ge(ffs[0]["gelu"].sem, ffs[0]["gelu"].done(FC * NT - 1))
            win_qkv(0)
            pe.wait_ge(w_fill.sem, w_fill.done(5))
            pe.sem_inc(w_fill.sem, 2)
            with pe.Fori(0, NT // 2 - 1) as i:
                for b in range(2):
                    win_tile(2 * i + b, b, True)
            win_tile(last - 1, 0, True)
            win_tile(last, 1, False)

            pe.wait_ge(w_drain.sem, w_drain.done(win_ring_proj(last, False) + 1))
            pe.wait_ge(w_sub.sem, w_sub.done(4 * last + 3))
            pe.wait_ge(w_o.sem, w_o.done(last))
            feed_forward(ffs[1])

            def grp_qk(t, b):
                n = 6 * t
                pe.wait_ge(g_hs.sem, g_hs.done(t))
                for u in range(4):
                    pe.wait_ge(g_drain.sem, g_drain.recycled(n + u))
                    lo, m = D * (u // 2) + DM * (u % 2), KROWS[u % 2]
                    w = kparts(wqkv2, slice(lo, lo + m))
                    for k in range(2):
                        mm = pe.matmul(PS[0:m, u % 2, :], w[k], hs[0:KROWS[k], b, k, :], start=k == 0, stop=k == 1)
                    mm.then_inc(g_fill.sem, 1)

            def grp_v(t, b):
                n = 6 * t
                w = kparts(wqkv2, slice(2 * D, 3 * D))
                for u in (4, 5):
                    pe.wait_ge(g_drain.sem, g_drain.recycled(n + u))
                    for r in range(2):
                        j = 2 * (u - 4) + r
                        for k in range(2):
                            mm = pe.matmul(PS[:, u % 2, D * r:D * r + D], hs[0:KROWS[k], b, k, P * j:P * j + P], w[k],
                                           start=k == 0, stop=k == 1)
                    mm.then_inc(g_fill.sem, 1)

            def grp_scores(t):
                pe.wait_ge(g_drain.sem, g_drain.done(6 * t + 3))
                for j in range(BPT):
                    for r in range(2):
                        a = slice(P * j + WIN * r, P * j + WIN * r + WIN)
                        for k in range(2):
                            mm = pe.matmul(PS[WIN * r:WIN * r + WIN, 2, WIN * j:WIN * j + WIN],
                                           q2[0:KROWS[k], k, a], k2[0:KROWS[k], k, a], start=k == 0, stop=k == 1)
                mm.then_inc(g_a.sem, 1)
                for j in range(BPT):
                    for k in range(2):
                        mm = pe.matmul(PS[:, 3, GP * j:GP * j + GP], q2[0:KROWS[k], k, P * j:P * j + P],
                                       wgp[0:KROWS[k], k, :], start=k == 0, stop=k == 1)
                mm.then_inc(g_a.sem, 1)

            def grp_turn_probs(t):
                pe.wait_ge(g_gw.sem, g_gw.done(t))
                pe.sem_inc(met_pe, 1)
                for j in range(BPT):
                    tr = pe.transpose(PS[0:GP, 4, P * j:P * j + P], lE[:, j, :], ident)
                tr.then_inc(g_gt.sem, 1)

            def grp_group(t):
                pe.wait_ge(g_gtc.sem, g_gtc.done(t))
                pe.sem_inc(met_pe, 1)
                for j in range(BPT):
                    for r in range(2):
                        a = slice(P * j + WIN * r, P * j + WIN * r + WIN)
                        mm = pe.matmul(PS[WIN * r:WIN * r + WIN, 5, WIN * j:WIN * j + WIN], gT[0:GP, a], gT[0:GP, a],
                                       start=True, stop=True)
                mm.then_inc(g_grp.sem, 1)

            def grp_turn_rows(t):
                pe.wait_ge(g_norm.sem, g_norm.done(t))
                for j in range(BPT):
                    pe.transpose(PS[:, 2, P * j:P * j + P], zw[:, j, 0:DM], ident)
                    tr = pe.transpose(PS[0:DT, 3, P * j:P * j + P], zw[:, j, DM:D], ident)
                tr.then_inc(g_tr.sem, 1)

            def grp_turn_weights(t):
                pe.wait_ge(g_wb.sem, g_wb.done(t))
                pe.wait_ge(g_ht.sem, g_ht.done(t - 1))
                for j in range(BPT):
                    tr = pe.transpose(PS[:, 3, P * j:P * j + P], wb[:, j, :], ident)
                tr.then_inc(g_wt.sem, 1)

            def grp_logits(t):
                pe.wait_ge(g_ht.sem, g_ht.done(t))
                for j in range(BPT):
                    for k in range(2):
                        mm = pe.matmul(PS[:, 6, NE * j:NE * j + NE], hT2[0:KROWS[k], k, P * j:P * j + P],
                                       wgate[0:KROWS[k], k, :], start=k == 0, stop=k == 1)
                mm.then_inc(g_lg.sem, 1)

            def grp_values(t, b):
                pe.wait_ge(g_wtc.sem, g_wtc.done(t))
                pe.wait_ge(g_drain.sem, g_drain.done(6 * t + 5))
                for k in range(2):
                    for j in range(BPT):
                        mm = pe.matmul(PS[0:KROWS[k], 4 + k, P * j:P * j + P], v2[:, b, j, halves(k)],
                                       wT[:, P * j:P * j + P], start=True, stop=True)
                mm.then_inc(g_pv.sem, 1)

            def grp_rows(t, b):
                pe.wait_ge(g_oc.sem, g_oc.done(t))
                pe.wait_ge(g_lgc.sem, g_lgc.done(t - 1))
                for j in range(BPT):
                    a = slice(P * j, P * j + P)
                    o, lo = PS[:, 6 + j // 2, :], D * (j % 2)
                    for k in range(2):
                        pe.matmul(o[:, lo:lo + D], oT2[0:KROWS[k], k, a], wproj2[0:KROWS[k], k, :],
                                  start=k == 0, stop=k == 1)
                    pe.matmul(o[:, lo:lo + DM], hs[:, b, 0, a], ident, start=False, stop=True, skip_group_check=True)
                    mm = pe.matmul(o[:, lo + DM:lo + D], hs[0:DT, b, 1, a], ident[0:DT, 0:DT], start=False, stop=True,
                                   skip_group_check=True)
                mm.then_inc(g_z.sem, 1)

            def grp_tile(t, b, first=False, final=False):
                grp_scores(t)
                if not final:
                    grp_qk(t + 1, 1 - b)
                grp_turn_probs(t)
                if not final:
                    grp_v(t + 1, 1 - b)
                grp_group(t)
                if not first:
                    grp_turn_rows(t - 1)
                grp_turn_weights(t)
                if not first:
                    grp_logits(t - 1)
                grp_values(t, b)
                grp_rows(t, b)

            pe.wait_ge(ffs[1]["out"].sem, ffs[1]["out"].done(last))
            pe.wait_ge(ffs[1]["gelu"].sem, ffs[1]["gelu"].done(FC * NT - 1))
            grp_qk(0, 0)
            grp_v(0, 0)
            grp_tile(0, 0, first=True)
            with pe.Fori(0, NT // 2 - 1) as i:
                grp_tile(2 * i + 1, 1)
                grp_tile(2 * i + 2, 0)
            grp_tile(last, 1, final=True)
            grp_turn_rows(last)
            grp_logits(last)

            pe.wait_ge(r_mask, 1)
            pe.wait_ge(g_lgc.sem, g_lgc.done(last))
            chosen, earlier = R[7].rearrange("p b n -> p (b n)"), R[5].rearrange("p b n -> p (b n)")
            pe.matmul(PS[:, 0, :], c("before"), chosen, start=True, stop=False)
            pe.matmul(PS[:, 0, :], c("ones"), earlier, start=False, stop=True)
            pe.matmul(PS[:, 1, 0:NE], c("ones"), R[4][:, NB - 1, :], start=True, stop=True).then_inc(r_pos, 1)

            def sh_turn(t, b):
                pe.wait_ge(s_x.sem, s_x.done(t))
                pe.wait_ge(s_xt.sem, s_xt.done(t - 1))
                for j in range(BPT):
                    pe.transpose(PS[:, 0, P * j:P * j + P], shx[:, j, 0:DM], ident)
                    tr = pe.transpose(PS[0:DT, 1, P * j:P * j + P], shx[:, j, DM:D], ident)
                tr.then_inc(s_tr.sem, 1)

            def sh_up(t, b, m):
                n = SC * t + m
                if m == 0:
                    pe.wait_ge(s_xt.sem, s_xt.done(t))
                pe.wait_ge(s_gg.sem, s_gg.recycled(n))
                for g in range(2):
                    o = PS[:, 2 + 2 * (m % 2) + g, :]
                    a = slice(64 * g, 64 * g + 64)
                    pe.matmul(o, shw13[:, SI * g + P * m:SI * g + P * m + P], sxT[:, b, 0, :], start=True, stop=False)
                    pe.matmul(o, shwt[a, P * m:P * m + P], sxT[a, b, 1, :], start=False, stop=True)\
                        .then_inc(s_up.sem, 1)

            def sh_down(t, m):
                n = SC * t + m
                pe.wait_ge(s_gg.sem, s_gg.done(n))
                if m == 0:
                    pe.wait_ge(s_z.sem, s_z.done(t - 1))
                for j in range(BPT):
                    mm = pe.matmul(PS[:, 6 + j // 2, D * (j % 2):D * (j % 2) + D], gg[:, m % 2, P * j:P * j + P],
                                   shw2[:, m, :], start=m == 0 and j % 2 == 0, stop=m == SC - 1,
                                   skip_group_check=True)
                mm.then_inc(s_dn.sem, 1)

            def sh_tile(t, b, more):
                sh_up(t, b, 0)
                for m in range(1, SC):
                    sh_up(t, b, m)
                    sh_down(t, m - 1)
                    if m == SC // 2 and more:
                        sh_turn(t + 1, 1 - b)
                sh_down(t, SC - 1)

            pe.wait_ge(shared_in, 16)
            pe.wait_ge(r_done, 1)
            sh_turn(0, 0)
            with pe.Fori(0, NT // 2 - 1) as i:
                for b in range(2):
                    sh_tile(2 * i + b, b, True)
            sh_tile(last - 1, 0, True)
            sh_tile(last, 1, False)

            def weights_at(j):
                return pe.value_load(emap[0:1, bass.ds(j, 1)], min_val=0, max_val=NE - 1) * EW

            def ex_turn(j, b, i):
                pe.wait_ge(e_in[b], 16 * (i + 1))
                pe.wait_ge(e_xt.sem, e_xt.done(j - 1))
                pe.transpose(PS[:, 4, 0:P], xg[:, b, 0:DM], ident)
                pe.transpose(PS[0:DT, 4, P:2 * P], xg[:, b, DM:D], ident).then_inc(e_tr.sem, 1)

            def ex_up(j, b, g, w):
                if g == 0:
                    pe.wait_ge(e_xt.sem, e_xt.done(j))
                    pe.wait_ge(e_silu.sem, e_silu.recycled(j))
                else:
                    pe.wait_ge(e_g.sem, e_g.recycled(j))
                o = PS[:, 2 * g + b, :]
                pe.matmul(o, exT[:, b, 0, :], mem[:, bass.ds(w + MI * g, MI)], start=True, stop=False)
                pe.matmul(o, exT[:, b, 1 + g, :], mem[:, bass.ds(w + 2 * MI, MI)], start=False, stop=True)\
                    .then_inc((e_h1, e_h3)[g].sem, 1)

            def ex_turn_hidden(j, b):
                pe.wait_ge(e_g.sem, e_g.done(j))
                pe.wait_ge(e_gtc.sem, e_gtc.done(j - 1))
                for q in range(MI // P):
                    tr = pe.transpose(PS[:, 5, P * q:P * q + P], eg[:, b, P * q:P * q + P], ident)
                tr.then_inc(e_gt.sem, 1)

            def ex_down(j, b, w):
                pe.wait_ge(e_gtc.sem, e_gtc.done(j))
                pe.wait_ge(e_ys.sem, e_ys.recycled(j))
                for q in range(MI // P):
                    mm = pe.matmul(PS[:, 6 + b, 0:D], egT[:, b, P * q:P * q + P],
                                   mem[:, bass.ds(w + 3 * MI + D * q, D)], start=q == 0, stop=q == MI // P - 1)
                mm.then_inc(e_y.sem, 1)

            def ex_step(j, b, i_next, first=False, final=False):
                w = weights_at(j)
                ex_up(j, b, 0, w)
                if not first:
                    ex_turn_hidden(j - 1, 1 - b)
                if not final:
                    ex_turn(j + 1, 1 - b, i_next)
                ex_up(j, b, 1, w)
                if not first:
                    ex_down(j - 1, 1 - b, weights_at(j - 1))

            pe.wait_ge(experts_in, 16 * (NE - 1))
            pe.wait_ge(lastw_in, 16)
            pe.wait_ge(s_z.sem, s_z.done(last))
            pe.wait_ge(s_gg.sem, s_gg.done(SC * NT - 1))
            ex_turn(0, 0, 0)
            ex_step(0, 0, 0, first=True)
            with pe.Fori(0, (ET - 3) // 2) as i:
                ex_step(2 * i + 1, 1, i + 1)
                ex_step(2 * i + 2, 0, i + 1)
            ex_step(ET - 2, 1, (ET - 1) // 2)
            ex_step(ET - 1, 0, 0, final=True)
            ex_turn_hidden(ET - 1, 0)
            ex_down(ET - 1, 0, weights_at(ET - 1))

        @block.scalar
        def _(act):
            for dst, name in ((wff1, "ff1_w"), (wff2, "ff2_w"), (wqkv, "qkv_w"), (wproj, "proj_w"),
                              (wqkv2, "qkv2_w"), (wproj2, "proj2_w"), (wgp, "gp_w"), (wgate, "gate_w")):
                if name == "ff2_w":
                    act.dma_start(dst, d[name]).then_inc(early_in, 16)
                    continue
                src = d[name]
                if name in ("ff1_w", "qkv_w", "qkv2_w"):
                    act.dma_start(dst[:, 0, :], src[0:DM, :]).then_inc(early_in, 16)
                    act.dma_start(dst[0:DT, 1, :], src[DM:D, :]).then_inc(early_in, 16)
                else:
                    act.dma_start(dst[:, 0, :], src[0:DM, :]).then_inc(early_in, 16)
                    act.dma_start(dst[0:DT, 1, :], src[DM:D, :]).then_inc(early_in, 16)
            act.wait_ge(late_in, 64)
            act.activation(mix[:, 0:1], alpha, ACT.Exp, scale=-1.0).then_inc(exp_alpha, 1)
            for s in (em_xt, ffs[0]["gelu"], ffs[1]["gelu"], w_exp, w_et, w_o, g_exp, g_gtc, g_wtc, g_oc, g_ht,
                      s_x, s_xt, s_silu, e_xt, e_silu, e_gtc):
                s.start(act)

            with act.Fori(0, NT // 2) as i:
                for b in range(2):
                    t = 2 * i + b
                    act.wait_ge(em_tr.sem, em_tr.done(t))
                    for k in range(2):
                        act.copy(XT[0:KROWS[k], k, bass.ds(t * TT, TT)], PS[0:KROWS[k], 4 + 2 * k + b, :])\
                            .then_inc(em_xt.sem, 1)

            def gelus(s):
                with act.Fori(0, NT) as t:
                    for m in range(FC):
                        n = FC * t + m
                        act.wait_ge(s["up"].sem, s["up"].done(n))
                        act.wait_ge(s["down"].sem, s["down"].recycled(n))
                        act.activation(hid[:, m % 3, :], PS[:, 4 + m % 3, :], ACT.Gelu_apprx_tanh,
                                       bias=bcols[:, _B["ff1"]][:, m:m + 1]).then_inc(s["gelu"].sem, 1)

            act.wait_ge(em_mm.sem, em_mm.done(last))
            act.wait_ge(em_raw.sem, em_raw.done(last))
            gelus(ffs[0])

            def win_exp(pair, p):
                act.wait_ge(w_sub.sem, w_sub.done(pair))
                act.activation(E[:, p % 2, :], E[:, p % 2, :], ACT.Exp).then_inc(w_exp.sem, 1)

            def win_turned(pair, p):
                act.wait_ge(w_tr.sem, w_tr.done(pair))
                act.wait_ge(w_pv.sem, w_pv.recycled(pair))
                act.copy(ETb[:, p % 2, 0:512], PS[:, 2, :]).then_inc(w_et.sem, 1)
                act.copy(ETb[:, p % 2, 512:], PS[:, 3, 0:NH * WIN - 512]).then_inc(w_et.sem, 1)

            with act.Fori(0, NT) as t:
                win_exp(4 * t, 0)
                win_exp(4 * t + 1, 1)
                win_turned(4 * t, 0)
                win_exp(4 * t + 2, 2)
                win_turned(4 * t + 1, 1)
                win_exp(4 * t + 3, 3)
                win_turned(4 * t + 2, 2)
                win_turned(4 * t + 3, 3)
                act.wait_ge(w_pv.sem, w_pv.done(4 * t + 3))
                for k in range(2):
                    act.activation(oT[0:KROWS[k], k, :], PS[0:KROWS[k], 4 + k, :], ACT.Identity,
                                   bias=bc("v", k, KROWS[k])).then_inc(w_o.sem, 1)
            act.wait_ge(w_drain.sem, w_drain.done(win_ring_proj(last, False) + 1))
            gelus(ffs[1])

            SCALE = float(D) ** -0.5

            def grp_exps(t):
                act.wait_ge(g_dif.sem, g_dif.done(t, 0))
                act.activation(sE, sE, ACT.Exp, scale=SCALE).then_inc(g_exp.sem, 1)
                act.wait_ge(g_dif.sem, g_dif.done(t, 1))
                act.activation(lE, lE, ACT.Exp).then_inc(g_exp.sem, 1)

            def grp_copies(t, k0, signal_in, signal_out, dst):
                act.wait_ge(signal_in.sem, signal_in.done(t))
                for k in range(2):
                    act.copy(dst[0:KROWS[k], k, :], PS[0:KROWS[k], k0 + k, :]).then_inc(signal_out.sem, 1)

            def grp_tile_act(t, first=False):
                grp_exps(t)
                act.wait_ge(g_gt.sem, g_gt.done(t))
                act.copy(gT[0:GP, :], PS[0:GP, 4, :]).then_inc(g_gtc.sem, 1)
                if not first:
                    grp_copies(t - 1, 2, g_tr, g_ht, hT2)
                act.wait_ge(g_wt.sem, g_wt.done(t))
                act.copy(wT, PS[:, 3, :]).then_inc(g_wtc.sem, 1)
                grp_copies(t, 4, g_pv, g_oc, oT2)

            grp_tile_act(0, first=True)
            with act.Fori(1, NT) as t:
                grp_tile_act(t)
            grp_copies(last, 2, g_tr, g_ht, hT2)

            act.wait_ge(r_chain, 2)
            act.activation(R[1], R[0], ACT.Exp).then_inc(r_exp, 1)

            def sh_rows(t):
                act.wait_ge(s_tr.sem, s_tr.done(t - 1))
                act.copy(shx, H2X[:, bass.ds(t * BPT, BPT), 0:D]).then_inc(s_x.sem, 1)

            def sh_turned(t, b):
                act.wait_ge(s_tr.sem, s_tr.done(t))
                act.copy(sxT[:, b, 0, :], PS[:, 0, :]).then_inc(s_xt.sem, 1)
                for a in (slice(0, 64), slice(64, 128)):
                    act.copy(sxT[a, b, 1, :], PS[0:DT, 1, :]).then_inc(s_xt.sem, 1)

            def sh_tile_act(t, b, more):
                for m in range(SC):
                    n = SC * t + m
                    act.wait_ge(s_up.sem, s_up.done(n, 0))
                    act.wait_ge(s_gg.sem, s_gg.recycled(n))
                    act.activation(sil[:, m % 2, :], PS[:, 2 + 2 * (m % 2), :], ACT.Silu).then_inc(s_silu.sem, 1)
                    if m == SC // 2 - 1 and more:
                        sh_rows(t + 1)
                    if m == SC // 2 and more:
                        sh_turned(t + 1, 1 - b)

            act.wait_ge(r_done, 1)
            sh_rows(0)
            sh_turned(0, 0)
            with act.Fori(0, NT // 2 - 1) as i:
                for b in range(2):
                    sh_tile_act(2 * i + b, b, True)
            sh_tile_act(last - 1, 0, True)
            sh_tile_act(last, 1, False)

            def ex_turned(j, b):
                act.wait_ge(e_tr.sem, e_tr.done(j))
                act.wait_ge(e_h3.sem, e_h3.recycled(j))
                act.copy(exT[:, b, 0, :], PS[:, 4, 0:P]).then_inc(e_xt.sem, 1)
                act.copy(exT[0:64, b, 1, :], PS[0:DT, 4, P:2 * P]).then_inc(e_xt.sem, 1)
                act.copy(exT[64:128, b, 2, :], PS[0:DT, 4, P:2 * P]).then_inc(e_xt.sem, 1)

            def ex_silu(j, b):
                act.wait_ge(e_h1.sem, e_h1.done(j))
                act.wait_ge(e_g.sem, e_g.recycled(j))
                act.activation(esil[:, b, :], PS[:, b, :], ACT.Silu).then_inc(e_silu.sem, 1)

            def ex_hidden_turned(j, b):
                act.wait_ge(e_gt.sem, e_gt.done(j))
                act.wait_ge(e_y.sem, e_y.recycled(j))
                act.copy(egT[:, b, :], PS[:, 5, :]).then_inc(e_gtc.sem, 1)

            def ex_step_act(j, b, first=False, final=False):
                ex_silu(j, b)
                if not first:
                    ex_hidden_turned(j - 1, 1 - b)
                if not final:
                    ex_turned(j + 1, 1 - b)

            act.wait_ge(e_zero, 1)
            ex_turned(0, 0)
            ex_step_act(0, 0, first=True)
            with act.Fori(0, (ET - 3) // 2) as i:
                ex_step_act(2 * i + 1, 1)
                ex_step_act(2 * i + 2, 0)
            ex_step_act(ET - 2, 1)
            ex_step_act(ET - 1, 0, final=True)
            ex_hidden_turned(ET - 1, 0)

        @block.vector
        def _(dve):
            for s in (em_raw, em_norm, ffs[0]["out"], ffs[1]["out"], w_drain, w_mx, w_sub, w_sum, w_rs, g_drain, g_mx,
                      g_dif, g_sum, g_gw, g_t1, g_wb, g_raw, g_norm, g_lgc, s_gg, s_z, e_g, e_ys, e_gate):
                s.start(dve)
            dve.wait_ge(late_in, 64)

            def rows(r, n):
                return rows5[:, r, :].unsqueeze(1).broadcast_to([P, n, D])

            def two(bank):
                return PS[:, bank, 0:2 * D].rearrange("p (j n) -> p j n", j=2)

            dve.wait_ge(exp_alpha, 1)
            dve.tensor_scalar(mix[:, 1:2], mix[:, 0:1], 1.0, None, ALU.add).then_inc(consts_ready, 1)
            dve.wait_ge(consts_ready, 1)
            dve.reciprocal(mix[:, 2:3], mix[:, 1:2]).then_inc(consts_ready, 1)
            dve.wait_ge(consts_ready, 2)
            dve.tensor_scalar(mix[:, 3:4], mix[:, 2:3], -1.0, 1.0, ALU.mult, ALU.add).then_inc(consts_ready, 1)

            with dve.Fori(0, NT // 2) as i:
                for b in range(2):
                    t = 2 * i + b
                    dve.wait_ge(em_mm.sem, em_mm.done(t))
                    dve.wait_ge(em_tr.sem, em_tr.recycled(t))
                    for g in range(2):
                        dve.tensor_tensor(xw[:, b, 2 * g:2 * g + 2, :], two(2 * b + g), rows(0, 2), ALU.add)\
                            .then_inc(em_raw.sem, 1)
                    dve.wait_ge(em_raw.sem, em_raw.done(t))
                    chain = Chain(dve, em_chain, N_EMBED * t)
                    norm_stats(dve, chain, [xw[:, b, j, :] for j in range(BPT)], stats, mv, rstd, tmp4, met_dve)
                    assert chain.n == N_EMBED
                    for j in range(BPT):
                        dve.tensor_scalar(xw[:, b, j, :], xw[:, b, j, :], mv[:, j, 0:1], rstd[:, j:j + 1],
                                          ALU.subtract, ALU.mult).then_inc(em_norm.sem, 1)

            def ff_banks(s, residual):
                with dve.Fori(0, NT // 2) as i:
                    for b in range(2):
                        t = 2 * i + b
                        dve.wait_ge(s["down"].sem, s["down"].done(FC * t + FC - 1))
                        for k in range(2):
                            rr = slice(0, KROWS[k])
                            x = XT[rr, k, bass.ds(t * TT, TT)]
                            if residual:
                                ins = dve.scalar_tensor_tensor(out=x, in0=PS[rr, 2 * b + k, :],
                                                               scalar=bc("ff2", k, KROWS[k]), in1=x,
                                                               op0=ALU.add, op1=ALU.add)
                            else:
                                ins = dve.tensor_scalar(YT[rr, k, bass.ds(t * TT, TT)], PS[rr, 2 * b + k, :],
                                                        bc("ff2", k, KROWS[k]), None, ALU.add)
                            ins.then_inc(s["out"].sem, 1)

            ff_banks(ffs[0], False)

            def win_drain_qkv(t, b):
                n = win_ring_qkv(t)
                for k in range(2):
                    rr = slice(0, KROWS[k])
                    dve.wait_ge(w_fill.sem, w_fill.done(n + k))
                    dve.tensor_scalar(qT[rr, k, :], PS[rr, 6 + k, :], bc("q", k, KROWS[k]), float(DH) ** -0.5,
                                      ALU.add, ALU.mult).then_inc(w_drain.sem, 1)
                for k in range(2):
                    rr = slice(0, KROWS[k])
                    dve.wait_ge(w_fill.sem, w_fill.done(n + 2 + k))
                    dve.tensor_scalar(kT[rr, k, :], PS[rr, 6 + k, :], bc("k", k, KROWS[k]), None, ALU.add)\
                        .then_inc(w_drain.sem, 1)
                for g in range(4):
                    dve.wait_ge(w_fill.sem, w_fill.done(n + 4 + g))
                    dve.tensor_tensor(vbd[:, b, 2 * g:2 * g + 2, :], two(6 + g % 2),
                                      c("vmask").unsqueeze(1).broadcast_to([P, 2, D]), ALU.mult)\
                        .then_inc(w_drain.sem, 1)

            def heads(x):
                return x.rearrange("p (h n) -> p h n", h=NH)

            def win_shift(pair, p):
                s = heads(PS[:, 0:2, :].rearrange("p b n -> p (b n)")[:, 0:NH * WIN])
                dve.wait_ge(w_s.sem, w_s.done(pair))
                dve.tensor_reduce(mx12[:, p % 2, :], s, AX, ALU.max).then_inc(w_mx.sem, 1)
                dve.wait_ge(w_mx.sem, w_mx.done(pair))
                dve.wait_ge(w_tr.sem, w_tr.recycled(pair))
                dve.tensor_tensor(heads(E[:, p % 2, :]), s,
                                  mx12[:, p % 2, :].unsqueeze(2).broadcast_to([P, NH, WIN]), ALU.subtract)\
                    .then_inc(w_sub.sem, 1)

            def win_sum(pair, p):
                dve.wait_ge(w_exp.sem, w_exp.done(pair))
                dve.tensor_reduce(sm12[:, p % 2, :], heads(E[:, p % 2, :]), AX, ALU.add).then_inc(w_sum.sem, 1)
                dve.wait_ge(w_sum.sem, w_sum.done(pair))
                dve.reciprocal(sm12[:, p % 2, :], sm12[:, p % 2, :]).then_inc(w_rs.sem, 1)

            def win_drain_proj(t, more):
                n = win_ring_proj(t, more)
                for k in range(2):
                    rr = slice(0, KROWS[k])
                    dve.wait_ge(w_fill.sem, w_fill.done(n + k))
                    x = XT[rr, k, bass.ds(t * TT, TT)]
                    dve.scalar_tensor_tensor(out=x, in0=PS[rr, 6 + k, :], scalar=bc("proj", k, KROWS[k]), in1=x,
                                             op0=ALU.add, op1=ALU.add).then_inc(w_drain.sem, 1)

            def win_tile_dve(t, b, more):
                win_shift(4 * t, 0)
                win_shift(4 * t + 1, 1)
                win_sum(4 * t, 0)
                win_shift(4 * t + 2, 2)
                win_sum(4 * t + 1, 1)
                win_shift(4 * t + 3, 3)
                win_sum(4 * t + 2, 2)
                win_sum(4 * t + 3, 3)
                if more:
                    win_drain_qkv(t + 1, 1 - b)
                win_drain_proj(t, more)

            win_drain_qkv(0, 0)
            dve.wait_ge(w_drain.sem, w_drain.done(5))
            dve.sem_inc(w_drain.sem, 2)
            with dve.Fori(0, NT // 2 - 1) as i:
                for b in range(2):
                    win_tile_dve(2 * i + b, b, True)
            win_tile_dve(last - 1, 0, True)
            win_tile_dve(last, 1, False)
            ff_banks(ffs[1], True)

            def grp_shift(t):
                sS = PS[:, 2, 0:BPT * WIN].rearrange("p (j n) -> p j n", j=BPT)
                sL = PS[:, 3, 0:BPT * GP].rearrange("p (j n) -> p j n", j=BPT)
                for part, (s, m, dst, n) in enumerate(((sS, mxS, sE, WIN), (sL, mxL, lE, GP))):
                    dve.wait_ge(g_a.sem, g_a.done(t, part))
                    dve.tensor_reduce(m, s, AX, ALU.max).then_inc(g_mx.sem, 1)
                    dve.wait_ge(g_mx.sem, g_mx.done(t, part))
                    dve.tensor_tensor(dst, s, m.unsqueeze(2).broadcast_to([P, BPT, n]), ALU.subtract)\
                        .then_inc(g_dif.sem, 1)

            def grp_probs(t):
                dve.wait_ge(g_exp.sem, g_exp.done(t, 0))
                dve.tensor_reduce(smS, sE, AX, ALU.add).then_inc(g_sum.sem, 1)
                dve.wait_ge(g_exp.sem, g_exp.done(t, 1))
                dve.tensor_reduce(smL, lE, AX, ALU.add).then_inc(g_sum.sem, 1)
                dve.wait_ge(g_sum.sem, g_sum.done(t, 1))
                dve.reciprocal(smL, smL).then_inc(g_sum.sem, 1)
                dve.reciprocal(smS, smS).then_inc(g_sum.sem, 1)
                dve.wait_ge(g_sum.sem, g_sum.done(t))
                dve.tensor_tensor(lE, lE, smL.unsqueeze(2).broadcast_to([P, BPT, GP]), ALU.mult).then_inc(g_gw.sem, 1)
                dve.tensor_tensor(sE, sE, smS.unsqueeze(2).broadcast_to([P, BPT, WIN]), ALU.mult).then_inc(g_gw.sem, 1)

            def grp_drain(t, b, us):
                n = 6 * t
                for u in us:
                    dve.wait_ge(g_fill.sem, g_fill.done(n + u))
                    if u < 4:
                        rr = slice(0, KROWS[u % 2])
                        ins = dve.tensor_scalar((q2, k2)[u // 2][rr, u % 2, :], PS[rr, u % 2, :],
                                                bc(("q2", "k2")[u // 2], u % 2, KROWS[u % 2]), None, ALU.add)
                    else:
                        ins = dve.tensor_tensor(v2[:, b, 2 * (u - 4):2 * (u - 4) + 2, :], two(u % 2), rows(3, 2), ALU.add)
                    ins.then_inc(g_drain.sem, 1)

            def grp_weights(t):
                dve.wait_ge(g_grp.sem, g_grp.done(t))
                dve.tensor_scalar(t1, PS[:, 5, 0:BPT * WIN].rearrange("p (j n) -> p j n", j=BPT), mix[:, 3:4],
                                  mix[:, 2:3], ALU.mult, ALU.add).then_inc(g_t1.sem, 1)
                dve.wait_ge(g_t1.sem, g_t1.done(t))
                dve.wait_ge(g_gw.sem, g_gw.done(t))
                for r in range(2):
                    a = slice(WIN * r, WIN * r + WIN)
                    dve.tensor_tensor(wb[a, :, a], t1[a], sE[a], ALU.mult).then_inc(g_wb.sem, 1)

            def grp_keep_logits(t):
                dve.wait_ge(g_lg.sem, g_lg.done(t))
                dve.tensor_copy(LG[:, bass.ds(t * BPT, BPT), :],
                                PS[:, 6, 0:BPT * NE].rearrange("p (j n) -> p j n", j=BPT)).then_inc(g_lgc.sem, 1)

            def grp_norm(t):
                dve.wait_ge(g_z.sem, g_z.done(t))
                dve.wait_ge(g_h2.sem, g_h2.done(t - 1))
                for g in range(2):
                    dve.tensor_tensor(zw[:, 2 * g:2 * g + 2, :], two(6 + g), rows(4, 2), ALU.add).then_inc(g_raw.sem, 1)
                dve.wait_ge(g_raw.sem, g_raw.done(t))
                chain = Chain(dve, g_chain, N_GROUP * t)
                norm_stats(dve, chain, [zw[:, j, :] for j in range(BPT)], stats, mv, rstd, tmp4, met_dve)
                for j in range(BPT):
                    dve.tensor_scalar(zw[:, j, :], zw[:, j, :], mv[:, j, 0:1], rstd[:, j:j + 1],
                                      ALU.subtract, ALU.mult).then_inc(g_norm.sem, 1)

            def grp_tile_dve(t, b, first=False, final=False):
                grp_shift(t)
                if not final:
                    grp_drain(t + 1, 1 - b, (0, 1))
                grp_probs(t)
                if not final:
                    grp_drain(t + 1, 1 - b, (2, 3, 4, 5))
                grp_weights(t)
                if not first:
                    grp_keep_logits(t - 1)
                grp_norm(t)

            dve.wait_ge(wb_zero, 1)
            dve.wait_ge(consts_ready, 3)
            grp_drain(0, 0, range(6))
            grp_tile_dve(0, 0, first=True)
            with dve.Fori(0, NT // 2 - 1) as i:
                grp_tile_dve(2 * i + 1, 1)
                grp_tile_dve(2 * i + 2, 0)
            grp_tile_dve(last, 1, final=True)
            grp_keep_logits(last)

            ch = Chain(dve, r_chain, 0)

            def step(ins):
                ch(ins)
                ch.join()

            def over_e(x):
                return x.unsqueeze(2).broadcast_to([P, NB, NE])

            def over_b(x):
                return x.unsqueeze(1).broadcast_to([P, NB, NE])

            top, total, m1, i1, m2, i2, p1, p2 = r1
            dve.wait_ge(g_lgc.sem, g_lgc.done(last))
            dve.wait_ge(g_h2.sem, g_h2.done(last))
            step(dve.tensor_reduce(top, LG, AX, ALU.max))
            step(dve.tensor_tensor(R[0], LG, over_e(top), ALU.subtract))
            dve.wait_ge(r_exp, 1)
            step(dve.tensor_reduce(total, R[1], AX, ALU.add))
            step(dve.reciprocal(total, total))
            step(dve.tensor_tensor(R[1], R[1], over_e(total), ALU.mult))
            scores, one1, one2 = R[1], R[2], R[3]
            for src, m, index, one in ((scores, m1, i1, one1), (R[6], m2, i2, one2)):
                if one is one2:
                    step(dve.scalar_tensor_tensor(out=R[6], in0=one1, scalar=-2.0, in1=scores, op0=ALU.mult, op1=ALU.add))
                step(dve.tensor_reduce(m, src, AX, ALU.max))
                step(dve.tensor_tensor(R[5], src, over_e(m), ALU.is_equal))
                step(dve.scalar_tensor_tensor(out=R[0], in0=R[5], scalar=-float(NE), in1=over_b(c("experts")),
                                              op0=ALU.mult, op1=ALU.add))
                step(dve.tensor_reduce(index, R[0], AX, ALU.min))
                step(dve.tensor_tensor(one, R[0], over_e(index), ALU.is_equal))
            step(dve.tensor_tensor(R[7], one1, one2, ALU.add))
            src, dst, s = R[7], R[4], 1
            while s < NB:
                ch(dve.tensor_copy(dst[:, 0:s, :], src[:, 0:s, :]))
                step(dve.tensor_tensor(dst[:, s:NB, :], src[:, s:NB, :], src[:, 0:NB - s, :], ALU.add))
                src, dst, s = dst, (R[6] if dst is R[4] else R[4]), 2 * s
            assert src is R[4]
            dve.tensor_tensor(R[5], R[4], R[7], ALU.subtract).then_inc(r_mask, 1)
            dve.wait_ge(r_pos, 1)
            step(dve.tensor_scalar(re[0].bitcast(I32), PS[:, 1, 0:NE], float(P - 1), None, ALU.add))
            step(dve.tensor_scalar(re[1].bitcast(I32), re[0].bitcast(I32), 7, None, ALU.arith_shift_right))
            step(dve.tensor_copy(re[2], re[1].bitcast(I32)))
            src, dst, s = re[2], re[3], 1
            while s < NE:
                ch(dve.tensor_copy(dst[:, 0:s], src[:, 0:s]))
                step(dve.tensor_tensor(dst[:, s:NE], src[:, s:NE], src[:, 0:NE - s], ALU.add))
                src, dst, s = dst, (re[4] if dst is re[3] else re[3]), 2 * s
            ends = src
            step(dve.tensor_tensor(re[5], ends, re[2], ALU.subtract))
            step(dve.tensor_scalar(re[6], re[5], float(P), None, ALU.mult))
            step(dve.tensor_tensor(R[0], PS[:, 0, :].rearrange("p (b n) -> p b n", b=NB), over_b(re[6]), ALU.add))
            for s, (one, place) in enumerate(((one1, p1), (one2, p2))):
                step(dve.tensor_tensor(R[6], one, R[0], ALU.mult))
                step(dve.tensor_reduce(place, R[6], AX, ALU.add))
                step(dve.tensor_copy(posi[:, s, :], place))
            ch(dve.tensor_copy(H2X[:, :, D], m1))
            ch(dve.tensor_copy(H2X[:, :, D + 1], m2))
            ch(dve.tensor_scalar(H2X[:, :, D + 2], i1, float(NE), None, ALU.add))
            ch(dve.tensor_copy(H2X[:, :, D + 3], c("token")))
            step(dve.tensor_tensor(tmap, ends.unsqueeze(1).broadcast_to([P, ET, NE]),
                                   c("tiles").unsqueeze(2).broadcast_to([P, ET, NE]), ALU.is_le))
            step(dve.tensor_reduce(emapf, tmap, AX, ALU.add))
            step(dve.tensor_scalar(emapf, emapf, float(NE - 1), None, ALU.min))
            dve.tensor_copy(emap, emapf).then_inc(r_done, 1)

            def sh_hidden(t, m):
                n = SC * t + m
                dve.wait_ge(s_silu.sem, s_silu.done(n))
                dve.wait_ge(s_up.sem, s_up.done(n))
                dve.wait_ge(s_dn.sem, s_dn.recycled(n))
                dve.tensor_tensor(gg[:, m % 2, :], sil[:, m % 2, :], PS[:, 3 + 2 * (m % 2), :], ALU.mult)\
                    .then_inc(s_gg.sem, 1)

            with dve.Fori(0, NT) as t:
                for m in range(SC):
                    sh_hidden(t, m)
                dve.wait_ge(s_dn.sem, s_dn.done(SC * t + SC - 1))
                dve.wait_ge(s_acc, 16 + 16 * t)
                for g in range(2):
                    dve.tensor_tensor(zo[:, 2 * g:2 * g + 2, :], two(6 + g), H2X[:, bass.ds(t * BPT + 2 * g, 2), 0:D],
                                      ALU.add).then_inc(s_z.sem, 1)

            def ex_gates(j, b, i):
                dve.wait_ge(e_in[b], 16 * (i + 1))
                dve.wait_ge(e_added.sem, e_added.recycled(j))
                g = Chain(dve, e_gate.sem, e_gate.depth * 5 + 5 * j)
                e1, mine = xg[:, b, D + 2:D + 3], emapf[:, bass.ds(j, 1)]
                g(dve.tensor_tensor(egate[:, b, 0:1], e1, mine, ALU.is_equal))
                g(dve.tensor_tensor(egate[:, b, 1:2], e1, mine, ALU.not_equal))
                g(dve.tensor_copy(tokidx[:, b:b + 1], xg[:, b, D + 3:D + 4]))
                g.join()
                g(dve.tensor_tensor(egate[:, b, 2:3], egate[:, b, 0:1], xg[:, b, D:D + 1], ALU.mult))
                g.join()
                g(dve.scalar_tensor_tensor(out=egate[:, b, 3:4], in0=egate[:, b, 1:2], scalar=xg[:, b, D + 1:D + 2],
                                           in1=egate[:, b, 2:3], op0=ALU.mult, op1=ALU.add))

            def ex_hidden(j, b):
                dve.wait_ge(e_silu.sem, e_silu.done(j))
                dve.wait_ge(e_h3.sem, e_h3.done(j))
                dve.wait_ge(e_gt.sem, e_gt.recycled(j))
                dve.tensor_tensor(eg[:, b, :], esil[:, b, :], PS[:, 2 + b, :], ALU.mult).then_inc(e_g.sem, 1)

            def ex_rows(j, b):
                dve.wait_ge(e_y.sem, e_y.done(j))
                dve.wait_ge(e_gate.sem, e_gate.done(j))
                dve.tensor_scalar(ey[:, b, :], PS[:, 6 + b, 0:D], egate[:, b, 3:4], None, ALU.mult)\
                    .then_inc(e_ys.sem, 1)

            def ex_step_dve(j, b, i, first=False):
                ex_hidden(j, b)
                ex_gates(j, b, i)
                if not first:
                    ex_rows(j - 1, 1 - b)

            ex_step_dve(0, 0, 0, first=True)
            with dve.Fori(0, (ET - 1) // 2) as i:
                ex_step_dve(2 * i + 1, 1, i)
                ex_step_dve(2 * i + 2, 0, i + 1)
            ex_rows(ET - 1, 0)

            for t in range(NT):
                dve.wait_ge(f_in[t], 16)
                chain = Chain(dve, f_chain, N_FIN * t)
                norm_stats(dve, chain, [fin[:, t, j, :] for j in range(BPT)], stats, mv, rstd, tmp4, met_dve)
                for j in range(BPT):
                    dve.tensor_scalar(fout[:, t, j, :], fin[:, t, j, :], mv[:, j, 0:1], rstd[:, j:j + 1],
                                      ALU.subtract, ALU.mult).then_inc(f_out, 1)

        @block.gpsimd
        def _(pool):
            for s in (em_mul, em_tok, w_yd, w_kbd, w_norm, g_hs, g_h2, e_added):
                s.start(pool)
            pool.wait_ge(late_in, 64)
            pool.tensor_tensor(bias_pe, rows5[:, 2, :], c("pe"), ALU.add).then_inc(bias_ready, 1)
            pool.wait_ge(bias_ready, 1)

            def over_j(x):
                return x.unsqueeze(1).broadcast_to([P, BPT, D])

            with pool.Fori(0, NT // 2) as i:
                for b in range(2):
                    t = 2 * i + b
                    pool.wait_ge(em_norm.sem, em_norm.done(t))
                    pool.tensor_tensor(xw[:, b, :, :], xw[:, b, :, :], over_j(rows5[:, 1, :]), ALU.mult)\
                        .then_inc(em_mul.sem, 1)
                    pool.wait_ge(em_mul.sem, em_mul.done(t))
                    pool.tensor_tensor(xw[:, b, :, :], xw[:, b, :, :], over_j(bias_pe), ALU.add)\
                        .then_inc(em_tok.sem, 1)

            def win_copy_y(t):
                pool.wait_ge(w_fill.sem, w_fill.done(win_ring_qkv(t - 1) + 7))
                for k in range(2):
                    src = YT[0:KROWS[k], k, bass.ds(t * TT, TT)].rearrange("p (i n) -> p i n", i=IPT)
                    for r in range(2):
                        pool.tensor_copy(yd[0:KROWS[k], k, :, r, :], src).then_inc(w_yd.sem, 1)

            def win_spread_k(pair, p):
                for img in (2 * p, 2 * p + 1):
                    for k, (h0, h1) in enumerate(((0, HM), (HM, NH))):
                        rr, n = slice(0, KROWS[k]), h1 - h0
                        pool.tensor_tensor(
                            kbd[rr, img, h0:h1, :],
                            kT[rr, k, WIN * img:WIN * img + WIN].unsqueeze(1).broadcast_to([KROWS[k], n, WIN]),
                            kmask[rr, 0:n].unsqueeze(2).broadcast_to([KROWS[k], n, WIN]), ALU.mult)\
                            .then_inc(w_kbd.sem, 1)

            def win_normalise(pair, p):
                pool.wait_ge(w_rs.sem, w_rs.done(pair))
                e = E[:, p % 2, :].rearrange("p (h n) -> p h n", h=NH)
                pool.tensor_tensor(e, e, sm12[:, p % 2, :].unsqueeze(2).broadcast_to([P, NH, WIN]), ALU.mult)\
                    .then_inc(w_norm.sem, 1)

            def win_spread_tile(t):
                pool.wait_ge(w_drain.sem, w_drain.done(win_ring_qkv(t) + 3))
                for p in range(4):
                    win_spread_k(4 * t + p, p)

            def win_pool_steps(t, more):
                win_normalise(4 * t, 0)
                win_normalise(4 * t + 1, 1)
                if more:
                    win_copy_y(t + 1)
                win_normalise(4 * t + 2, 2)
                win_normalise(4 * t + 3, 3)
                if more:
                    win_spread_tile(t + 1)

            pool.wait_ge(ffs[0]["out"].sem, ffs[0]["out"].done(last))
            for k in range(2):
                src = YT[0:KROWS[k], k, 0:TT].rearrange("p (i n) -> p i n", i=IPT)
                for r in range(2):
                    pool.tensor_copy(yd[0:KROWS[k], k, :, r, :], src).then_inc(w_yd.sem, 1)
            win_spread_tile(0)
            with pool.Fori(0, NT - 1) as t:
                win_pool_steps(t, True)
            win_pool_steps(last, False)

            def grp_copy_h(t, b, first=False):
                if not first:
                    pool.wait_ge(g_z.sem, g_z.done(t - 2))
                for k in range(2):
                    pool.tensor_copy(hs[0:KROWS[k], b, k, :], XT[0:KROWS[k], k, bass.ds(t * TT, TT)])\
                        .then_inc(g_hs.sem, 1)

            def grp_keep(t):
                pool.wait_ge(g_norm.sem, g_norm.done(t))
                pool.tensor_copy(H2X[:, bass.ds(t * BPT, BPT), 0:D], zw).then_inc(g_h2.sem, 1)

            pool.wait_ge(ffs[1]["out"].sem, ffs[1]["out"].done(last))
            pool.memset(wb, 0.0).then_inc(wb_zero, 1)
            grp_copy_h(0, 0, first=True)
            grp_copy_h(1, 1, first=True)
            with pool.Fori(0, NT // 2 - 1) as i:
                for b in range(2):
                    grp_keep(2 * i + b)
                    grp_copy_h(2 * i + b + 2, b)
            grp_keep(last - 1)
            grp_keep(last)

            pool.wait_ge(r_done, 1)
            pool.wait_ge(table_filled, 16)
            for t in range(NT):
                for blk in range(BPT * t, BPT * t + BPT):
                    for s in range(2):
                        pool.indirect_dma_start(XS, bass.IndirectOffsetOnAxis(ap=posi[:, s, blk:blk + 1], axis=0),
                                                H2X[:, blk, :], None).then_inc(scat[t % 2], 16)
                if t >= 1:
                    pool.wait_ge(scat[(t - 1) % 2], 32 * BPT * ((t - 1) // 2 + 1))
                    pool.sem_inc(scattered, 1)
            pool.wait_ge(scat[last % 2], 32 * BPT * (last // 2 + 1))
            pool.sem_inc(scattered, 1)

            pool.wait_ge(s_z.sem, s_z.done(last))
            for b in range(2):
                pool.memset(exT[64:128, b, 1, :], 0.0)
                pad = pool.memset(exT[0:64, b, 2, :], 0.0)
            pad.then_inc(e_zero, 1)
            pool.wait_ge(s_acc, 16 + 16 * NT)
            pool.wait_ge(dummies_filled, 16)

            def ex_add(j, b, i):
                pool.wait_ge(e_ys.sem, e_ys.done(j))
                pool.sem_inc(met_pool, 1)
                pool.indirect_dma_start(ACC, bass.IndirectOffsetOnAxis(ap=tokidx[:, b:b + 1], axis=0),
                                        ey[:, b, :], None, compute_op=ALU.add).then_inc(e_acc[b], 16)
                pool.wait_ge(e_acc[b], 16 * (i + 1))
                pool.sem_inc(e_added.sem, 1)

            with pool.Fori(0, ET // 2) as i:
                ex_add(2 * i, 0, i)
                ex_add(2 * i + 1, 1, i)
            ex_add(ET - 1, 0, ET // 2)


def _constants():
    a = np.zeros((P, CONST), np.float32)
    p = np.arange(P)
    a[:, _C["ident"]] = np.eye(P)
    a[:, _C["before"]] = p[:, None] < p[None, :]
    a[:, _C["ones"]] = 1
    a[:, _C["kmask"]] = p[:, None] // DH == np.arange(HM)[None, :]
    a[:, _C["vmask"]] = (np.arange(D)[None, :] % 32 // DH) == (p[:, None] // WIN)
    pos = np.arange(WIN, dtype=np.float32)[:, None]
    i = np.arange(D // 2, dtype=np.float32)[None, :]
    angle = pos / np.power(np.float32(10000.0), np.float32(2.0) * i / np.float32(D))
    pe = np.zeros((WIN, D), np.float32)
    pe[:, 0::2], pe[:, 1::2] = np.sin(angle), np.cos(angle)
    a[:, _C["pe"]] = np.concatenate([pe, pe])
    a[:, _C["experts"]] = np.arange(NE)
    a[:, _C["tiles"]] = np.arange(ET)
    a[:, _C["padrow"]][:, D + 2] = -1
    a[:, _C["padrow"]][:, D + 3] = TOK + p
    a[:, _C["token"]] = np.arange(NB)[None, :] * P + p[:, None]
    return a


def _split(v):
    out = np.zeros((P, 2), v.dtype)
    out[:, 0], out[:DT, 1] = v[:DM], v[DM:]
    return out


def _arrays(x, L0_tok_patch_w, L0_tok_patch_b, L0_tok_ln_g, L0_tok_ln_b, L0_tok_qkv_w, L0_tok_qkv_b, L0_tok_proj_w,
            L0_tok_proj_b, L0_tok_ff1_w, L0_tok_ff1_b, L0_tok_ff2_w, L0_tok_ff2_b, L0_attn_W_qkv, L0_attn_b_qkv,
            L0_attn_W_proj, L0_attn_b_proj, L0_attn_W_gp, L0_attn_alpha, L0_ffn_gate_w, L0_ffn_w1, L0_ffn_w2,
            L0_ffn_w3, L0_ffn_sw1, L0_ffn_sw2, L0_ffn_sw3):
    d = {"const": _constants()}
    a = x.reshape(IMAGES, CH, GRID, PATCH, GRID, PATCH).transpose(1, 3, 5, 0, 2, 4)
    d["patches"] = a.reshape(PK, P, NT, TT).transpose(2, 1, 0, 3)
    d["patch_w"] = L0_tok_patch_w.reshape(D, PK, P).transpose(2, 1, 0)
    d["rows5"] = np.concatenate([L0_tok_patch_b, L0_tok_ln_g, L0_tok_ln_b, L0_attn_b_qkv[2 * D:], L0_attn_b_proj])[None]
    d["alpha"] = L0_attn_alpha[None]
    d["bcols"] = np.concatenate(
        [L0_tok_ff1_b.reshape(FC, P).T, _split(L0_tok_ff2_b)] + [_split(L0_tok_qkv_b[n * D:n * D + D]) for n in range(3)]
        + [_split(L0_tok_proj_b)] + [_split(L0_attn_b_qkv[n * D:n * D + D]) for n in range(2)], axis=1)
    d["ff1_w"], d["ff2_w"] = L0_tok_ff1_w, L0_tok_ff2_w.reshape(FC, P, D).transpose(1, 0, 2)
    d["qkv_w"], d["proj_w"], d["qkv2_w"], d["proj2_w"] = L0_tok_qkv_w, L0_tok_proj_w, L0_attn_W_qkv, L0_attn_W_proj
    d["gp_w"], d["gate_w"] = L0_attn_W_gp, L0_ffn_gate_w.T
    def up(w1, w3):
        w1, w3 = np.swapaxes(w1, -1, -2), np.swapaxes(w3, -1, -2)
        return [w1[..., :DM, :], w3[..., :DM, :], np.concatenate([w1[..., DM:, :], w3[..., DM:, :]], axis=-2)]

    def down(w2):
        w2 = np.swapaxes(w2, -1, -2)
        n = w2.shape[-2] // P
        w2 = np.swapaxes(w2.reshape(*w2.shape[:-2], n, P, D), -2, -3)
        return [w2.reshape(*w2.shape[:-2], n * D)]

    d["shared"] = np.concatenate(up(L0_ffn_sw1, L0_ffn_sw3) + down(L0_ffn_sw2), axis=-1)
    d["experts"] = np.concatenate(up(L0_ffn_w1, L0_ffn_w3) + down(L0_ffn_w2), axis=-1)
    return {n: np.ascontiguousarray(v) for n, v in d.items()}


def kernel(**inputs):
    import concourse.bacc as _bacc
    from concourse.bass_utils import run_bass_kernel_spmd as _run

    arrays = {f"in_{n}": a for n, a in _arrays(**{n: np.asarray(a) for n, a in inputs.items()}).items()}
    nc = _bacc.Bacc("TRN2", target_bir_lowering=False, num_devices=1)
    d = {n[3:]: nc.dram_tensor(n, a.shape, mybir.dt.from_np(a.dtype), kind="ExternalInput").ap()
         for n, a in arrays.items()}
    out = nc.dram_tensor("out_dram", (TOK, D), F32, kind="ExternalOutput").ap()
    build(nc, d, out)
    r = _run(nc, [arrays], core_ids=[0])
    return r.results[0]["out_dram"].reshape(IMAGES, WIN, D)
```

```python
from contextlib import ExitStack

import numpy as np

import concourse.bass as bass
from concourse import mybir

F32 = mybir.dt.float32
I32 = mybir.dt.int32
U32 = mybir.dt.uint32
ALU = mybir.AluOpType
ACT = mybir.ActivationFunctionType
AX = mybir.AxisListType.X

P = 128
IMAGES, CH, SIDE, PATCH = 64, 3, 128, 16
GRID = SIDE // PATCH
WIN = GRID * GRID
TOK = IMAGES * WIN
D = 192
DM, DT = P, D - P
PK = CH * PATCH * PATCH // P
TT = 512
NT = TOK // TT
IPT = TT // WIN
BPT = TT // P
NB = TOK // P
FF = 768
FC = FF // P
NH, DH = 12, 16
HM = DM // DH
GP = 49
NE, MI = 16, 512
SI = 1024
SC = SI // P
ROW = D + 4
ET = TOK * 2 // P + NE - 1
EPS = 1e-5
EW = 2 * MI + MI + (MI // P) * D

_C = {}
_at = 0
for _name, _n in (("ident", P), ("before", P), ("ones", P), ("kmask", HM), ("pe", D),
                  ("experts", NE), ("tiles", ET), ("padrow", ROW), ("token", NB)):
    _C[_name] = slice(_at, _at + _n)
    _at += _n
CONST = _at
_B = {}
_at = 0
for _name, _n in (("ff1", FC), ("ff2", 2), ("qk", 3), ("v", 2), ("proj", 2), ("qk2", 3)):
    _B[_name] = slice(_at, _at + _n)
    _at += _n
BCOLS = _at


class Signal:

    def __init__(self, sem, depth, per=1, first=0):
        self.sem, self.depth, self.per, self.first = sem, depth, per, first

    def start(self, engine):
        engine.sem_inc(self.sem, self.depth * self.per)

    def done(self, item, part=None):
        return (item - self.first + self.depth) * self.per + (self.per if part is None else part + 1)

    def recycled(self, item):
        return (item - self.first) * self.per + self.per


class Chain:

    def __init__(self, engine, sem, base):
        self.engine, self.sem, self.base, self.n = engine, sem, base, 0

    def __call__(self, instruction):
        self.n += 1
        instruction.then_inc(self.sem, 1)

    def join(self):
        self.engine.wait_ge(self.sem, self.base + self.n)


NEWTON = 3
RSQRT_STEPS = 3 + 3 * NEWTON


def rsqrt(dve, chain, out, var, tmp):
    chain(dve.tensor_scalar(var, var, EPS, None, ALU.add))
    chain.join()
    chain(dve.tensor_scalar(tmp.bitcast(I32), var.bitcast(I32), 1, None, ALU.logical_shift_right))
    chain.join()
    chain(dve.tensor_scalar(out.bitcast(I32), tmp.bitcast(I32), -1.0, float(0x5F3759DF), ALU.mult, ALU.add))
    chain.join()
    for _ in range(NEWTON):
        chain(dve.tensor_tensor(tmp, out, out, ALU.mult))
        chain.join()
        chain(dve.scalar_tensor_tensor(out=tmp, in0=tmp, scalar=-0.5, in1=var, op0=ALU.mult, op1=ALU.mult))
        chain.join()
        chain(dve.scalar_tensor_tensor(out=out, in0=tmp, scalar=1.5, in1=out, op0=ALU.add, op1=ALU.mult))
        chain.join()


def norm_steps(n):
    return 2 * n + RSQRT_STEPS


def norm_stats(dve, chain, rows, stats, mv, rstd, tmp, met):
    for j, row in enumerate(rows):
        chain(dve.bn_stats(stats[:, j, :], row))
    chain.join()
    dve.sem_inc(met, 1)
    for j in range(len(rows)):
        chain(dve.bn_aggr(mv[:, j, :], stats[:, j, :]))
    chain.join()
    rsqrt(dve, chain, rstd, mv[:, :, 1], tmp)


def build(nc, d, out):
    XS = nc.dram_tensor("sorted_rows", (ET * P, ROW), F32).ap()
    ACC = nc.dram_tensor("acc_rows", (TOK + P, D), F32).ap()
    ACC1 = nc.dram_tensor("acc_rows_odd", (TOK + P, D), F32).ap()

    with ExitStack() as ctx:
        MEM = 53200
        mem = ctx.enter_context(nc.sbuf_tensor("mem", [P, MEM], F32))[:, :]
        PS = ctx.enter_context(nc.psum_tensor("PS", [P, 8, 512], F32))

        def sem(name):
            return ctx.enter_context(nc.semaphore(name))

        def signal(name, depth, per=1, first=0):
            return Signal(sem(name), depth, per, first)

        class Region:
            def __init__(self, lo, hi):
                self.at, self.hi = lo, hi

            def __call__(self, n, **shape):
                a = mem[:, self.at:self.at + n]
                self.at += n
                assert self.at <= self.hi, (self.at, self.hi)
                if not shape:
                    return a
                keys = list(shape)
                return a.rearrange(f"p ({' '.join(keys)} n) -> p {' '.join(keys)} n", **shape)

        EXPERTS = NE * EW
        SHW = (NE - 1) * EW
        H2 = SHW + 3 * SI + SC * D
        SHWORK = H2 + NB * ROW
        CONSTS = MEM - 1400

        early = Region(0, SHW)
        XT = early(2 * TOK, k=2)
        YT = early(2 * TOK, k=2)
        wpatch = early(PK * D, c=PK)
        wff1 = early(2 * FF, k=2)
        wff2 = early(FC * D, c=FC)
        wqkv = early(2 * 3 * D, k=2)
        wproj = early(2 * D, k=2)
        wqkv2 = early(2 * 3 * D, k=2)
        wproj2 = early(2 * D, k=2)
        wgp = early(2 * GP, k=2)
        wgate = early(2 * NE, k=2)
        rows5 = early(5 * D, r=5)
        bias_pe = early(D)
        WORK = early.at
        work = Region(WORK, CONSTS)
        patches = work(2 * PK * TT, b=2, c=PK)
        xw = work(2 * BPT * D, b=2, j=BPT)
        work = Region(WORK, CONSTS)
        hid = work(4 * TT, b=4)
        work = Region(WORK, CONSTS)
        ys = work(2 * 2 * TT, b=2, k=2)
        qT = work(2 * 2 * TT, b=2, k=2)
        kbd = work(2 * IPT * NH * WIN, b=2, i=IPT, h=NH)
        vbd = work(2 * IPT * D, b=2, i=IPT)
        E = work(2 * NH * WIN, b=2)
        ETb = work(2 * NH * WIN, b=2)
        oT = work(2 * TT, k=2)
        work = Region(WORK, SHW)
        hs = work(2 * 2 * TT, b=2, k=2)
        q2 = work(2 * TT, k=2)
        k2 = work(2 * TT, k=2)
        v2 = work(2 * BPT * D, b=2, j=BPT)
        sE = work(BPT * WIN, j=BPT)
        lE = work(BPT * GP, j=BPT)
        gT = work(TT)
        t1 = work(BPT * WIN, j=BPT)
        wb = work(BPT * P, j=BPT)
        wT = work(TT)
        oT2 = work(2 * TT, k=2)
        work = Region(SHWORK, CONSTS)
        zw = work(BPT * D, j=BPT)
        hT2 = work(2 * TT, k=2)
        LG = work(NB * NE, b=NB)
        work = Region(WORK, SHW)
        R = [work(NB * NE, b=NB) for _ in range(8)]
        r1 = [work(NB) for _ in range(8)]
        re = [work(NE) for _ in range(8)]
        tmap = work(ET * NE, j=ET)
        work = Region(SHW, H2)
        shw13 = work(2 * SI)
        shwt = work(SI)
        shw2 = work(SC * D, c=SC)
        H2X = Region(H2, SHWORK)(NB * ROW, b=NB)
        work = Region(SHWORK, CONSTS)
        sxT = work(4 * TT, b=2, k=2)
        shx = work(BPT * D, j=BPT)
        sil = work(2 * TT, b=2)
        gg = work(2 * TT, b=2)
        zo = work(BPT * D, j=BPT)
        behind_rows = work(4 * ET, t=ET)
        gates, gates2, tokens = work(ET), work(ET), work(ET)
        work = Region(H2, SHWORK)
        xg = work(2 * ROW, b=2)
        exT = work(2 * 2 * P, b=2, k=2)
        esil = work(2 * MI, b=2)
        eg = work(2 * MI, b=2)
        ey = work(2 * D, b=2)
        egate = work(2)
        ew = Region(SHWORK, CONSTS)(2 * 3 * MI, b=2)
        work = Region(0, SHW)
        fin = work(NT * BPT * D, t=NT, j=BPT)
        fin1 = work(NT * BPT * D, t=NT, j=BPT)
        fout = work(NT * BPT * D, t=NT, j=BPT)
        work = Region(CONSTS, MEM)
        const = work(CONST)
        bcols = work(BCOLS)
        stats = work(24, j=4)
        mv = work(8, j=4)
        rstd, tmp4 = work(4), work(4)
        mix = work(4)
        alpha = work(1)
        mx12, sm12 = work(2 * NH, b=2), work(2 * NH, b=2)
        mxS, smS, mxL, smL = work(4), work(4), work(4), work(4)
        posi = work(2 * NB, s=2).bitcast(I32)
        emap = work(ET).bitcast(I32)
        emapf = work(ET)
        tokidx = work(2).bitcast(I32)
        qbias = work(1)
        kbias = work(HM)

        def c(name):
            return const[:, _C[name]]

        def bc(name, k, rows=P):
            return bcols[0:rows, _B[name]][:, k:k + 1]

        ident, kmask = c("ident"), c("kmask")
        KROWS = (P, DT)


        early_in, late_in, shared_in, experts_in, lastw_in = (
            sem("early_weights_loaded"), sem("row_constants_loaded"), sem("shared_weights_loaded"),
            sem("expert_weights_loaded"), sem("last_expert_loaded"))
        table_filled, dummies_filled = sem("sorted_rows_filled"), sem("dummy_rows_filled")
        consts_ready, bias_ready = sem("mix_ready"), sem("position_bias_ready")
        exp_alpha = sem("exp_alpha")

        patch_in = [sem("patches_in0"), sem("patches_in1")]
        em_mm, em_raw, em_norm = signal("embed_products", 2), signal("embed_raw", 2, 2), signal("embed_normed", 2, BPT)
        em_mul, em_tok = signal("embed_scaled", 2), signal("embed_tokens", 2)
        em_tr, em_xt = signal("embed_transposed", 2), signal("embed_xt", 2, 2)
        em_chain = sem("embed_chain")

        ffs = []
        for which in "ab":
            ffs.append({n: signal(f"ff_{which}_{n}", depth, per) for n, depth, per in
                        (("up", 3, 1), ("gelu", 3, 1), ("down", 4, 1), ("half", 2, 1), ("out", 2, 2))})

        w_y, w_fill = signal("win_y_copied", 2, 2), signal("win_ring_filled", 2)
        w_drain = [signal(f"win_ring_drained{n}", 1) for n in range(2)]
        w_zero = sem("win_values_zeroed")
        w_s, w_mx, w_sub, w_exp = (signal(f"win_{n}", 2) for n in ("scores", "max", "shifted", "exp"))
        w_sum, w_rs, w_norm = (signal(f"win_{n}", 2) for n in ("sum", "reciprocal", "weights"))
        w_tr, w_et, w_pv, w_o = (signal("win_transposed", 2), signal("win_turned", 2, 2),
                                 signal("win_values", 2), signal("win_heads_out", 1, 2))

        g_hs, g_fill, g_drain = signal("grp_h_copied", 2, 2), signal("grp_ring_filled", 2), signal("grp_ring_drained", 2)
        g_a = signal("grp_scores", 1, 2)
        g_mx, g_dif = signal("grp_max", 1, 2), signal("grp_shifted", 1, 2)
        g_exp, g_sum, g_gw = signal("grp_exp", 1, 2), signal("grp_sums", 1, 4), signal("grp_group_probs", 1, 2)
        g_gt, g_gtc, g_grp = signal("grp_probs_turned", 1), signal("grp_probs_copied", 1), signal("grp_group", 1)
        g_t1, g_wb = signal("grp_mix", 1), signal("grp_weights", 1, 2)
        g_wt, g_wtc, g_pv = signal("grp_weights_turned", 1), signal("grp_weights_copied", 1), signal("grp_values", 1)
        g_oc, g_z, g_raw = signal("grp_values_copied", 1, 2), signal("grp_rows", 1), signal("grp_rows_raw", 1, 2)
        g_norm, g_h2 = signal("grp_rows_normed", 1, BPT), signal("grp_rows_kept", 1)
        g_tr, g_ht = signal("grp_rows_turned", 1), signal("grp_rows_turned_copied", 1, 2)
        g_lg, g_lgc = signal("grp_logits", 1), signal("grp_logits_copied", 1)
        g_chain, wb_zero = sem("grp_chain"), sem("grp_weights_zeroed")

        r_chain, r_exp, r_pos, r_mask = sem("route_chain"), sem("route_exp"), sem("route_counts"), sem("route_chosen")
        r_done = sem("route_done")
        scat = [sem("scatter0"), sem("scatter1")]
        scattered = sem("scattered_tiles")

        s_x, s_tr, s_xt = signal("sh_rows", 1), signal("sh_turned", 2), signal("sh_x", 2, 3)
        s_up, s_silu, s_gg, s_dn = signal("sh_up", 2, 2), signal("sh_silu", 2), signal("sh_hidden", 2), signal("sh_down", 2)
        s_z, s_acc = signal("sh_out", 1, 2), sem("acc_rows_stored")

        e_in = [sem("ex_rows0"), sem("ex_rows1")]
        e_tr, e_xt, e_h1, e_h3 = signal("ex_turned", 2), signal("ex_x", 2), signal("ex_h1", 2), signal("ex_h3", 2)
        e_silu, e_g, e_w = signal("ex_silu", 2), signal("ex_hidden", 2), signal("ex_weights", 2)
        e_y, e_ys, e_gate = signal("ex_y", 2), signal("ex_rows_out", 2), signal("ex_gate", 2, 2)
        behind_in, gates_ready = sem("rows_ends_loaded"), sem("gates_ready")
        e_acc = [sem("ex_add_landed0"), sem("ex_add_landed1")]
        e_added = signal("ex_added", 2)

        f_in = [sem(f"fin_in{n}") for n in range(NT)]
        f_chain, f_out, f_st = sem("fin_chain"), sem("fin_rows"), sem("fin_stored")

        met_dve, met_pe, met_pool = sem("waits_met_vector"), sem("waits_met_tensor"), sem("waits_met_pool")
        EARLY = 16
        N_EMBED = norm_steps(BPT)
        N_GROUP = norm_steps(BPT)
        N_FIN = norm_steps(BPT) + 1
        last = NT - 1

        def kparts(weights, cols):
            return [weights[0:KROWS[k], k, cols] for k in range(2)]

        def halves(k):
            return slice(0, DM) if k == 0 else slice(DM, D)

        WU = 7
        WQ, WK, WQK, WP, WV = 0, 1, 2, 3, 5

        class RingItem:
            def __init__(self, i, off):
                self.n, self.bank, self.drain = 2 * WU * i + off, 6 + off % 2, w_drain[off % 2]
                self.at = WU * i + off // 2

            def free(self):
                return self.drain.sem, self.drain.recycled(self.at)

            def drained(self):
                return self.drain.sem, self.drain.done(self.at)

            def filled(self):
                return w_fill.sem, w_fill.done(self.n)

        def win_item(i, b, u):
            return RingItem(i, WU * b + u)

        def win_item_proj(i, b, u, ending=False):
            return RingItem(i, 2 * WU + (2 * b if ending else WU * b + WP) + u)

        def win_skip(engine, i, b, u):
            item = win_item(i, b, u)
            engine.wait_ge(*item.drained())
            engine.sem_inc(item.drain.sem, 1)

        def win_neighbours(i, b):
            return ((i - 1, 1) if b == 0 else (i, 0)), ((i, 1) if b == 0 else (i + 1, 0))

        GU = 5

        def grp_bank(b, u):
            return (GU * b + u) % 2

        def weights_at(engine, j):
            return engine.value_load(emap[0:1, bass.ds(j, 1)], min_val=0, max_val=NE - 1) * EW

        block = ctx.enter_context(nc.Block())

        @block.sync
        def _(sp):
            sp.sem_inc(s_acc, 16)
            sp.dma_start(const, d["const"]).then_inc(late_in, 16)
            sp.dma_start(rows5, d["rows5"].partition_broadcast(P)).then_inc(late_in, 16)
            sp.dma_start(alpha, d["alpha"].partition_broadcast(P)).then_inc(late_in, 16)
            sp.dma_start(bcols, d["bcols"]).then_inc(late_in, 16)
            sp.dma_start(wpatch, d["patch_w"]).then_inc(early_in, 16)

            with sp.Fori(0, NT // 2) as i:
                for b in range(2):
                    sp.wait_ge(em_mm.sem, em_mm.recycled(2 * i + b))
                    sp.dma_start(patches[:, b, :, :], d["patches"][bass.ds(2 * i + b, 1)]
                                 .rearrange("o p c n -> (o p) c n")).then_inc(patch_in[b], 16)

            sp.wait_ge(late_in, 64)
            sp.dma_start(XS.rearrange("(t p) n -> p t n", p=P),
                         c("padrow").unsqueeze(1).broadcast_to([P, ET, ROW])).then_inc(table_filled, 16)
            sp.dma_start(ACC[TOK:TOK + P, :], c("padrow")[:, 0:D]).then_inc(dummies_filled, 16)
            sp.dma_start(ACC1.rearrange("(t p) n -> p t n", p=P),
                         c("padrow")[:, 0:D].unsqueeze(1).broadcast_to([P, NB + 1, D])).then_inc(dummies_filled, 16)

            for u in range(2):
                sp.wait_ge(*win_item_proj(NT // 2 - 1, 1, u, True).drained())
            sp.dma_start(mem[:, SHW:H2], d["shared"]).then_inc(shared_in, 16)
            sp.wait_ge(r_done, 1)
            for e in range(NE - 1):
                sp.dma_start(mem[:, e * EW:(e + 1) * EW], d["experts"][e]).then_inc(experts_in, 16)
            with sp.Fori(0, NT) as t:
                sp.wait_ge(s_z.sem, s_z.done(t))
                sp.dma_start(ACC[bass.ds(t * TT, TT), :].rearrange("(j p) n -> p j n", p=P), zo).then_inc(s_acc, 16)
            sp.dma_start(mem[:, SHW:SHW + EW], d["experts"][NE - 1]).then_inc(lastw_in, 16)
            sp.wait_ge(scattered, NT)

            def rows_in(j, b):
                sp.wait_ge(e_tr.sem, e_tr.recycled(j))
                sp.dma_start(xg[:, b, :], XS[bass.ds(j * P, P), :]).then_inc(e_in[b], 16)

            with sp.Fori(0, ET // 2) as i:
                for b in range(2):
                    rows_in(2 * i + b, b)
            rows_in(ET - 1, (ET - 1) % 2)
            sp.wait_ge(e_added.sem, e_added.done(ET - 1))
            for t in range(NT):
                for dst, src in ((fin, ACC), (fin1, ACC1)):
                    sp.dma_start(dst[:, t, :, :], src[t * TT:(t + 1) * TT, :]
                                 .rearrange("(j p) n -> p j n", p=P)).then_inc(f_in[t], 16)
            for t in range(NT):
                sp.wait_ge(f_out, BPT * (t + 1))
                sp.dma_start(out[t * TT:(t + 1) * TT, :].rearrange("(j p) n -> p j n", p=P),
                             fout[:, t, :, :]).then_inc(f_st, 16)
            sp.wait_ge(f_st, 16 * NT)

        @block.tensor
        def _(pe):
            for s in (em_mm, em_tr, ffs[0]["up"], ffs[0]["down"], ffs[1]["up"], ffs[1]["down"], w_fill, w_s, w_tr, w_pv,
                      g_fill, g_a, g_gt, g_grp, g_wt, g_pv, g_z, g_tr, g_lg, s_tr, s_up, s_dn,
                      e_tr, e_h1, e_h3, e_y):
                s.start(pe)
            pe.wait_ge(early_in, 16 * EARLY)
            pe.wait_ge(late_in, 64)

            def embed_mm(t, b, i):
                pe.wait_ge(patch_in[b], 16 * (i + 1))
                pe.wait_ge(em_raw.sem, em_raw.recycled(t))
                for j in range(BPT):
                    for k in range(PK):
                        mm = pe.matmul(PS[:, 2 * b + j // 2, D * (j % 2):D * (j % 2) + D],
                                       patches[:, b, k, P * j:P * j + P], wpatch[:, k, :],
                                       start=k == 0, stop=k == PK - 1)
                mm.then_inc(em_mm.sem, 1)

            def embed_tr(t, b):
                pe.wait_ge(em_tok.sem, em_tok.done(t))
                pe.wait_ge(em_xt.sem, em_xt.recycled(t))
                for j in range(BPT):
                    pe.transpose(PS[:, 4 + b, P * j:P * j + P], xw[:, b, j, 0:DM], ident)
                    tr = pe.transpose(PS[0:DT, 6 + b, P * j:P * j + P], xw[:, b, j, DM:D], ident)
                tr.then_inc(em_tr.sem, 1)

            embed_mm(0, 0, 0)
            with pe.Fori(0, NT // 2 - 1) as i:
                embed_mm(2 * i + 1, 1, i)
                embed_tr(2 * i, 0)
                embed_mm(2 * i + 2, 0, i + 1)
                embed_tr(2 * i + 1, 1)
            embed_mm(last, 1, NT // 2 - 1)
            embed_tr(last - 1, 0)
            embed_tr(last, 1)

            def feed_forward(s):
                def up(t, b, m):
                    pe.wait_ge(s["gelu"].sem, s["gelu"].recycled(FC * t + m))
                    w = kparts(wff1, slice(P * m, P * m + P))
                    for k in range(2):
                        mm = pe.matmul(PS[:, 4 + m % 3, :], w[k], XT[0:KROWS[k], k, bass.ds(t * TT, TT)],
                                       start=k == 0, stop=k == 1)
                    mm.then_inc(s["up"].sem, 1)

                def down(t, b, m):
                    pe.wait_ge(s["gelu"].sem, s["gelu"].done(FC * t + m + 1))
                    if m == 0:
                        pe.wait_ge(s["out"].sem, s["out"].recycled(t))
                    for q in (m, m + 1):
                        pe.matmul(PS[:, 2 * b, :], wff2[:, q, 0:DM], hid[:, (FC * b + q) % 4, :],
                                  start=q == 0, stop=q == FC - 1)
                    for r in range(2):
                        mm = pe.matmul(PS[64 * r:64 * r + 64, 2 * b + 1, :], wff2[:, m + r, DM:D],
                                       hid[:, (FC * b + m + r) % 4, :], start=m == 0, stop=m == FC - 2)
                        mm.then_inc(s["down"].sem, 1)

                def tile(t, b, more):
                    for m in range(2, FC + 2, 2):
                        up(t, b, m - 1)
                        if m < FC:
                            up(t, b, m)
                        elif more:
                            up(t + 1, 1 - b, 0)
                        down(t, b, m - 2)

                up(0, 0, 0)
                with pe.Fori(0, NT // 2 - 1) as i:
                    for b in range(2):
                        tile(2 * i + b, b, True)
                tile(last - 1, 0, True)
                tile(last, 1, False)

            pe.wait_ge(em_raw.sem, em_raw.done(last))
            pe.wait_ge(em_xt.sem, em_xt.done(last))
            feed_forward(ffs[0])

            def win_qk(i, b, u):
                t, item = 2 * i + b, win_item(i, b, (WQ, WK, WQK)[u])
                if u == 0:
                    pe.wait_ge(w_y.sem, w_y.done(t))
                pe.wait_ge(*item.free())
                w = kparts(wqkv, slice(P * u, P * u + P))
                for k in range(2):
                    mm = pe.matmul(PS[:, item.bank, :], w[k], ys[0:KROWS[k], b, k, :], start=k == 0, stop=k == 1)
                mm.then_inc(w_fill.sem, 1)

            def win_v(i, b, g):
                item = win_item(i, b, WV + g)
                pe.wait_ge(*item.free())
                w = kparts(wqkv, slice(2 * D, 3 * D))
                for r in range(2):
                    a = P * (2 * g + r)
                    for k in range(2):
                        mm = pe.matmul(PS[:, item.bank, D * r:D * r + D], ys[0:KROWS[k], b, k, a:a + P], w[k],
                                       start=k == 0, stop=k == 1)
                mm.then_inc(w_fill.sem, 1)

            def win_scores(i, b, p):
                pair = 4 * (2 * i + b) + p
                for u in (WQ, WK, WQK):
                    pe.wait_ge(*win_item(i, b, u).drained())
                pe.wait_ge(w_sub.sem, w_sub.done(pair - 1))
                for part in range(2):
                    for r in range(2):
                        img = 2 * p + r
                        q = slice(WIN * img, WIN * img + WIN)
                        o = slice(WIN * r, WIN * r + WIN)
                        rr, h0, h1 = ((slice(0, P), 0, HM), (slice(DT, P), HM, NH))[part]
                        mm = pe.matmul(PS[o, part, 0:(h1 - h0) * WIN].rearrange("p (h n) -> p h n", n=WIN),
                                       qT[rr, b, part, q], kbd[rr, b, img, h0:h1, :], start=True, stop=True)
                mm.then_inc(w_s.sem, 1)

            def win_turn(i, b, p):
                pair = 4 * (2 * i + b) + p
                pe.wait_ge(w_norm.sem, w_norm.done(pair))
                pe.wait_ge(w_et.sem, w_et.done(pair - 1))
                for hp in range(NH // 2):
                    tr = pe.transpose(PS[:, 2 + hp // 4, P * (hp % 4):P * (hp % 4) + P],
                                      E[:, p % 2, P * hp:P * hp + P], ident)
                tr.then_inc(w_tr.sem, 1)

            def win_values(i, b, p):
                pair = 4 * (2 * i + b) + p
                pe.wait_ge(w_et.sem, w_et.done(pair))
                if p == 0:
                    for g in range(2):
                        pe.wait_ge(*win_item(i, b, WV + g).drained())
                    pe.wait_ge(w_o.sem, w_o.done(2 * i + b - 1))
                for r in range(2):
                    img = 2 * p + r
                    for hp in range(NH // 2):
                        o = 32 * (hp % 4)
                        mm = pe.matmul(PS[o:o + 32, 4 + hp // 4, WIN * img:WIN * img + WIN],
                                       vbd[:, b, img, 32 * hp:32 * hp + 32],
                                       ETb[:, p % 2, P * hp + WIN * r:P * hp + WIN * r + WIN],
                                       start=True, stop=True)
                mm.then_inc(w_pv.sem, 1)

            def win_proj(i, b, u, ending=False):
                if u == 0:
                    pe.wait_ge(w_o.sem, w_o.done(2 * i + b))
                item = win_item_proj(i, b, u, ending)
                pe.wait_ge(*item.free())
                w = kparts(wproj, halves(u))
                for k in range(2):
                    mm = pe.matmul(PS[0:KROWS[u], item.bank, :], w[k], oT[0:KROWS[k], k, :], start=k == 0, stop=k == 1)
                mm.then_inc(w_fill.sem, 1)

            def win_skip_fill(i, b):
                pe.wait_ge(*win_item(i, b, WQK).filled())
                pe.sem_inc(w_fill.sem, 2)

            def win_tile(i, b, first=False, more=True):
                before, behind = win_neighbours(i, b)
                win_scores(i, b, 0)
                if not first:
                    win_turn(*before, 3)
                if more:
                    win_qk(*behind, 0)
                if not first:
                    win_values(*before, 3)
                if more:
                    win_qk(*behind, 1)
                win_scores(i, b, 1)
                win_turn(i, b, 0)
                if more:
                    win_qk(*behind, 2)
                if first:
                    win_skip_fill(*behind)
                win_values(i, b, 0)
                win_scores(i, b, 2)
                win_turn(i, b, 1)
                if not first:
                    win_proj(*before, 0, not more)
                win_values(i, b, 1)
                if not first:
                    win_proj(*before, 1, not more)
                win_scores(i, b, 3)
                win_turn(i, b, 2)
                if more:
                    win_v(*behind, 0)
                win_values(i, b, 2)
                if more:
                    win_v(*behind, 1)

            pe.wait_ge(ffs[0]["out"].sem, ffs[0]["out"].done(last))
            pe.wait_ge(ffs[0]["gelu"].sem, ffs[0]["gelu"].done(FC * NT - 1))
            win_qk(0, 0, 0)
            win_qk(0, 0, 1)
            win_qk(0, 0, 2)
            win_skip_fill(0, 0)
            for g in range(2):
                win_v(0, 0, g)
            win_tile(0, 0, first=True)
            win_tile(0, 1)
            with pe.Fori(1, NT // 2 - 1) as i:
                for b in range(2):
                    win_tile(i, b)
            win_tile(NT // 2 - 1, 0)
            win_tile(NT // 2 - 1, 1, more=False)
            win_turn(NT // 2 - 1, 1, 3)
            win_values(NT // 2 - 1, 1, 3)
            for u in range(2):
                win_proj(NT // 2 - 1, 1, u, True)

            for u in range(2):
                pe.wait_ge(*win_item_proj(NT // 2 - 1, 1, u, True).drained())
            pe.wait_ge(w_sub.sem, w_sub.done(4 * last + 3))
            pe.wait_ge(w_o.sem, w_o.done(last))
            feed_forward(ffs[1])

            def grp_qk(t, b):
                pe.wait_ge(g_hs.sem, g_hs.done(t))
                for u in range(3):
                    pe.wait_ge(g_drain.sem, g_drain.recycled(GU * t + u))
                    w = kparts(wqkv2, slice(P * u, P * u + P))
                    for k in range(2):
                        mm = pe.matmul(PS[:, grp_bank(b, u), :], w[k], hs[0:KROWS[k], b, k, :], start=k == 0, stop=k == 1)
                    mm.then_inc(g_fill.sem, 1)

            def grp_v(t, b):
                w = kparts(wqkv2, slice(2 * D, 3 * D))
                for u in (3, 4):
                    pe.wait_ge(g_drain.sem, g_drain.recycled(GU * t + u))
                    for r in range(2):
                        j = 2 * (u - 3) + r
                        for k in range(2):
                            mm = pe.matmul(PS[:, grp_bank(b, u), D * r:D * r + D],
                                           hs[0:KROWS[k], b, k, P * j:P * j + P], w[k], start=k == 0, stop=k == 1)
                    mm.then_inc(g_fill.sem, 1)

            def grp_scores(t):
                pe.wait_ge(g_drain.sem, g_drain.done(GU * t + 2))
                for j in range(BPT):
                    for r in range(2):
                        a = slice(P * j + WIN * r, P * j + WIN * r + WIN)
                        for k in range(2):
                            mm = pe.matmul(PS[WIN * r:WIN * r + WIN, 2, WIN * j:WIN * j + WIN],
                                           q2[0:KROWS[k], k, a], k2[0:KROWS[k], k, a], start=k == 0, stop=k == 1)
                mm.then_inc(g_a.sem, 1)
                for j in range(BPT):
                    for k in range(2):
                        mm = pe.matmul(PS[:, 3, GP * j:GP * j + GP], q2[0:KROWS[k], k, P * j:P * j + P],
                                       wgp[0:KROWS[k], k, :], start=k == 0, stop=k == 1)
                mm.then_inc(g_a.sem, 1)

            def grp_turn_probs(t):
                pe.wait_ge(g_gw.sem, g_gw.done(t))
                pe.sem_inc(met_pe, 1)
                for j in range(BPT):
                    tr = pe.transpose(PS[0:GP, 4, P * j:P * j + P], lE[:, j, :], ident)
                tr.then_inc(g_gt.sem, 1)

            def grp_group(t):
                pe.wait_ge(g_gtc.sem, g_gtc.done(t))
                pe.sem_inc(met_pe, 1)
                for j in range(BPT):
                    for r in range(2):
                        a = slice(P * j + WIN * r, P * j + WIN * r + WIN)
                        mm = pe.matmul(PS[WIN * r:WIN * r + WIN, 5, WIN * j:WIN * j + WIN], gT[0:GP, a], gT[0:GP, a],
                                       start=True, stop=True)
                mm.then_inc(g_grp.sem, 1)

            def grp_turn_rows(t):
                pe.wait_ge(g_norm.sem, g_norm.done(t))
                for j in range(BPT):
                    pe.transpose(PS[:, 2, P * j:P * j + P], zw[:, j, 0:DM], ident)
                    tr = pe.transpose(PS[0:DT, 3, P * j:P * j + P], zw[:, j, DM:D], ident)
                tr.then_inc(g_tr.sem, 1)

            def grp_turn_weights(t):
                pe.wait_ge(g_wb.sem, g_wb.done(t))
                pe.wait_ge(g_ht.sem, g_ht.done(t - 1))
                for j in range(BPT):
                    tr = pe.transpose(PS[:, 3, P * j:P * j + P], wb[:, j, :], ident)
                tr.then_inc(g_wt.sem, 1)

            def grp_logits(t):
                pe.wait_ge(g_ht.sem, g_ht.done(t))
                for j in range(BPT):
                    for k in range(2):
                        mm = pe.matmul(PS[:, 6, NE * j:NE * j + NE], hT2[0:KROWS[k], k, P * j:P * j + P],
                                       wgate[0:KROWS[k], k, :], start=k == 0, stop=k == 1)
                mm.then_inc(g_lg.sem, 1)

            def grp_values(t, b):
                pe.wait_ge(g_wtc.sem, g_wtc.done(t))
                pe.wait_ge(g_drain.sem, g_drain.done(GU * t + 4))
                for k in range(2):
                    for j in range(BPT):
                        mm = pe.matmul(PS[0:KROWS[k], 4 + k, P * j:P * j + P], v2[:, b, j, halves(k)],
                                       wT[:, P * j:P * j + P], start=True, stop=True)
                mm.then_inc(g_pv.sem, 1)

            def grp_rows(t, b):
                pe.wait_ge(g_oc.sem, g_oc.done(t))
                pe.wait_ge(g_lgc.sem, g_lgc.done(t - 1))
                for j in range(BPT):
                    a = slice(P * j, P * j + P)
                    o, lo = PS[:, 6 + j // 2, :], D * (j % 2)
                    for k in range(2):
                        pe.matmul(o[:, lo:lo + D], oT2[0:KROWS[k], k, a], wproj2[0:KROWS[k], k, :],
                                  start=k == 0, stop=k == 1)
                    pe.matmul(o[:, lo:lo + DM], hs[:, b, 0, a], ident, start=False, stop=True, skip_group_check=True)
                    mm = pe.matmul(o[:, lo + DM:lo + D], hs[0:DT, b, 1, a], ident[0:DT, 0:DT], start=False, stop=True,
                                   skip_group_check=True)
                mm.then_inc(g_z.sem, 1)

            def grp_tile(t, b, first=False, final=False):
                grp_scores(t)
                if not final:
                    grp_qk(t + 1, 1 - b)
                grp_turn_probs(t)
                if not final:
                    grp_v(t + 1, 1 - b)
                grp_group(t)
                if not first:
                    grp_turn_rows(t - 1)
                grp_turn_weights(t)
                if not first:
                    grp_logits(t - 1)
                grp_values(t, b)
                grp_rows(t, b)

            pe.wait_ge(ffs[1]["out"].sem, ffs[1]["out"].done(last))
            pe.wait_ge(ffs[1]["gelu"].sem, ffs[1]["gelu"].done(FC * NT - 1))
            grp_qk(0, 0)
            grp_v(0, 0)
            grp_tile(0, 0, first=True)
            with pe.Fori(0, NT // 2 - 1) as i:
                grp_tile(2 * i + 1, 1)
                grp_tile(2 * i + 2, 0)
            grp_tile(last, 1, final=True)
            grp_turn_rows(last)
            grp_logits(last)

            pe.wait_ge(r_mask, 1)
            pe.wait_ge(g_lgc.sem, g_lgc.done(last))
            chosen, earlier = R[7].rearrange("p b n -> p (b n)"), R[5].rearrange("p b n -> p (b n)")
            pe.matmul(PS[:, 0, :], c("before"), chosen, start=True, stop=False)
            pe.matmul(PS[:, 0, :], c("ones"), earlier, start=False, stop=True)
            pe.matmul(PS[:, 1, 0:NE], c("ones"), R[4][:, NB - 1, :], start=True, stop=True).then_inc(r_pos, 1)

            def sh_turn(t, b):
                pe.wait_ge(s_x.sem, s_x.done(t))
                pe.wait_ge(s_xt.sem, s_xt.done(t - 1))
                for j in range(BPT):
                    pe.transpose(PS[:, 0, P * j:P * j + P], shx[:, j, 0:DM], ident)
                    tr = pe.transpose(PS[0:DT, 1, P * j:P * j + P], shx[:, j, DM:D], ident)
                tr.then_inc(s_tr.sem, 1)

            def sh_up(t, b, m):
                n = SC * t + m
                if m == 0:
                    pe.wait_ge(s_xt.sem, s_xt.done(t))
                pe.wait_ge(s_gg.sem, s_gg.recycled(n))
                for g in range(2):
                    o = PS[:, 2 + 2 * (m % 2) + g, :]
                    a = slice(64 * g, 64 * g + 64)
                    pe.matmul(o, shw13[:, SI * g + P * m:SI * g + P * m + P], sxT[:, b, 0, :], start=True, stop=False)
                    pe.matmul(o, shwt[a, P * m:P * m + P], sxT[a, b, 1, :], start=False, stop=True)\
                        .then_inc(s_up.sem, 1)

            def sh_down(t, m):
                n = SC * t + m
                pe.wait_ge(s_gg.sem, s_gg.done(n))
                if m == 0:
                    pe.wait_ge(s_z.sem, s_z.done(t - 1))
                for j in range(BPT):
                    mm = pe.matmul(PS[:, 6 + j // 2, D * (j % 2):D * (j % 2) + D], gg[:, m % 2, P * j:P * j + P],
                                   shw2[:, m, :], start=m == 0 and j % 2 == 0, stop=m == SC - 1,
                                   skip_group_check=True)
                mm.then_inc(s_dn.sem, 1)

            def sh_tile(t, b, more):
                sh_up(t, b, 0)
                for m in range(1, SC):
                    sh_up(t, b, m)
                    sh_down(t, m - 1)
                    if m == SC // 2 and more:
                        sh_turn(t + 1, 1 - b)
                sh_down(t, SC - 1)

            pe.wait_ge(shared_in, 16)
            pe.wait_ge(r_done, 1)
            sh_turn(0, 0)
            with pe.Fori(0, NT // 2 - 1) as i:
                for b in range(2):
                    sh_tile(2 * i + b, b, True)
            sh_tile(last - 1, 0, True)
            sh_tile(last, 1, False)

            def ex_turn(j, b, i):
                pe.wait_ge(e_in[b], 16 * (i + 1))
                pe.wait_ge(e_xt.sem, e_xt.recycled(j))
                pe.transpose(PS[:, 4 + b, 0:P], xg[:, b, 0:DM], ident)
                pe.transpose(PS[0:DT, 4 + b, P:2 * P], xg[:, b, DM:D], ident).then_inc(e_tr.sem, 1)

            def ex_up(j, b, g):
                if g == 0:
                    pe.wait_ge(e_xt.sem, e_xt.done(j))
                    pe.wait_ge(e_w.sem, e_w.done(j))
                    pe.wait_ge(e_silu.sem, e_silu.recycled(j))
                else:
                    pe.wait_ge(e_g.sem, e_g.recycled(j))
                tail = slice(DT * g, DT * g + DT)
                for q in range(MI // P):
                    o, a = PS[:, 2 * g + b, P * q:P * q + P], slice(P * q, P * q + P)
                    pe.matmul(o, ew[:, b, MI * g:MI * g + MI][:, a], exT[:, b, 0, :], start=True, stop=False)
                    mm = pe.matmul(o, ew[tail, b, 2 * MI:3 * MI][:, a], exT[tail, b, 1, :], start=False, stop=True)
                mm.then_inc((e_h1, e_h3)[g].sem, 1)

            def ex_down(j, b):
                w = weights_at(pe, j)
                pe.wait_ge(e_g.sem, e_g.done(j))
                pe.wait_ge(e_ys.sem, e_ys.recycled(j))
                for q in range(MI // P):
                    mm = pe.matmul(PS[:, 6 + b, 0:D], eg[:, b, P * q:P * q + P],
                                   mem[:, bass.ds(w + 3 * MI + D * q, D)], start=q == 0, stop=q == MI // P - 1)
                mm.then_inc(e_y.sem, 1)

            def ex_step(j, b, i_next, first=False, final=False):
                ex_up(j, b, 0)
                if not final:
                    ex_turn(j + 1, 1 - b, i_next)
                ex_up(j, b, 1)
                if not first:
                    ex_down(j - 1, 1 - b)

            pe.wait_ge(experts_in, 16 * (NE - 1))
            pe.wait_ge(lastw_in, 16)
            pe.wait_ge(s_z.sem, s_z.done(last))
            pe.wait_ge(s_gg.sem, s_gg.done(SC * NT - 1))
            ex_turn(0, 0, 0)
            ex_step(0, 0, 0, first=True)
            with pe.Fori(0, (ET - 3) // 2) as i:
                ex_step(2 * i + 1, 1, i + 1)
                ex_step(2 * i + 2, 0, i + 1)
            ex_step(ET - 2, 1, (ET - 1) // 2)
            ex_step(ET - 1, 0, 0, final=True)
            ex_down(ET - 1, 0)

        @block.scalar
        def _(act):
            for dst, name in ((wff1, "ff1_w"), (wff2, "ff2_w"), (wqkv, "qkv_w"), (wproj, "proj_w"),
                              (wqkv2, "qkv2_w"), (wproj2, "proj2_w"), (wgp, "gp_w"), (wgate, "gate_w")):
                if name == "ff2_w":
                    act.dma_start(dst, d[name]).then_inc(early_in, 16)
                    continue
                src = d[name]
                if name in ("ff1_w", "qkv_w", "qkv2_w"):
                    act.dma_start(dst[:, 0, :], src[0:DM, :]).then_inc(early_in, 16)
                    act.dma_start(dst[0:DT, 1, :], src[DM:D, :]).then_inc(early_in, 16)
                else:
                    act.dma_start(dst[:, 0, :], src[0:DM, :]).then_inc(early_in, 16)
                    act.dma_start(dst[0:DT, 1, :], src[DM:D, :]).then_inc(early_in, 16)
            act.wait_ge(late_in, 64)
            act.activation(mix[:, 0:1], alpha, ACT.Exp, scale=-1.0).then_inc(exp_alpha, 1)
            for s in (em_xt, ffs[0]["gelu"], ffs[1]["gelu"], w_exp, w_et, w_o, g_exp, g_gtc, g_wtc, g_oc, g_ht,
                      s_x, s_xt, s_silu, e_xt, e_silu, e_w):
                s.start(act)

            with act.Fori(0, NT // 2) as i:
                for b in range(2):
                    t = 2 * i + b
                    act.wait_ge(em_tr.sem, em_tr.done(t))
                    for k in range(2):
                        act.copy(XT[0:KROWS[k], k, bass.ds(t * TT, TT)], PS[0:KROWS[k], 4 + 2 * k + b, :])\
                            .then_inc(em_xt.sem, 1)

            def gelus(s):
                with act.Fori(0, NT // 2) as i:
                    for q in range(2 * FC):
                        m, n = q % FC, 2 * FC * i + q
                        act.wait_ge(s["up"].sem, s["up"].done(n))
                        act.wait_ge(s["down"].sem, s["down"].recycled(n))
                        act.activation(hid[:, q % 4, :], PS[:, 4 + m % 3, :], ACT.Gelu_apprx_tanh,
                                       bias=bcols[:, _B["ff1"]][:, m:m + 1]).then_inc(s["gelu"].sem, 1)

            act.wait_ge(em_mm.sem, em_mm.done(last))
            act.wait_ge(em_raw.sem, em_raw.done(last))
            gelus(ffs[0])

            def win_exp(pair, p):
                act.wait_ge(w_sub.sem, w_sub.done(pair))
                act.activation(E[:, p % 2, :], E[:, p % 2, :], ACT.Exp).then_inc(w_exp.sem, 1)

            def win_turned(pair, p):
                act.wait_ge(w_tr.sem, w_tr.done(pair))
                act.wait_ge(w_pv.sem, w_pv.recycled(pair))
                act.copy(ETb[:, p % 2, 0:512], PS[:, 2, :]).then_inc(w_et.sem, 1)
                act.copy(ETb[:, p % 2, 512:], PS[:, 3, 0:NH * WIN - 512]).then_inc(w_et.sem, 1)

            def win_heads(i, b):
                t = 2 * i + b
                act.wait_ge(w_pv.sem, w_pv.done(4 * t + 3))
                for k in range(2):
                    act.activation(oT[0:KROWS[k], k, :], PS[0:KROWS[k], 4 + k, :], ACT.Identity,
                                   bias=bc("v", k, KROWS[k])).then_inc(w_o.sem, 1)

            def win_q_main(i, b):
                item = win_item(i, b, WQ)
                act.wait_ge(*item.filled())
                act.activation(qT[:, b, 0, :], PS[:, item.bank, :], ACT.Identity, bias=qbias[:, 0:1],
                               scale=float(DH) ** -0.5).then_inc(item.drain.sem, 1)

            def win_k_main(i, b, heads):
                item = win_item(i, b, WK)
                act.wait_ge(*item.filled())
                for h in heads:
                    ins = act.activation(kbd[:, b, :, h, :], PS[:, item.bank, :].rearrange("p (i n) -> p i n", i=IPT),
                                         ACT.Identity, bias=kbias[:, h:h + 1], scale=kmask[:, h:h + 1])
                if heads[-1] == HM - 1:
                    ins.then_inc(item.drain.sem, 1)

            def win_tile_act(i, b, first=False, more=True):
                t = 2 * i + b
                before, behind = win_neighbours(i, b)
                if not first:
                    win_turned(4 * t - 1, 3)
                win_exp(4 * t, 0)
                if more:
                    win_q_main(*behind)
                if not first:
                    win_heads(*before)
                if more:
                    win_k_main(*behind, range(0, HM // 2))
                win_turned(4 * t, 0)
                win_exp(4 * t + 1, 1)
                if more:
                    win_k_main(*behind, range(HM // 2, HM))
                if first:
                    win_skip(act, *behind, WK)
                win_turned(4 * t + 1, 1)
                win_exp(4 * t + 2, 2)
                win_turned(4 * t + 2, 2)
                win_exp(4 * t + 3, 3)

            act.wait_ge(consts_ready, 5)
            act.wait_ge(ffs[0]["down"].sem, ffs[0]["down"].done(FC * NT - 1))
            win_q_main(0, 0)
            win_k_main(0, 0, range(HM))
            win_skip(act, 0, 0, WK)
            win_tile_act(0, 0, first=True)
            win_tile_act(0, 1)
            with act.Fori(1, NT // 2 - 1) as i:
                for b in range(2):
                    win_tile_act(i, b)
            win_tile_act(NT // 2 - 1, 0)
            win_tile_act(NT // 2 - 1, 1, more=False)
            win_turned(4 * last + 3, 3)
            win_heads(NT // 2 - 1, 1)
            for u in range(2):
                act.wait_ge(*win_item_proj(NT // 2 - 1, 1, u, True).drained())
            gelus(ffs[1])

            SCALE = float(D) ** -0.5

            def grp_exps(t):
                act.wait_ge(g_dif.sem, g_dif.done(t, 0))
                act.activation(sE, sE, ACT.Exp, scale=SCALE).then_inc(g_exp.sem, 1)
                act.wait_ge(g_dif.sem, g_dif.done(t, 1))
                act.activation(lE, lE, ACT.Exp).then_inc(g_exp.sem, 1)

            def grp_copies(t, k0, signal_in, signal_out, dst):
                act.wait_ge(signal_in.sem, signal_in.done(t))
                for k in range(2):
                    act.copy(dst[0:KROWS[k], k, :], PS[0:KROWS[k], k0 + k, :]).then_inc(signal_out.sem, 1)

            def grp_tile_act(t, first=False):
                grp_exps(t)
                act.wait_ge(g_gt.sem, g_gt.done(t))
                act.copy(gT[0:GP, :], PS[0:GP, 4, :]).then_inc(g_gtc.sem, 1)
                if not first:
                    grp_copies(t - 1, 2, g_tr, g_ht, hT2)
                act.wait_ge(g_wt.sem, g_wt.done(t))
                act.copy(wT, PS[:, 3, :]).then_inc(g_wtc.sem, 1)
                grp_copies(t, 4, g_pv, g_oc, oT2)

            grp_tile_act(0, first=True)
            with act.Fori(1, NT) as t:
                grp_tile_act(t)
            grp_copies(last, 2, g_tr, g_ht, hT2)

            act.wait_ge(r_chain, 2)
            act.activation(R[1], R[0], ACT.Exp).then_inc(r_exp, 1)

            def sh_rows(t):
                act.wait_ge(s_tr.sem, s_tr.done(t - 1))
                act.copy(shx, H2X[:, bass.ds(t * BPT, BPT), 0:D]).then_inc(s_x.sem, 1)

            def sh_turned(t, b):
                act.wait_ge(s_tr.sem, s_tr.done(t))
                act.copy(sxT[:, b, 0, :], PS[:, 0, :]).then_inc(s_xt.sem, 1)
                for a in (slice(0, 64), slice(64, 128)):
                    act.copy(sxT[a, b, 1, :], PS[0:DT, 1, :]).then_inc(s_xt.sem, 1)

            def sh_tile_act(t, b, more):
                for m in range(SC):
                    n = SC * t + m
                    act.wait_ge(s_up.sem, s_up.done(n, 0))
                    act.wait_ge(s_gg.sem, s_gg.recycled(n))
                    act.activation(sil[:, m % 2, :], PS[:, 2 + 2 * (m % 2), :], ACT.Silu).then_inc(s_silu.sem, 1)
                    if m == SC // 2 - 1 and more:
                        sh_rows(t + 1)
                    if m == SC // 2 and more:
                        sh_turned(t + 1, 1 - b)

            act.wait_ge(r_done, 1)
            sh_rows(0)
            sh_turned(0, 0)
            with act.Fori(0, NT // 2 - 1) as i:
                for b in range(2):
                    sh_tile_act(2 * i + b, b, True)
            sh_tile_act(last - 1, 0, True)
            sh_tile_act(last, 1, False)

            def ex_weights(j, b):
                w = weights_at(act, j)
                act.wait_ge(e_h3.sem, e_h3.recycled(j))
                act.copy(ew[:, b, :], mem[:, bass.ds(w, 3 * MI)]).then_inc(e_w.sem, 1)

            def ex_turned(j, b):
                act.wait_ge(e_tr.sem, e_tr.done(j))
                act.wait_ge(e_h3.sem, e_h3.recycled(j))
                act.copy(exT[:, b, 0, :], PS[:, 4 + b, 0:P])
                act.copy(exT[0:64, b, 1, :], PS[0:DT, 4 + b, P:2 * P])
                act.copy(exT[64:128, b, 1, :], PS[0:DT, 4 + b, P:2 * P]).then_inc(e_xt.sem, 1)

            def ex_silu(j, b):
                act.wait_ge(e_h1.sem, e_h1.done(j))
                act.wait_ge(e_g.sem, e_g.recycled(j))
                act.activation(esil[:, b, :], PS[:, b, :], ACT.Silu).then_inc(e_silu.sem, 1)

            def ex_step_act(j, b, final=False):
                if not final:
                    ex_weights(j + 1, 1 - b)
                ex_silu(j, b)
                if not final:
                    ex_turned(j + 1, 1 - b)

            act.wait_ge(s_z.sem, s_z.done(last))
            act.wait_ge(scattered, NT)
            act.wait_ge(s_acc, 16 + 16 * NT)
            act.wait_ge(experts_in, 16 * (NE - 1))
            act.wait_ge(lastw_in, 16)
            ex_weights(0, 0)
            ex_turned(0, 0)
            with act.Fori(0, (ET - 1) // 2) as i:
                ex_step_act(2 * i, 0)
                ex_step_act(2 * i + 1, 1)
            ex_step_act(ET - 1, 0, final=True)

        @block.vector
        def _(dve):
            for s in (em_raw, em_norm, ffs[0]["out"], ffs[1]["out"], ffs[0]["half"], ffs[1]["half"], *w_drain, w_mx, w_sub, w_sum, w_rs, g_drain, g_mx,
                      g_dif, g_sum, g_gw, g_t1, g_wb, g_raw, g_norm, g_lgc, s_gg, s_z, e_g, e_ys, e_gate):
                s.start(dve)
            dve.wait_ge(late_in, 64)

            def rows(r, n):
                return rows5[:, r, :].unsqueeze(1).broadcast_to([P, n, D])

            def two(bank):
                return PS[:, bank, 0:2 * D].rearrange("p (j n) -> p j n", j=2)

            dve.wait_ge(exp_alpha, 1)
            dve.tensor_scalar(mix[:, 1:2], mix[:, 0:1], 1.0, None, ALU.add).then_inc(consts_ready, 1)
            dve.wait_ge(consts_ready, 1)
            dve.reciprocal(mix[:, 2:3], mix[:, 1:2]).then_inc(consts_ready, 1)
            dve.wait_ge(consts_ready, 2)
            dve.tensor_scalar(mix[:, 3:4], mix[:, 2:3], -1.0, 1.0, ALU.mult, ALU.add).then_inc(consts_ready, 1)
            qk = bcols[:, _B["qk"]]
            dve.tensor_scalar(qbias, qk[:, 0:1], float(DH) ** -0.5, None, ALU.mult).then_inc(consts_ready, 1)
            dve.tensor_tensor(kbias, kmask, qk[:, 1:2].broadcast_to([P, HM]), ALU.mult).then_inc(consts_ready, 1)

            with dve.Fori(0, NT // 2) as i:
                for b in range(2):
                    t = 2 * i + b
                    dve.wait_ge(em_mm.sem, em_mm.done(t))
                    dve.wait_ge(em_tr.sem, em_tr.recycled(t))
                    for g in range(2):
                        dve.tensor_tensor(xw[:, b, 2 * g:2 * g + 2, :], two(2 * b + g), rows(0, 2), ALU.add)\
                            .then_inc(em_raw.sem, 1)
                    dve.wait_ge(em_raw.sem, em_raw.done(t))
                    chain = Chain(dve, em_chain, N_EMBED * t)
                    norm_stats(dve, chain, [xw[:, b, j, :] for j in range(BPT)], stats, mv, rstd, tmp4, met_dve)
                    assert chain.n == N_EMBED
                    for j in range(BPT):
                        dve.tensor_scalar(xw[:, b, j, :], xw[:, b, j, :], mv[:, j, 0:1], rstd[:, j:j + 1],
                                          ALU.subtract, ALU.mult).then_inc(em_norm.sem, 1)

            def ff_banks(s, residual):
                with dve.Fori(0, NT // 2) as i:
                    for b in range(2):
                        t = 2 * i + b
                        dve.wait_ge(s["down"].sem, s["down"].done(FC * t + FC - 1))
                        lo, n = slice(0, DT), s["half"]
                        dst = XT if residual else YT
                        main, tail = dst[:, 0, bass.ds(t * TT, TT)], dst[lo, 1, bass.ds(t * TT, TT)]
                        if residual:
                            dve.scalar_tensor_tensor(out=tail, in0=PS[lo, 2 * b + 1, :], scalar=bc("ff2", 1, DT),
                                                     in1=tail, op0=ALU.add, op1=ALU.add).then_inc(n.sem, 1)
                            dve.scalar_tensor_tensor(out=main, in0=PS[:, 2 * b, :], scalar=bc("ff2", 0), in1=main,
                                                     op0=ALU.add, op1=ALU.add).then_inc(s["out"].sem, 1)
                        else:
                            dve.tensor_scalar(tail, PS[lo, 2 * b + 1, :], bc("ff2", 1, DT), None, ALU.add)\
                                .then_inc(n.sem, 1)
                            dve.tensor_scalar(main, PS[:, 2 * b, :], bc("ff2", 0), None, ALU.add)\
                                .then_inc(s["out"].sem, 1)
                        dve.wait_ge(n.sem, n.done(t))
                        dve.tensor_tensor(tail, PS[DT:P, 2 * b + 1, :], tail, ALU.add).then_inc(s["out"].sem, 1)

            ff_banks(ffs[0], False)

            def win_tails(i, b, ops):
                item, qk = win_item(i, b, WQK), bcols[:, _B["qk"]]
                dve.wait_ge(*item.filled())
                for op in ops:
                    if op == 0:
                        ins = dve.tensor_scalar(qT[DT:P, b, 1, :], PS[0:DT, item.bank, :], qk[0:DT, 2:3],
                                                float(DH) ** -0.5, ALU.add, ALU.mult)
                    else:
                        mine = DT // DH + op - 1
                        ins = dve.tensor_scalar(kbd[DT:P, b, :, HM + op - 1, :],
                                                PS[DT:P, item.bank, :].rearrange("p (i n) -> p i n", i=IPT),
                                                qk[DT:P, 2:3], kmask[DT:P, mine:mine + 1], ALU.add, ALU.mult)
                if ops[-1] == NH - HM:
                    ins.then_inc(item.drain.sem, 1)

            def win_v(i, b, g):
                item = win_item(i, b, WV + g)
                dve.wait_ge(*item.filled())
                for image in range(2):
                    for odd in range(2):
                        src = two(item.bank)[WIN * image:WIN * image + WIN]
                        dst = vbd[WIN * odd:WIN * odd + WIN, b, 4 * g + image:4 * g + 4:2, :]
                        src, dst = (x.rearrange("p j (g h n) -> p j g h n", h=2, n=DH)[:, :, :, odd, :] for x in (src, dst))
                        ins = dve.tensor_copy(dst, src)
                ins.then_inc(item.drain.sem, 1)

            def heads(x):
                return x.rearrange("p (h n) -> p h n", h=NH)

            def win_shift(pair, p):
                s = heads(PS[:, 0:2, :].rearrange("p b n -> p (b n)")[:, 0:NH * WIN])
                dve.wait_ge(w_s.sem, w_s.done(pair))
                dve.tensor_reduce(mx12[:, p % 2, :], s, AX, ALU.max).then_inc(w_mx.sem, 1)
                dve.wait_ge(w_mx.sem, w_mx.done(pair))
                dve.wait_ge(w_tr.sem, w_tr.recycled(pair))
                dve.tensor_tensor(heads(E[:, p % 2, :]), s,
                                  mx12[:, p % 2, :].unsqueeze(2).broadcast_to([P, NH, WIN]), ALU.subtract)\
                    .then_inc(w_sub.sem, 1)

            def win_sum(pair, p):
                dve.wait_ge(w_exp.sem, w_exp.done(pair))
                dve.tensor_reduce(sm12[:, p % 2, :], heads(E[:, p % 2, :]), AX, ALU.add).then_inc(w_sum.sem, 1)
                dve.wait_ge(w_sum.sem, w_sum.done(pair))
                dve.reciprocal(sm12[:, p % 2, :], sm12[:, p % 2, :]).then_inc(w_rs.sem, 1)

            def win_drain_proj(i, b, k, ending=False):
                rr, item = slice(0, KROWS[k]), win_item_proj(i, b, k, ending)
                dve.wait_ge(*item.filled())
                x = XT[rr, k, bass.ds((2 * i + b) * TT, TT)]
                dve.scalar_tensor_tensor(out=x, in0=PS[rr, item.bank, :], scalar=bc("proj", k, KROWS[k]), in1=x,
                                         op0=ALU.add, op1=ALU.add).then_inc(item.drain.sem, 1)

            def win_tile_dve(i, b, first=False, more=True):
                t = 2 * i + b
                before, behind = win_neighbours(i, b)
                win_shift(4 * t, 0)
                win_sum(4 * t, 0)
                win_shift(4 * t + 1, 1)
                win_sum(4 * t + 1, 1)
                if more:
                    win_tails(*behind, range(0, 3))
                win_shift(4 * t + 2, 2)
                if more:
                    win_tails(*behind, range(3, NH - HM + 1))
                if first:
                    win_skip(dve, *behind, WQK)
                win_sum(4 * t + 2, 2)
                if not first:
                    win_drain_proj(*before, 0, not more)
                win_shift(4 * t + 3, 3)
                if not first:
                    win_drain_proj(*before, 1, not more)
                win_sum(4 * t + 3, 3)
                if more:
                    win_v(*behind, 0)
                    win_v(*behind, 1)

            dve.wait_ge(ffs[0]["down"].sem, ffs[0]["down"].done(FC * NT - 1))
            dve.wait_ge(w_zero, 1)
            win_tails(0, 0, range(NH - HM + 1))
            win_skip(dve, 0, 0, WQK)
            win_v(0, 0, 0)
            win_v(0, 0, 1)
            win_tile_dve(0, 0, first=True)
            win_tile_dve(0, 1)
            with dve.Fori(1, NT // 2 - 1) as i:
                for b in range(2):
                    win_tile_dve(i, b)
            win_tile_dve(NT // 2 - 1, 0)
            win_tile_dve(NT // 2 - 1, 1, more=False)
            for k in range(2):
                win_drain_proj(NT // 2 - 1, 1, k, True)
            ff_banks(ffs[1], True)

            def grp_shift(t):
                sS = PS[:, 2, 0:BPT * WIN].rearrange("p (j n) -> p j n", j=BPT)
                sL = PS[:, 3, 0:BPT * GP].rearrange("p (j n) -> p j n", j=BPT)
                for part, (s, m, dst, n) in enumerate(((sS, mxS, sE, WIN), (sL, mxL, lE, GP))):
                    dve.wait_ge(g_a.sem, g_a.done(t, part))
                    dve.tensor_reduce(m, s, AX, ALU.max).then_inc(g_mx.sem, 1)
                    dve.wait_ge(g_mx.sem, g_mx.done(t, part))
                    dve.tensor_tensor(dst, s, m.unsqueeze(2).broadcast_to([P, BPT, n]), ALU.subtract)\
                        .then_inc(g_dif.sem, 1)

            def grp_probs(t):
                dve.wait_ge(g_exp.sem, g_exp.done(t, 0))
                dve.tensor_reduce(smS, sE, AX, ALU.add).then_inc(g_sum.sem, 1)
                dve.wait_ge(g_exp.sem, g_exp.done(t, 1))
                dve.tensor_reduce(smL, lE, AX, ALU.add).then_inc(g_sum.sem, 1)
                dve.wait_ge(g_sum.sem, g_sum.done(t, 1))
                dve.reciprocal(smL, smL).then_inc(g_sum.sem, 1)
                dve.reciprocal(smS, smS).then_inc(g_sum.sem, 1)
                dve.wait_ge(g_sum.sem, g_sum.done(t))
                dve.tensor_tensor(lE, lE, smL.unsqueeze(2).broadcast_to([P, BPT, GP]), ALU.mult).then_inc(g_gw.sem, 1)
                dve.tensor_tensor(sE, sE, smS.unsqueeze(2).broadcast_to([P, BPT, WIN]), ALU.mult).then_inc(g_gw.sem, 1)

            def grp_drain(t, b, us):
                qk, lo = bcols[:, _B["qk2"]], slice(0, DT)
                for u in us:
                    bank = grp_bank(b, u)
                    dve.wait_ge(g_fill.sem, g_fill.done(GU * t + u))
                    if u < 2:
                        ins = dve.tensor_scalar((q2, k2)[u][:, 0, :], PS[:, bank, :], qk[:, u:u + 1], None, ALU.add)
                    elif u == 2:
                        dve.tensor_scalar(q2[lo, 1, :], PS[lo, bank, :], qk[lo, 2:3], None, ALU.add)
                        ins = dve.tensor_scalar(k2[lo, 1, :], PS[DT:P, bank, :], qk[DT:P, 2:3], None, ALU.add)
                    else:
                        ins = dve.tensor_tensor(v2[:, b, 2 * (u - 3):2 * (u - 3) + 2, :], two(bank), rows(3, 2), ALU.add)
                    ins.then_inc(g_drain.sem, 1)

            def grp_weights(t):
                dve.wait_ge(g_grp.sem, g_grp.done(t))
                dve.tensor_scalar(t1, PS[:, 5, 0:BPT * WIN].rearrange("p (j n) -> p j n", j=BPT), mix[:, 3:4],
                                  mix[:, 2:3], ALU.mult, ALU.add).then_inc(g_t1.sem, 1)
                dve.wait_ge(g_t1.sem, g_t1.done(t))
                dve.wait_ge(g_gw.sem, g_gw.done(t))
                for r in range(2):
                    a = slice(WIN * r, WIN * r + WIN)
                    dve.tensor_tensor(wb[a, :, a], t1[a], sE[a], ALU.mult).then_inc(g_wb.sem, 1)

            def grp_keep_logits(t):
                dve.wait_ge(g_lg.sem, g_lg.done(t))
                dve.tensor_copy(LG[:, bass.ds(t * BPT, BPT), :],
                                PS[:, 6, 0:BPT * NE].rearrange("p (j n) -> p j n", j=BPT)).then_inc(g_lgc.sem, 1)

            def grp_norm(t):
                dve.wait_ge(g_z.sem, g_z.done(t))
                dve.wait_ge(g_h2.sem, g_h2.done(t - 1))
                for g in range(2):
                    dve.tensor_tensor(zw[:, 2 * g:2 * g + 2, :], two(6 + g), rows(4, 2), ALU.add).then_inc(g_raw.sem, 1)
                dve.wait_ge(g_raw.sem, g_raw.done(t))
                chain = Chain(dve, g_chain, N_GROUP * t)
                norm_stats(dve, chain, [zw[:, j, :] for j in range(BPT)], stats, mv, rstd, tmp4, met_dve)
                for j in range(BPT):
                    dve.tensor_scalar(zw[:, j, :], zw[:, j, :], mv[:, j, 0:1], rstd[:, j:j + 1],
                                      ALU.subtract, ALU.mult).then_inc(g_norm.sem, 1)

            def grp_tile_dve(t, b, first=False, final=False):
                grp_shift(t)
                if not final:
                    grp_drain(t + 1, 1 - b, (0, 1))
                grp_probs(t)
                if not final:
                    grp_drain(t + 1, 1 - b, (2, 3, 4))
                grp_weights(t)
                if not first:
                    grp_keep_logits(t - 1)
                grp_norm(t)

            dve.wait_ge(wb_zero, 1)
            dve.wait_ge(consts_ready, 3)
            grp_drain(0, 0, range(GU))
            grp_tile_dve(0, 0, first=True)
            with dve.Fori(0, NT // 2 - 1) as i:
                grp_tile_dve(2 * i + 1, 1)
                grp_tile_dve(2 * i + 2, 0)
            grp_tile_dve(last, 1, final=True)
            grp_keep_logits(last)

            ch = Chain(dve, r_chain, 0)

            def step(ins):
                ch(ins)
                ch.join()

            def over_e(x):
                return x.unsqueeze(2).broadcast_to([P, NB, NE])

            def over_b(x):
                return x.unsqueeze(1).broadcast_to([P, NB, NE])

            top, total, m1, i1, m2, i2, p1, p2 = r1
            dve.wait_ge(g_lgc.sem, g_lgc.done(last))
            dve.wait_ge(g_h2.sem, g_h2.done(last))
            step(dve.tensor_reduce(top, LG, AX, ALU.max))
            step(dve.tensor_tensor(R[0], LG, over_e(top), ALU.subtract))
            dve.wait_ge(r_exp, 1)
            step(dve.tensor_reduce(total, R[1], AX, ALU.add))
            step(dve.reciprocal(total, total))
            step(dve.tensor_tensor(R[1], R[1], over_e(total), ALU.mult))
            scores, one1, one2 = R[1], R[2], R[3]
            for src, m, index, one in ((scores, m1, i1, one1), (R[6], m2, i2, one2)):
                if one is one2:
                    step(dve.scalar_tensor_tensor(out=R[6], in0=one1, scalar=-2.0, in1=scores, op0=ALU.mult, op1=ALU.add))
                step(dve.tensor_reduce(m, src, AX, ALU.max))
                step(dve.tensor_tensor(R[5], src, over_e(m), ALU.is_equal))
                step(dve.scalar_tensor_tensor(out=R[0], in0=R[5], scalar=-float(NE), in1=over_b(c("experts")),
                                              op0=ALU.mult, op1=ALU.add))
                step(dve.tensor_reduce(index, R[0], AX, ALU.min))
                step(dve.tensor_tensor(one, R[0], over_e(index), ALU.is_equal))
            step(dve.tensor_tensor(R[7], one1, one2, ALU.add))
            src, dst, s = R[7], R[4], 1
            while s < NB:
                ch(dve.tensor_copy(dst[:, 0:s, :], src[:, 0:s, :]))
                step(dve.tensor_tensor(dst[:, s:NB, :], src[:, s:NB, :], src[:, 0:NB - s, :], ALU.add))
                src, dst, s = dst, (R[6] if dst is R[4] else R[4]), 2 * s
            assert src is R[4]
            dve.tensor_tensor(R[5], R[4], R[7], ALU.subtract).then_inc(r_mask, 1)
            dve.wait_ge(r_pos, 1)
            step(dve.tensor_scalar(re[0].bitcast(I32), PS[:, 1, 0:NE], float(P - 1), None, ALU.add))
            step(dve.tensor_scalar(re[1].bitcast(I32), re[0].bitcast(I32), 7, None, ALU.arith_shift_right))
            step(dve.tensor_copy(re[2], re[1].bitcast(I32)))
            src, dst, s = re[2], re[3], 1
            while s < NE:
                ch(dve.tensor_copy(dst[:, 0:s], src[:, 0:s]))
                step(dve.tensor_tensor(dst[:, s:NE], src[:, s:NE], src[:, 0:NE - s], ALU.add))
                src, dst, s = dst, (re[4] if dst is re[3] else re[3]), 2 * s
            ends = src
            step(dve.tensor_tensor(re[5], ends, re[2], ALU.subtract))
            step(dve.tensor_scalar(re[6], re[5], float(P), None, ALU.mult))
            step(dve.tensor_tensor(R[0], PS[:, 0, :].rearrange("p (b n) -> p b n", b=NB), over_b(re[6]), ALU.add))
            for s, (one, place) in enumerate(((one1, p1), (one2, p2))):
                step(dve.tensor_tensor(R[6], one, R[0], ALU.mult))
                step(dve.tensor_reduce(place, R[6], AX, ALU.add))
                step(dve.tensor_copy(posi[:, s, :], place))
            ch(dve.tensor_copy(H2X[:, :, D], m1))
            ch(dve.tensor_copy(H2X[:, :, D + 1], m2))
            ch(dve.tensor_scalar(H2X[:, :, D + 2], i1, float(NE), None, ALU.add))
            ch(dve.tensor_copy(H2X[:, :, D + 3], c("token")))
            step(dve.tensor_tensor(tmap, ends.unsqueeze(1).broadcast_to([P, ET, NE]),
                                   c("tiles").unsqueeze(2).broadcast_to([P, ET, NE]), ALU.is_le))
            step(dve.tensor_reduce(emapf, tmap, AX, ALU.add))
            step(dve.tensor_scalar(emapf, emapf, float(NE - 1), None, ALU.min))
            dve.tensor_copy(emap, emapf).then_inc(r_done, 1)

            def sh_hidden(t, m):
                n = SC * t + m
                dve.wait_ge(s_silu.sem, s_silu.done(n))
                dve.wait_ge(s_up.sem, s_up.done(n))
                dve.wait_ge(s_dn.sem, s_dn.recycled(n))
                dve.tensor_tensor(gg[:, m % 2, :], sil[:, m % 2, :], PS[:, 3 + 2 * (m % 2), :], ALU.mult)\
                    .then_inc(s_gg.sem, 1)

            with dve.Fori(0, NT) as t:
                for m in range(SC):
                    sh_hidden(t, m)
                dve.wait_ge(s_dn.sem, s_dn.done(SC * t + SC - 1))
                dve.wait_ge(s_acc, 16 + 16 * t)
                for g in range(2):
                    dve.tensor_tensor(zo[:, 2 * g:2 * g + 2, :], two(6 + g), H2X[:, bass.ds(t * BPT + 2 * g, 2), 0:D],
                                      ALU.add).then_inc(s_z.sem, 1)

            ch = Chain(dve, gates_ready, 0)
            dve.wait_ge(behind_in, 16)
            ch(dve.tensor_tensor(gates, behind_rows[:, :, 2], emapf, ALU.is_equal))
            ch(dve.tensor_tensor(gates2, behind_rows[:, :, 2], emapf, ALU.not_equal))
            ch(dve.tensor_copy(tokens.bitcast(I32), behind_rows[:, :, 3]))
            ch.join()
            ch(dve.tensor_tensor(gates, gates, behind_rows[:, :, 0], ALU.mult))
            ch(dve.tensor_tensor(gates2, gates2, behind_rows[:, :, 1], ALU.mult))
            ch.join()
            ch(dve.tensor_tensor(gates, gates, gates2, ALU.add))
            ch.join()

            def ex_hidden(j, b):
                dve.wait_ge(e_silu.sem, e_silu.done(j))
                dve.wait_ge(e_h3.sem, e_h3.done(j))
                dve.wait_ge(e_y.sem, e_y.recycled(j))
                dve.tensor_tensor(eg[:, b, :], esil[:, b, :], PS[:, 2 + b, :], ALU.mult).then_inc(e_g.sem, 1)

            def ex_rows(j, b):
                dve.wait_ge(e_added.sem, e_added.recycled(j))
                dve.tensor_copy(egate[:, b:b + 1], gates[:, bass.ds(j, 1)]).then_inc(e_gate.sem, 1)
                dve.tensor_copy(tokidx[:, b:b + 1], tokens.bitcast(I32)[:, bass.ds(j, 1)]).then_inc(e_gate.sem, 1)
                dve.wait_ge(e_y.sem, e_y.done(j))
                dve.wait_ge(e_gate.sem, e_gate.done(j))
                dve.tensor_scalar(ey[:, b, :], PS[:, 6 + b, 0:D], egate[:, b:b + 1], None, ALU.mult)\
                    .then_inc(e_ys.sem, 1)

            ex_hidden(0, 0)
            with dve.Fori(0, (ET - 1) // 2) as i:
                ex_hidden(2 * i + 1, 1)
                ex_rows(2 * i, 0)
                ex_hidden(2 * i + 2, 0)
                ex_rows(2 * i + 1, 1)
            ex_rows(ET - 1, 0)

            for t in range(NT):
                dve.wait_ge(f_in[t], 32)
                chain = Chain(dve, f_chain, N_FIN * t)
                chain(dve.tensor_tensor(fin[:, t, :, :], fin[:, t, :, :], fin1[:, t, :, :], ALU.add))
                chain.join()
                norm_stats(dve, chain, [fin[:, t, j, :] for j in range(BPT)], stats, mv, rstd, tmp4, met_dve)
                for j in range(BPT):
                    dve.tensor_scalar(fout[:, t, j, :], fin[:, t, j, :], mv[:, j, 0:1], rstd[:, j:j + 1],
                                      ALU.subtract, ALU.mult).then_inc(f_out, 1)

        @block.gpsimd
        def _(pool):
            for s in (em_mul, em_tok, w_y, w_norm, g_hs, g_h2, e_added):
                s.start(pool)
            pool.wait_ge(late_in, 64)
            pool.tensor_tensor(bias_pe, rows5[:, 2, :], c("pe"), ALU.add).then_inc(bias_ready, 1)
            pool.wait_ge(bias_ready, 1)

            def over_j(x):
                return x.unsqueeze(1).broadcast_to([P, BPT, D])

            with pool.Fori(0, NT // 2) as i:
                for b in range(2):
                    t = 2 * i + b
                    pool.wait_ge(em_norm.sem, em_norm.done(t))
                    pool.tensor_tensor(xw[:, b, :, :], xw[:, b, :, :], over_j(rows5[:, 1, :]), ALU.mult)\
                        .then_inc(em_mul.sem, 1)
                    pool.wait_ge(em_mul.sem, em_mul.done(t))
                    pool.tensor_tensor(xw[:, b, :, :], xw[:, b, :, :], over_j(bias_pe), ALU.add)\
                        .then_inc(em_tok.sem, 1)

            def win_copy_y(t, b, k):
                pool.tensor_copy(ys[0:KROWS[k], b, k, :], YT[0:KROWS[k], k, bass.ds(t * TT, TT)]).then_inc(w_y.sem, 1)

            def win_normalise(pair, p):
                pool.wait_ge(w_rs.sem, w_rs.done(pair))
                e = E[:, p % 2, :].rearrange("p (h n) -> p h n", h=NH)
                pool.tensor_tensor(e, e, sm12[:, p % 2, :].unsqueeze(2).broadcast_to([P, NH, WIN]), ALU.mult)\
                    .then_inc(w_norm.sem, 1)

            def win_tile_steps(t, b, more=True):
                win_normalise(4 * t, 0)
                if more:
                    win_copy_y(t + 2, b, 0)
                win_normalise(4 * t + 1, 1)
                if more:
                    win_copy_y(t + 2, b, 1)
                win_normalise(4 * t + 2, 2)
                win_normalise(4 * t + 3, 3)

            pool.wait_ge(ffs[0]["out"].sem, ffs[0]["out"].done(last))
            for b in range(2):
                for k in range(2):
                    win_copy_y(b, b, k)
                if b == 0:
                    pool.memset(vbd, 0.0).then_inc(w_zero, 1)
            with pool.Fori(0, NT // 2 - 1) as i:
                for b in range(2):
                    win_tile_steps(2 * i + b, b)
            win_tile_steps(last - 1, 0, False)
            win_tile_steps(last, 1, False)

            def grp_copy_h(t, b, first=False):
                if not first:
                    pool.wait_ge(g_z.sem, g_z.done(t - 2))
                for k in range(2):
                    pool.tensor_copy(hs[0:KROWS[k], b, k, :], XT[0:KROWS[k], k, bass.ds(t * TT, TT)])\
                        .then_inc(g_hs.sem, 1)

            def grp_keep(t):
                pool.wait_ge(g_norm.sem, g_norm.done(t))
                pool.tensor_copy(H2X[:, bass.ds(t * BPT, BPT), 0:D], zw).then_inc(g_h2.sem, 1)

            pool.wait_ge(ffs[1]["out"].sem, ffs[1]["out"].done(last))
            pool.memset(wb, 0.0).then_inc(wb_zero, 1)
            grp_copy_h(0, 0, first=True)
            grp_copy_h(1, 1, first=True)
            with pool.Fori(0, NT // 2 - 1) as i:
                for b in range(2):
                    grp_copy_h(2 * i + b + 2, b)
                    grp_keep(2 * i + b)
            grp_keep(last - 1)
            grp_keep(last)

            pool.wait_ge(r_done, 1)
            pool.wait_ge(table_filled, 16)
            for t in range(NT):
                for blk in range(BPT * t, BPT * t + BPT):
                    for s in range(2):
                        pool.indirect_dma_start(XS, bass.IndirectOffsetOnAxis(ap=posi[:, s, blk:blk + 1], axis=0),
                                                H2X[:, blk, :], None).then_inc(scat[t % 2], 16)
                if t >= 1:
                    pool.wait_ge(scat[(t - 1) % 2], 32 * BPT * ((t - 1) // 2 + 1))
                    pool.sem_inc(scattered, 1)
            pool.wait_ge(scat[last % 2], 32 * BPT * (last // 2 + 1))
            pool.sem_inc(scattered, 1)
            pool.dma_start(behind_rows, XS.rearrange("(t p) n -> p t n", p=P)[:, :, D:ROW]).then_inc(behind_in, 16)

            pool.wait_ge(s_acc, 16 + 16 * NT)
            pool.wait_ge(dummies_filled, 32)

            def ex_add(j, b):
                pool.wait_ge(e_ys.sem, e_ys.done(j))
                pool.sem_inc(met_pool, 1)
                pool.indirect_dma_start((ACC, ACC1)[b], bass.IndirectOffsetOnAxis(ap=tokidx[:, b:b + 1], axis=0),
                                        ey[:, b, :], None, compute_op=ALU.add).then_inc(e_acc[b], 16)

            def ex_landed(b, i):
                pool.wait_ge(e_acc[b], 16 * (i + 1))
                pool.sem_inc(e_added.sem, 1)

            ex_add(0, 0)
            with pool.Fori(0, (ET - 1) // 2) as i:
                ex_add(2 * i + 1, 1)
                ex_landed(0, i)
                ex_add(2 * i + 2, 0)
                ex_landed(1, i)
            ex_landed(0, ET // 2)


def _constants():
    a = np.zeros((P, CONST), np.float32)
    p = np.arange(P)
    a[:, _C["ident"]] = np.eye(P)
    a[:, _C["before"]] = p[:, None] < p[None, :]
    a[:, _C["ones"]] = 1
    a[:, _C["kmask"]] = p[:, None] // DH == np.arange(HM)[None, :]
    pos = np.arange(WIN, dtype=np.float32)[:, None]
    i = np.arange(D // 2, dtype=np.float32)[None, :]
    angle = pos / np.power(np.float32(10000.0), np.float32(2.0) * i / np.float32(D))
    pe = np.zeros((WIN, D), np.float32)
    pe[:, 0::2], pe[:, 1::2] = np.sin(angle), np.cos(angle)
    a[:, _C["pe"]] = np.concatenate([pe, pe])
    a[:, _C["experts"]] = np.arange(NE)
    a[:, _C["tiles"]] = np.arange(ET)
    a[:, _C["padrow"]][:, D + 2] = -1
    a[:, _C["padrow"]][:, D + 3] = TOK + p
    a[:, _C["token"]] = np.arange(NB)[None, :] * P + p[:, None]
    return a


def _split(v):
    out = np.zeros((P, 2), v.dtype)
    out[:, 0], out[:DT, 1] = v[:DM], v[DM:]
    return out


def _arrays(x, L0_tok_patch_w, L0_tok_patch_b, L0_tok_ln_g, L0_tok_ln_b, L0_tok_qkv_w, L0_tok_qkv_b, L0_tok_proj_w,
            L0_tok_proj_b, L0_tok_ff1_w, L0_tok_ff1_b, L0_tok_ff2_w, L0_tok_ff2_b, L0_attn_W_qkv, L0_attn_b_qkv,
            L0_attn_W_proj, L0_attn_b_proj, L0_attn_W_gp, L0_attn_alpha, L0_ffn_gate_w, L0_ffn_w1, L0_ffn_w2,
            L0_ffn_w3, L0_ffn_sw1, L0_ffn_sw2, L0_ffn_sw3):
    d = {"const": _constants()}
    a = x.reshape(IMAGES, CH, GRID, PATCH, GRID, PATCH).transpose(1, 3, 5, 0, 2, 4)
    d["patches"] = a.reshape(PK, P, NT, TT).transpose(2, 1, 0, 3)
    d["patch_w"] = L0_tok_patch_w.reshape(D, PK, P).transpose(2, 1, 0)
    d["rows5"] = np.concatenate([L0_tok_patch_b, L0_tok_ln_g, L0_tok_ln_b, L0_attn_b_qkv[2 * D:], L0_attn_b_proj])[None]
    d["alpha"] = L0_attn_alpha[None]
    def qk_columns(b):
        q, k = b[0:D], b[D:2 * D]
        return np.stack([q[:DM], k[:DM], np.concatenate([q[DM:], k[DM:]])], axis=1)

    d["bcols"] = np.concatenate(
        [L0_tok_ff1_b.reshape(FC, P).T, _split(L0_tok_ff2_b), qk_columns(L0_tok_qkv_b), _split(L0_tok_qkv_b[2 * D:]),
         _split(L0_tok_proj_b), qk_columns(L0_attn_b_qkv)], axis=1)
    d["ff1_w"], d["ff2_w"] = L0_tok_ff1_w, L0_tok_ff2_w.reshape(FC, P, D).transpose(1, 0, 2)
    d["proj_w"], d["proj2_w"] = L0_tok_proj_w, L0_attn_W_proj
    for name, w in (("qkv_w", L0_tok_qkv_w), ("qkv2_w", L0_attn_W_qkv)):
        q, k, v = w[:, 0:D], w[:, D:2 * D], w[:, 2 * D:]
        d[name] = np.concatenate([q[:, :DM], k[:, :DM], q[:, DM:], k[:, DM:], v], axis=1)
    d["gp_w"], d["gate_w"] = L0_attn_W_gp, L0_ffn_gate_w.T
    def up(w1, w3):
        w1, w3 = np.swapaxes(w1, -1, -2), np.swapaxes(w3, -1, -2)
        return [w1[..., :DM, :], w3[..., :DM, :], np.concatenate([w1[..., DM:, :], w3[..., DM:, :]], axis=-2)]

    def down(w2):
        w2 = np.swapaxes(w2, -1, -2)
        n = w2.shape[-2] // P
        w2 = np.swapaxes(w2.reshape(*w2.shape[:-2], n, P, D), -2, -3)
        return [w2.reshape(*w2.shape[:-2], n * D)]

    d["shared"] = np.concatenate(up(L0_ffn_sw1, L0_ffn_sw3) + down(L0_ffn_sw2), axis=-1)
    d["experts"] = np.concatenate(up(L0_ffn_w1, L0_ffn_w3) + down(L0_ffn_w2), axis=-1)
    return {n: np.ascontiguousarray(v) for n, v in d.items()}


def kernel(**inputs):
    import concourse.bacc as _bacc
    from concourse.bass_utils import run_bass_kernel_spmd as _run

    arrays = {f"in_{n}": a for n, a in _arrays(**{n: np.asarray(a) for n, a in inputs.items()}).items()}
    nc = _bacc.Bacc("TRN2", target_bir_lowering=False, num_devices=1)
    d = {n[3:]: nc.dram_tensor(n, a.shape, mybir.dt.from_np(a.dtype), kind="ExternalInput").ap()
         for n, a in arrays.items()}
    out = nc.dram_tensor("out_dram", (TOK, D), F32, kind="ExternalOutput").ap()
    build(nc, d, out)
    r = _run(nc, [arrays], core_ids=[0])
    return r.results[0]["out_dram"].reshape(IMAGES, WIN, D)
```

```python
from contextlib import ExitStack

import numpy as np

import concourse.bass as bass
from concourse import mybir

F32 = mybir.dt.float32
F32R = mybir.dt.float32r
I32 = mybir.dt.int32
U32 = mybir.dt.uint32
ALU = mybir.AluOpType
ACT = mybir.ActivationFunctionType
AX = mybir.AxisListType.X

P = 128
IMAGES, CH, SIDE, PATCH = 64, 3, 128, 16
GRID = SIDE // PATCH
WIN = GRID * GRID
TOK = IMAGES * WIN
D = 192
DM, DT = P, D - P
PK = CH * PATCH * PATCH // P
TT = 512
NT = TOK // TT
IPT = TT // WIN
BPT = TT // P
NB = TOK // P
FF = 768
FC = FF // P
NH, DH = 12, 16
HM = DM // DH
GP = 49
NE, MI = 16, 512
SI = 1024
SC = SI // P
ROW = D + 4
ET = TOK * 2 // P + NE - 1
EPS = 1e-5
EW = 2 * MI + MI + (MI // P) * D

_C = {}
_at = 0
for _name, _n in (("ident", P), ("before", P), ("ones", P), ("kmask", HM), ("pe", D),
                  ("experts", NE), ("tiles", ET), ("padrow", ROW), ("token", NB)):
    _C[_name] = slice(_at, _at + _n)
    _at += _n
CONST = _at
_B = {}
_at = 0
for _name, _n in (("ff1", FC), ("ff2", 2), ("qk", 3), ("v", 2), ("proj", 2), ("qk2", 3)):
    _B[_name] = slice(_at, _at + _n)
    _at += _n
BCOLS = _at


class Signal:

    def __init__(self, sem, depth, per=1, first=0):
        self.sem, self.depth, self.per, self.first = sem, depth, per, first

    def start(self, engine):
        engine.sem_inc(self.sem, self.depth * self.per)

    def done(self, item, part=None):
        return (item - self.first + self.depth) * self.per + (self.per if part is None else part + 1)

    def recycled(self, item):
        return (item - self.first) * self.per + self.per


class Chain:

    def __init__(self, engine, sem, base):
        self.engine, self.sem, self.base, self.n = engine, sem, base, 0

    def __call__(self, instruction):
        self.n += 1
        instruction.then_inc(self.sem, 1)

    def join(self):
        self.engine.wait_ge(self.sem, self.base + self.n)


NEWTON = 3
RSQRT_STEPS = 3 + 3 * NEWTON


def rsqrt(dve, chain, out, var, tmp):
    chain(dve.tensor_scalar(var, var, EPS, None, ALU.add))
    chain.join()
    chain(dve.tensor_scalar(tmp.bitcast(I32), var.bitcast(I32), 1, None, ALU.logical_shift_right))
    chain.join()
    chain(dve.tensor_scalar(out.bitcast(I32), tmp.bitcast(I32), -1.0, float(0x5F3759DF), ALU.mult, ALU.add))
    chain.join()
    for _ in range(NEWTON):
        chain(dve.tensor_tensor(tmp, out, out, ALU.mult))
        chain.join()
        chain(dve.scalar_tensor_tensor(out=tmp, in0=tmp, scalar=-0.5, in1=var, op0=ALU.mult, op1=ALU.mult))
        chain.join()
        chain(dve.scalar_tensor_tensor(out=out, in0=tmp, scalar=1.5, in1=out, op0=ALU.add, op1=ALU.mult))
        chain.join()


def norm_steps(n):
    return 2 * n + RSQRT_STEPS


def norm_stats(dve, chain, rows, stats, mv, rstd, tmp, met):
    for j, row in enumerate(rows):
        chain(dve.bn_stats(stats[:, j, :], row))
    chain.join()
    dve.sem_inc(met, 1)
    for j in range(len(rows)):
        chain(dve.bn_aggr(mv[:, j, :], stats[:, j, :]))
    chain.join()
    rsqrt(dve, chain, rstd, mv[:, :, 1], tmp)


def build(nc, d, out):
    XS = nc.dram_tensor("sorted_rows", (ET * P, ROW), F32).ap()
    ACC = nc.dram_tensor("acc_rows", (TOK + P, D), F32).ap()
    ACC1 = nc.dram_tensor("acc_rows_odd", (TOK + P, D), F32).ap()

    with ExitStack() as ctx:
        MEM = 53200
        BASE = -(-nc.sbuf_base // 32) * 32
        mem = ctx.enter_context(nc.sbuf_tensor("mem", [P, MEM], F32))[:, :]
        PS = ctx.enter_context(nc.psum_tensor("PS", [P, 8, 512], F32))

        def sem(name):
            return ctx.enter_context(nc.semaphore(name))

        def signal(name, depth, per=1, first=0):
            return Signal(sem(name), depth, per, first)

        class Region:
            def __init__(self, lo, hi):
                self.at, self.hi = lo, hi

            def __call__(self, n, **shape):
                a = mem[:, self.at:self.at + n]
                self.at += n
                assert self.at <= self.hi, (self.at, self.hi)
                if not shape:
                    return a
                keys = list(shape)
                return a.rearrange(f"p ({' '.join(keys)} n) -> p {' '.join(keys)} n", **shape)

            def rounded(self, name, n, **shape):
                self.at = -(-self.at // 8) * 8
                t = nc.alloc_sbuf_tensor_at(name, [P, n], F32R, offset=BASE + 4 * self.at)
                self.at += n
                assert self.at <= self.hi, (self.at, self.hi)
                keys = list(shape)
                return t[:, :].rearrange(f"p ({' '.join(keys)} n) -> p {' '.join(keys)} n", **shape)

        LATE = 4
        FG = 2
        SHW = (NE - LATE) * EW
        H2 = SHW + 8 * SI + SC * D
        SHWORK = H2 + NB * ROW
        CONSTS = MEM - 1400

        early = Region(0, SHW)
        XT = early(2 * TOK, k=2)
        YT = early(2 * TOK, k=2)
        wpatch = early(PK * D, c=PK)
        wff1 = early(2 * FF, k=2)
        wff2 = early(FC * D, c=FC)
        wqkv = early(2 * 3 * D, k=2)
        wproj = early(2 * D, k=2)
        wqkv2 = early(2 * 3 * D, k=2)
        wproj2 = early(2 * D, k=2)
        wgp = early(2 * GP, k=2)
        wgate = early(2 * NE, k=2)
        rows5 = early(5 * D, r=5)
        bias_pe = early(D)
        WORK = early.at
        work = Region(WORK, CONSTS)
        patches = work(2 * PK * TT, b=2, c=PK)
        xw = work(2 * BPT * D, b=2, j=BPT)
        EMBED_END = work.at
        ff_memory = []
        for at in (EMBED_END, 2 * TOK):
            work = Region(at, CONSTS)
            ff_memory.append((work(4 * TT, b=4), work.rounded(f"x_split{at}", 2 * 3 * TT, b=2, s=3),
                              work(TT)))
        ff1s = Region(CONSTS - 4 * FF, CONSTS).rounded("ff1_split", 4 * FF, s=4)
        work = Region(WORK, CONSTS)
        ys = work(2 * 2 * TT, b=2, k=2)
        qT = work(2 * 2 * TT, b=2, k=2)
        kbd = work(2 * IPT * NH * WIN, b=2, i=IPT, h=NH)
        vbd = work(2 * IPT * D, b=2, i=IPT)
        E = work(2 * NH * WIN, b=2)
        ETb = work(2 * NH * WIN, b=2)
        oT = work(2 * TT, k=2)
        assert work.at <= CONSTS - 4 * FF
        hs = Region(WORK, SHW)(2 * 2 * TT, b=2, k=2)
        work = Region(2 * TOK, 4 * TOK)
        q2 = work(2 * TT, k=2)
        k2 = work(2 * TT, k=2)
        v2 = work(2 * BPT * D, b=2, j=BPT)
        sE = work(BPT * WIN, j=BPT)
        lE = work(BPT * GP, j=BPT)
        gT = work(TT)
        t1 = work(BPT * WIN, j=BPT)
        wb = work(BPT * P, j=BPT)
        wT = work(TT)
        oT2 = work(2 * TT, k=2)
        work = Region(SHWORK + 8 + 6 * TT + BPT * D, CONSTS)
        hT2 = work(2 * TT, k=2)
        zw = Region(work.at, CONSTS)(BPT * D, j=BPT)
        LG = Region(work.at + 2 * TT, CONSTS)(NB * NE, b=NB)
        work = Region(2 * TOK, 4 * TOK)
        R = [work(NB * NE, b=NB) for _ in range(8)]
        r1 = [work(NB) for _ in range(8)]
        re = [work(NE) for _ in range(8)]
        tmap = work(ET * NE, j=ET)
        work = Region(SHW, H2)
        shs = work.rounded("shared_split", 8 * SI, s=4, g=2)
        shw2 = work(SC * D, c=SC)
        raw_shared = Region(H2, SHWORK)(4 * SI, s=2)
        H2X = Region(H2, SHWORK)(NB * ROW, b=NB)
        work = Region(SHWORK, CONSTS)
        sx = work.rounded("rows_split", 2 * 3 * TT, b=2, s=3)
        shx = work(BPT * D, j=BPT)
        sil = work(2 * TT, b=2)
        gg = work(2 * TT, b=2)
        zo = work(BPT * D, j=BPT)
        behind_rows = work(4 * ET, t=ET)
        gates, gates2, tokens = work(ET), work(ET), work(ET)
        need_f, need = work(ET), work(ET).bitcast(I32)
        up3 = work(TT)
        work = Region(H2, SHWORK)
        xg = work(2 * ROW, b=2)
        exT = work(2 * 2 * P, b=2, k=2)
        esil = work(2 * MI, b=2)
        eg = work(2 * MI, b=2)
        ey = work(2 * D, b=2)
        egate = work(2)
        ew = Region(SHWORK, CONSTS)(2 * 3 * MI, b=2)
        work = Region(0, SHW)
        fin = work(NT * BPT * D, t=NT, j=BPT)
        fin1 = work(NT * BPT * D, t=NT, j=BPT)
        fout = work(NT * BPT * D, t=NT, j=BPT)
        fb = FG * BPT
        fstats = work(6 * fb, j=fb)
        fmv = [work(2 * fb, j=fb) for _ in range(NT // FG)]
        frstd, fshift = [work(fb) for _ in range(NT // FG)], [work(fb) for _ in range(NT // FG)]
        ftmp = work(fb)
        work = Region(CONSTS, MEM)
        const = work(CONST)
        bcols = work(BCOLS)
        stats = work(24, j=4)
        mv = work(8, j=4)
        rstd, tmp4 = work(4), work(4)
        mix = work(4)
        alpha = work(1)
        mx12, sm12 = work(2 * NH, b=2), work(2 * NH, b=2)
        mxS, smS, mxL, smL = work(4), work(4), work(4), work(4)
        posi = work(2 * NB, s=2).bitcast(I32)
        emap = work(ET).bitcast(I32)
        emapf = work(ET)
        tokidx = work(2).bitcast(I32)
        qbias = work(1)
        kbias = work(HM)

        def c(name):
            return const[:, _C[name]]

        def bc(name, k, rows=P):
            return bcols[0:rows, _B[name]][:, k:k + 1]

        ident, kmask = c("ident"), c("kmask")
        KROWS = (P, DT)


        patch_w_in = sem("patch_weights_loaded")
        early_in, late_in, shared_in, experts_in, lastw_in = (
            sem("early_weights_loaded"), sem("row_constants_loaded"), sem("shared_weights_loaded"),
            sem("expert_weights_loaded"), sem("last_experts_loaded"))
        first_down = sem("sh_first_down_copied")
        sh_split = sem("shared_weights_split")
        table_filled, dummies_filled = sem("sorted_rows_filled"), sem("dummy_rows_filled")
        consts_ready, bias_ready = sem("mix_ready"), sem("position_bias_ready")
        exp_alpha = sem("exp_alpha")

        patch_in = [sem("patches_in0"), sem("patches_in1")]
        em_mm, em_raw, em_norm = signal("embed_products", 2), signal("embed_raw", 2, 2), signal("embed_normed", 2, BPT)
        em_mul, em_tok = signal("embed_scaled", 2), signal("embed_tokens", 2)
        em_tr, em_xt = signal("embed_transposed", 2), signal("embed_xt", 2, 2)
        em_chain = sem("embed_chain")

        ffs = []
        for which, (hidden, split, left) in zip("ab", ff_memory):
            ffs.append({"hid": hidden, "xs": split, "left": left})
            ffs[-1].update({n: signal(f"ff_{which}_{n}", depth, per) for n, depth, per in
                        (("x", 2, 5), ("up", 3, 1), ("gelu", 3, 1), ("down", 4, 1), ("half", 2, 1), ("out", 2, 2))})

        w_y, w_fill = signal("win_y_copied", 2, 2), signal("win_ring_filled", 2)
        w_drain = [signal(f"win_ring_drained{n}", 1) for n in range(2)]
        w_zero = sem("win_values_zeroed")
        w_s, w_mx, w_sub, w_exp = (signal(f"win_{n}", 2) for n in ("scores", "max", "shifted", "exp"))
        w_sum, w_rs, w_norm = (signal(f"win_{n}", 2) for n in ("sum", "reciprocal", "weights"))
        w_tr, w_et, w_pv, w_o = (signal("win_transposed", 2), signal("win_turned", 2, 2),
                                 signal("win_values", 2), signal("win_heads_out", 1, 2))

        g_hs, g_fill, g_drain = signal("grp_h_copied", 2, 2), signal("grp_ring_filled", 2), signal("grp_ring_drained", 2)
        g_a = signal("grp_scores", 1, 2)
        g_mx, g_dif = signal("grp_max", 1, 2), signal("grp_shifted", 1, 2)
        g_exp, g_sum, g_gw = signal("grp_exp", 1, 2), signal("grp_sums", 1, 4), signal("grp_group_probs", 1, 2)
        g_gt, g_gtc, g_grp = signal("grp_probs_turned", 1), signal("grp_probs_copied", 1), signal("grp_group", 1)
        g_t1, g_wb = signal("grp_mix", 1), signal("grp_weights", 1, 2)
        g_wt, g_wtc, g_pv = signal("grp_weights_turned", 1), signal("grp_weights_copied", 1), signal("grp_values", 1)
        g_oc, g_z, g_raw = signal("grp_values_copied", 1, 2), signal("grp_rows", 1), signal("grp_rows_raw", 1, 2)
        g_norm, g_h2 = signal("grp_rows_normed", 1, BPT), signal("grp_rows_kept", 1)
        g_tr, g_ht = signal("grp_rows_turned", 1), signal("grp_rows_turned_copied", 1, 2)
        g_lg, g_lgc = signal("grp_logits", 1), signal("grp_logits_copied", 1)
        g_chain, wb_zero = sem("grp_chain"), sem("grp_weights_zeroed")

        r_chain, r_exp, r_pos, r_mask = sem("route_chain"), sem("route_exp"), sem("route_counts"), sem("route_chosen")
        r_read, r_done = sem("route_counts_read"), sem("route_done")
        scat = [sem("scatter0"), sem("scatter1")]
        scattered = sem("scattered_tiles")

        s_x, s_tr, s_xt = signal("sh_rows", 1), signal("sh_turned", 2), signal("sh_x", 2, 5)
        s_up, s_silu, s_gg, s_dn = signal("sh_up", 2, 2), signal("sh_silu", 2), signal("sh_hidden", 2), signal("sh_down", 2)
        s_z, s_acc = signal("sh_out", 1, 2), sem("acc_rows_stored")

        e_in = [sem("ex_rows0"), sem("ex_rows1")]
        e_tr, e_xt, e_h1, e_h3 = signal("ex_turned", 2), signal("ex_x", 2), signal("ex_h1", 2), signal("ex_h3", 2)
        e_silu, e_g, e_w = signal("ex_silu", 2), signal("ex_hidden", 2), signal("ex_weights", 2)
        e_y, e_ys, e_gate = signal("ex_y", 2), signal("ex_rows_out", 2), signal("ex_gate", 2, 2)
        behind_in, gates_ready = sem("rows_ends_loaded"), sem("gates_ready")
        e_acc = [sem("ex_add_landed0"), sem("ex_add_landed1")]
        e_added = signal("ex_added", 2)

        f_in = [sem(f"fin_in{n}") for n in range(NT)]
        f_chain, f_sum, f_norm, f_st = sem("fin_chain"), sem("fin_summed"), sem("fin_factors"), sem("fin_stored")
        f_out = [sem("fin_rows_even"), sem("fin_rows_odd"), sem("fin_rows_vector")]

        ff1_high, ff1_low = sem("ff1_weights_high"), sem("ff1_weights_low")
        met_act = sem("waits_met_scalar")
        met_dve, met_pe, met_pool = sem("waits_met_vector"), sem("waits_met_tensor"), sem("waits_met_pool")
        EARLY = 16
        N_EMBED = norm_steps(BPT)
        N_GROUP = norm_steps(BPT)
        N_FIN = norm_steps(FG * BPT) + 1
        last = NT - 1

        def plain(x):
            return x.bitcast(F32)

        def kparts(weights, cols):
            return [weights[0:KROWS[k], k, cols] for k in range(2)]

        def halves(k):
            return slice(0, DM) if k == 0 else slice(DM, D)

        WU = 7
        WQ, WK, WQK, WP, WV = 0, 1, 2, 3, 5

        class RingItem:
            def __init__(self, i, off):
                self.n, self.bank, self.drain = 2 * WU * i + off, 6 + off % 2, w_drain[off % 2]
                self.at = WU * i + off // 2

            def free(self):
                return self.drain.sem, self.drain.recycled(self.at)

            def drained(self):
                return self.drain.sem, self.drain.done(self.at)

            def filled(self):
                return w_fill.sem, w_fill.done(self.n)

        def win_item(i, b, u):
            return RingItem(i, WU * b + u)

        def win_item_proj(i, b, u, ending=False):
            return RingItem(i, 2 * WU + (2 * b if ending else WU * b + WP) + u)

        def win_skip(engine, i, b, u):
            item = win_item(i, b, u)
            engine.wait_ge(*item.drained())
            engine.sem_inc(item.drain.sem, 1)

        def win_neighbours(i, b):
            return ((i - 1, 1) if b == 0 else (i, 0)), ((i, 1) if b == 0 else (i + 1, 0))

        GU = 5

        def grp_bank(b, u):
            return (GU * b + u) % 2

        def split_x(engine, s, t, b, first=False):
            if not first:
                engine.wait_ge(s["up"].sem, s["up"].done(FC * (t - 1) - 1))
                engine.sem_inc(met_pool, 1)
            x, n, xs = XT[:, :, bass.ds(t * TT, TT)], s["x"], s["xs"]
            engine.tensor_copy(xs[:, b, 0, :], x[:, 0, :]).then_inc(n.sem, 1)
            engine.tensor_copy(xs[0:DT, b, 2, :], x[0:DT, 1, :]).then_inc(n.sem, 1)
            engine.wait_ge(n.sem, n.done(t, 1))
            if not first:
                engine.sem_inc(met_pool, 1)
            engine.tensor_tensor(s["left"][0:DT, :], x[0:DT, 1, :], plain(xs[0:DT, b, 2, :]), ALU.subtract)\
                .then_inc(n.sem, 1)
            engine.tensor_tensor(xs[:, b, 1, :], x[:, 0, :], plain(xs[:, b, 0, :]), ALU.subtract).then_inc(n.sem, 1)
            engine.wait_ge(n.sem, n.done(t, 3))
            if not first:
                engine.sem_inc(met_pool, 1)
            engine.tensor_copy(xs[DT:P, b, 2, :], s["left"][0:DT, :]).then_inc(n.sem, 1)
            engine.wait_ge(n.sem, n.done(t))
            if not first:
                engine.sem_inc(met_pool, 1)

        FIRST = 0

        def two(bank):
            return PS[:, bank, 0:2 * D].rearrange("p (j n) -> p j n", j=2)

        def sh_low(engine, t, b):
            engine.wait_ge(s_xt.sem, s_xt.done(t, 2))
            engine.tensor_tensor(sx[:, b, 1, :], PS[:, 0, :], plain(sx[:, b, 0, :]), ALU.subtract).then_inc(s_xt.sem, 1)
            engine.tensor_tensor(sx[DT:P, b, 2, :], PS[0:DT, 1, :], plain(sx[DT:P, b, 2, :]), ALU.subtract)\
                .then_inc(s_xt.sem, 1)

        def weights_at(engine, j, met):
            engine.wait_ge(lastw_in, engine.value_load(need[0:1, bass.ds(j, 1)], min_val=16, max_val=16 + 16 * LATE))
            engine.sem_inc(met, 1)
            return engine.value_load(emap[0:1, bass.ds(j, 1)], min_val=0, max_val=NE - 1) * EW

        block = ctx.enter_context(nc.Block())

        @block.sync
        def _(sp):
            sp.sem_inc(lastw_in, 16)
            sp.sem_inc(s_acc, 16)
            sp.dma_start(wpatch, d["patch_w"]).then_inc(patch_w_in, 16)

            def load_patches(t, b):
                sp.dma_start(patches[:, b, :, :], d["patches"][bass.ds(t, 1)]
                             .rearrange("o p c n -> (o p) c n")).then_inc(patch_in[b], 16)

            load_patches(0, 0)
            sp.dma_start(const, d["const"]).then_inc(late_in, 16)
            sp.dma_start(rows5, d["rows5"].partition_broadcast(P)).then_inc(late_in, 16)
            sp.dma_start(alpha, d["alpha"].partition_broadcast(P)).then_inc(late_in, 16)
            sp.dma_start(bcols, d["bcols"]).then_inc(late_in, 16)
            load_patches(1, 1)
            with sp.Fori(1, NT // 2) as i:
                for b in range(2):
                    sp.wait_ge(em_mm.sem, em_mm.recycled(2 * i + b))
                    load_patches(2 * i + b, b)

            sp.wait_ge(late_in, 64)
            sp.dma_start(XS.rearrange("(t p) n -> p t n", p=P),
                         c("padrow").unsqueeze(1).broadcast_to([P, ET, ROW])).then_inc(table_filled, 16)
            sp.dma_start(ACC[TOK:TOK + P, :], c("padrow")[:, 0:D]).then_inc(dummies_filled, 16)
            sp.dma_start(ACC1.rearrange("(t p) n -> p t n", p=P),
                         c("padrow")[:, 0:D].unsqueeze(1).broadcast_to([P, NB + 1, D])).then_inc(dummies_filled, 16)

            for u in range(2):
                sp.wait_ge(*win_item_proj(NT // 2 - 1, 1, u, True).drained())
            sp.dma_start(raw_shared[:, 0, :], d["shared"][:, 0:2 * SI]).then_inc(shared_in, 16)
            for g in range(2):
                for a in (slice(0, DT), slice(DT, P)):
                    sp.dma_start(raw_shared[a, 1, SI * g:SI * g + SI], d["shared"][DT * g:DT * g + DT, 2 * SI:3 * SI])\
                        .then_inc(shared_in, 16)
            sp.dma_start(shw2, d["shared"][:, 3 * SI:]).then_inc(shared_in, 16)
            sp.wait_ge(r_done, 1)
            few = 2
            for t in range(NT):
                for e in range(few * t, min(few * t + few, NE - LATE)):
                    sp.dma_start(mem[:, e * EW:(e + 1) * EW], d["experts"][e]).then_inc(experts_in, 16)
                sp.wait_ge(s_z.sem, s_z.done(t))
                sp.dma_start(ACC[t * TT:t * TT + TT, :].rearrange("(j p) n -> p j n", p=P), zo).then_inc(s_acc, 16)
            assert few * NT >= NE - LATE
            sp.wait_ge(scattered, NT)

            def rows_in(j, b):
                sp.wait_ge(e_tr.sem, e_tr.recycled(j))
                sp.dma_start(xg[:, b, :], XS[bass.ds(j * P, P), :]).then_inc(e_in[b], 16)

            with sp.Fori(0, ET // 2) as i:
                for b in range(2):
                    rows_in(2 * i + b, b)
            rows_in(ET - 1, (ET - 1) % 2)
            sp.wait_ge(e_added.sem, e_added.done(ET - 1))
            sp.wait_ge(lastw_in, 16 + 16 * LATE)
            for t in range(NT):
                for dst, src in ((fin, ACC), (fin1, ACC1)):
                    sp.dma_start(dst[:, t, :, :], src[t * TT:(t + 1) * TT, :]
                                 .rearrange("(j p) n -> p j n", p=P)).then_inc(f_in[t], 16)
            for t in range(NT):
                if t == NT - FG:
                    sp.wait_ge(f_out[2], BPT)
                else:
                    sp.wait_ge(f_out[t % 2], BPT * (t // 2 + 1))
                sp.dma_start(out[t * TT:(t + 1) * TT, :].rearrange("(j p) n -> p j n", p=P),
                             fout[:, t, :, :]).then_inc(f_st, 16)
            sp.wait_ge(f_st, 16 * NT)

        @block.tensor
        def _(pe):
            for s in (em_mm, em_tr, ffs[0]["up"], ffs[0]["down"], ffs[1]["up"], ffs[1]["down"], w_fill, w_s, w_tr, w_pv,
                      g_fill, g_a, g_gt, g_grp, g_wt, g_pv, g_z, g_tr, g_lg, s_tr, s_up, s_dn,
                      e_tr, e_h1, e_h3, e_y):
                s.start(pe)
            pe.wait_ge(patch_w_in, 16)

            def embed_mm(t, b, i):
                pe.wait_ge(patch_in[b], 16 * (i + 1))
                pe.wait_ge(em_raw.sem, em_raw.recycled(t))
                for j in range(BPT):
                    for k in range(PK):
                        mm = pe.matmul(PS[:, 2 * b + j // 2, D * (j % 2):D * (j % 2) + D],
                                       patches[:, b, k, P * j:P * j + P], wpatch[:, k, :],
                                       start=k == 0, stop=k == PK - 1)
                mm.then_inc(em_mm.sem, 1)

            def embed_tr(t, b):
                pe.wait_ge(em_tok.sem, em_tok.done(t))
                pe.wait_ge(em_xt.sem, em_xt.recycled(t))
                for j in range(BPT):
                    pe.transpose(PS[:, 4 + b, P * j:P * j + P], xw[:, b, j, 0:DM], ident)
                    tr = pe.transpose(PS[0:DT, 6 + b, P * j:P * j + P], xw[:, b, j, DM:D], ident)
                tr.then_inc(em_tr.sem, 1)

            embed_mm(0, 0, 0)
            pe.wait_ge(late_in, 64)
            with pe.Fori(0, NT // 2 - 1) as i:
                embed_mm(2 * i + 1, 1, i)
                embed_tr(2 * i, 0)
                embed_mm(2 * i + 2, 0, i + 1)
                embed_tr(2 * i + 1, 1)
            embed_mm(last, 1, NT // 2 - 1)
            embed_tr(last - 1, 0)
            embed_tr(last, 1)

            def feed_forward(s):
                def up(t, b, m):
                    if m == 0:
                        pe.wait_ge(s["x"].sem, s["x"].done(t))
                    pe.wait_ge(s["gelu"].sem, s["gelu"].recycled(FC * t + m))
                    for n, (w, x) in enumerate(((0, 0), (0, 1), (1, 0), (2, 2), (3, 2))):
                        mm = pe.matmul(PS[:, 4 + m % 3, :], ff1s[:, w, P * m:P * m + P], s["xs"][:, b, x, :],
                                       start=n == 0, stop=n == 4)
                    mm.then_inc(s["up"].sem, 1)

                def down(t, b, m):
                    pe.wait_ge(s["gelu"].sem, s["gelu"].done(FC * t + m + 1))
                    if m == 0:
                        pe.wait_ge(s["out"].sem, s["out"].recycled(t))
                    for q in (m, m + 1):
                        pe.matmul(PS[:, 2 * b, :], wff2[:, q, 0:DM], s["hid"][:, (FC * b + q) % 4, :],
                                  start=q == 0, stop=q == FC - 1)
                    for r in range(2):
                        mm = pe.matmul(PS[64 * r:64 * r + 64, 2 * b + 1, :], wff2[:, m + r, DM:D],
                                       s["hid"][:, (FC * b + m + r) % 4, :], start=m == 0, stop=m == FC - 2)
                        mm.then_inc(s["down"].sem, 1)

                def tile(t, b, more):
                    for m in range(2, FC + 2, 2):
                        up(t, b, m - 1)
                        if m < FC:
                            up(t, b, m)
                        elif more:
                            up(t + 1, 1 - b, 0)
                        down(t, b, m - 2)

                up(0, 0, 0)
                with pe.Fori(0, NT // 2 - 1) as i:
                    for b in range(2):
                        tile(2 * i + b, b, True)
                tile(last - 1, 0, True)
                tile(last, 1, False)

            pe.wait_ge(em_raw.sem, em_raw.done(last))
            pe.wait_ge(em_xt.sem, em_xt.done(last))
            pe.wait_ge(ff1_low, 1)
            feed_forward(ffs[0])

            def win_qk(i, b, u):
                t, item = 2 * i + b, win_item(i, b, (WQ, WK, WQK)[u])
                if u == 0:
                    pe.wait_ge(w_y.sem, w_y.done(t))
                pe.wait_ge(*item.free())
                w = kparts(wqkv, slice(P * u, P * u + P))
                for k in range(2):
                    mm = pe.matmul(PS[:, item.bank, :], w[k], ys[0:KROWS[k], b, k, :], start=k == 0, stop=k == 1)
                mm.then_inc(w_fill.sem, 1)

            def win_v(i, b, g):
                item = win_item(i, b, WV + g)
                pe.wait_ge(*item.free())
                w = kparts(wqkv, slice(2 * D, 3 * D))
                for r in range(2):
                    a = P * (2 * g + r)
                    for k in range(2):
                        mm = pe.matmul(PS[:, item.bank, D * r:D * r + D], ys[0:KROWS[k], b, k, a:a + P], w[k],
                                       start=k == 0, stop=k == 1)
                mm.then_inc(w_fill.sem, 1)

            def win_scores(i, b, p):
                pair = 4 * (2 * i + b) + p
                for u in (WQ, WK, WQK):
                    pe.wait_ge(*win_item(i, b, u).drained())
                pe.wait_ge(w_sub.sem, w_sub.done(pair - 1))
                for part in range(2):
                    for r in range(2):
                        img = 2 * p + r
                        q = slice(WIN * img, WIN * img + WIN)
                        o = slice(WIN * r, WIN * r + WIN)
                        rr, h0, h1 = ((slice(0, P), 0, HM), (slice(DT, P), HM, NH))[part]
                        mm = pe.matmul(PS[o, part, 0:(h1 - h0) * WIN].rearrange("p (h n) -> p h n", n=WIN),
                                       qT[rr, b, part, q], kbd[rr, b, img, h0:h1, :], start=True, stop=True)
                mm.then_inc(w_s.sem, 1)

            def win_turn(i, b, p):
                pair = 4 * (2 * i + b) + p
                pe.wait_ge(w_norm.sem, w_norm.done(pair))
                pe.wait_ge(w_et.sem, w_et.done(pair - 1))
                for hp in range(NH // 2):
                    tr = pe.transpose(PS[:, 2 + hp // 4, P * (hp % 4):P * (hp % 4) + P],
                                      E[:, p % 2, P * hp:P * hp + P], ident)
                tr.then_inc(w_tr.sem, 1)

            def win_values(i, b, p):
                pair = 4 * (2 * i + b) + p
                pe.wait_ge(w_et.sem, w_et.done(pair))
                if p == 0:
                    for g in range(2):
                        pe.wait_ge(*win_item(i, b, WV + g).drained())
                    pe.wait_ge(w_o.sem, w_o.done(2 * i + b - 1))
                for r in range(2):
                    img = 2 * p + r
                    for hp in range(NH // 2):
                        o = 32 * (hp % 4)
                        mm = pe.matmul(PS[o:o + 32, 4 + hp // 4, WIN * img:WIN * img + WIN],
                                       vbd[:, b, img, 32 * hp:32 * hp + 32],
                                       ETb[:, p % 2, P * hp + WIN * r:P * hp + WIN * r + WIN],
                                       start=True, stop=True)
                mm.then_inc(w_pv.sem, 1)

            def win_proj(i, b, u, ending=False):
                if u == 0:
                    pe.wait_ge(w_o.sem, w_o.done(2 * i + b))
                item = win_item_proj(i, b, u, ending)
                pe.wait_ge(*item.free())
                w = kparts(wproj, halves(u))
                for k in range(2):
                    mm = pe.matmul(PS[0:KROWS[u], item.bank, :], w[k], oT[0:KROWS[k], k, :], start=k == 0, stop=k == 1)
                mm.then_inc(w_fill.sem, 1)

            def win_skip_fill(i, b):
                pe.wait_ge(*win_item(i, b, WQK).filled())
                pe.sem_inc(w_fill.sem, 2)

            def win_tile(i, b, first=False, more=True):
                before, behind = win_neighbours(i, b)
                win_scores(i, b, 0)
                if not first:
                    win_turn(*before, 3)
                if more:
                    win_qk(*behind, 0)
                if not first:
                    win_values(*before, 3)
                if more:
                    win_qk(*behind, 1)
                win_scores(i, b, 1)
                win_turn(i, b, 0)
                if more:
                    win_qk(*behind, 2)
                if first:
                    win_skip_fill(*behind)
                win_values(i, b, 0)
                win_scores(i, b, 2)
                win_turn(i, b, 1)
                if not first:
                    win_proj(*before, 0, not more)
                win_values(i, b, 1)
                if not first:
                    win_proj(*before, 1, not more)
                win_scores(i, b, 3)
                win_turn(i, b, 2)
                if more:
                    win_v(*behind, 0)
                win_values(i, b, 2)
                if more:
                    win_v(*behind, 1)

            pe.wait_ge(ffs[0]["out"].sem, ffs[0]["out"].done(last))
            pe.wait_ge(ffs[0]["gelu"].sem, ffs[0]["gelu"].done(FC * NT - 1))
            win_qk(0, 0, 0)
            win_qk(0, 0, 1)
            win_qk(0, 0, 2)
            win_skip_fill(0, 0)
            for g in range(2):
                win_v(0, 0, g)
            win_tile(0, 0, first=True)
            win_tile(0, 1)
            with pe.Fori(1, NT // 2 - 1) as i:
                for b in range(2):
                    win_tile(i, b)
            win_tile(NT // 2 - 1, 0)
            win_tile(NT // 2 - 1, 1, more=False)
            win_turn(NT // 2 - 1, 1, 3)
            win_values(NT // 2 - 1, 1, 3)
            for u in range(2):
                win_proj(NT // 2 - 1, 1, u, True)

            for u in range(2):
                pe.wait_ge(*win_item_proj(NT // 2 - 1, 1, u, True).drained())
            pe.wait_ge(w_sub.sem, w_sub.done(4 * last + 3))
            pe.wait_ge(w_o.sem, w_o.done(last))
            feed_forward(ffs[1])

            def grp_qk(t, b):
                pe.wait_ge(g_hs.sem, g_hs.done(t))
                for u in range(3):
                    pe.wait_ge(g_drain.sem, g_drain.recycled(GU * t + u))
                    w = kparts(wqkv2, slice(P * u, P * u + P))
                    for k in range(2):
                        mm = pe.matmul(PS[:, grp_bank(b, u), :], w[k], hs[0:KROWS[k], b, k, :], start=k == 0, stop=k == 1)
                    mm.then_inc(g_fill.sem, 1)

            def grp_v(t, b):
                w = kparts(wqkv2, slice(2 * D, 3 * D))
                for u in (3, 4):
                    pe.wait_ge(g_drain.sem, g_drain.recycled(GU * t + u))
                    for r in range(2):
                        j = 2 * (u - 3) + r
                        for k in range(2):
                            mm = pe.matmul(PS[:, grp_bank(b, u), D * r:D * r + D],
                                           hs[0:KROWS[k], b, k, P * j:P * j + P], w[k], start=k == 0, stop=k == 1)
                    mm.then_inc(g_fill.sem, 1)

            def grp_scores(t):
                pe.wait_ge(g_drain.sem, g_drain.done(GU * t + 2))
                for j in range(BPT):
                    for r in range(2):
                        a = slice(P * j + WIN * r, P * j + WIN * r + WIN)
                        for k in range(2):
                            mm = pe.matmul(PS[WIN * r:WIN * r + WIN, 2, WIN * j:WIN * j + WIN],
                                           q2[0:KROWS[k], k, a], k2[0:KROWS[k], k, a], start=k == 0, stop=k == 1)
                mm.then_inc(g_a.sem, 1)
                for j in range(BPT):
                    for k in range(2):
                        mm = pe.matmul(PS[:, 3, GP * j:GP * j + GP], q2[0:KROWS[k], k, P * j:P * j + P],
                                       wgp[0:KROWS[k], k, :], start=k == 0, stop=k == 1)
                mm.then_inc(g_a.sem, 1)

            def grp_turn_probs(t):
                pe.wait_ge(g_gw.sem, g_gw.done(t))
                pe.sem_inc(met_pe, 1)
                for j in range(BPT):
                    tr = pe.transpose(PS[0:GP, 4, P * j:P * j + P], lE[:, j, :], ident)
                tr.then_inc(g_gt.sem, 1)

            def grp_group(t):
                pe.wait_ge(g_gtc.sem, g_gtc.done(t))
                pe.sem_inc(met_pe, 1)
                for j in range(BPT):
                    for r in range(2):
                        a = slice(P * j + WIN * r, P * j + WIN * r + WIN)
                        mm = pe.matmul(PS[WIN * r:WIN * r + WIN, 5, WIN * j:WIN * j + WIN], gT[0:GP, a], gT[0:GP, a],
                                       start=True, stop=True)
                mm.then_inc(g_grp.sem, 1)

            def grp_turn_rows(t):
                pe.wait_ge(g_norm.sem, g_norm.done(t))
                for j in range(BPT):
                    pe.transpose(PS[:, 2, P * j:P * j + P], zw[:, j, 0:DM], ident)
                    tr = pe.transpose(PS[0:DT, 3, P * j:P * j + P], zw[:, j, DM:D], ident)
                tr.then_inc(g_tr.sem, 1)

            def grp_turn_weights(t):
                pe.wait_ge(g_wb.sem, g_wb.done(t))
                pe.wait_ge(g_ht.sem, g_ht.done(t - 1))
                for j in range(BPT):
                    tr = pe.transpose(PS[:, 3, P * j:P * j + P], wb[:, j, :], ident)
                tr.then_inc(g_wt.sem, 1)

            def grp_logits(t):
                pe.wait_ge(g_ht.sem, g_ht.done(t))
                for j in range(BPT):
                    for k in range(2):
                        mm = pe.matmul(PS[:, 6, NE * j:NE * j + NE], hT2[0:KROWS[k], k, P * j:P * j + P],
                                       wgate[0:KROWS[k], k, :], start=k == 0, stop=k == 1)
                mm.then_inc(g_lg.sem, 1)

            def grp_values(t, b):
                pe.wait_ge(g_wtc.sem, g_wtc.done(t))
                pe.wait_ge(g_drain.sem, g_drain.done(GU * t + 4))
                for k in range(2):
                    for j in range(BPT):
                        mm = pe.matmul(PS[0:KROWS[k], 4 + k, P * j:P * j + P], v2[:, b, j, halves(k)],
                                       wT[:, P * j:P * j + P], start=True, stop=True)
                mm.then_inc(g_pv.sem, 1)

            def grp_rows(t, b):
                pe.wait_ge(g_oc.sem, g_oc.done(t))
                pe.wait_ge(g_lgc.sem, g_lgc.done(t - 1))
                for j in range(BPT):
                    a = slice(P * j, P * j + P)
                    o, lo = PS[:, 6 + j // 2, :], D * (j % 2)
                    for k in range(2):
                        pe.matmul(o[:, lo:lo + D], oT2[0:KROWS[k], k, a], wproj2[0:KROWS[k], k, :],
                                  start=k == 0, stop=k == 1)
                    pe.matmul(o[:, lo:lo + DM], hs[:, b, 0, a], ident, start=False, stop=True, skip_group_check=True)
                    mm = pe.matmul(o[:, lo + DM:lo + D], hs[0:DT, b, 1, a], ident[0:DT, 0:DT], start=False, stop=True,
                                   skip_group_check=True)
                mm.then_inc(g_z.sem, 1)

            def grp_tile(t, b, first=False, final=False):
                grp_scores(t)
                if not final:
                    grp_qk(t + 1, 1 - b)
                grp_turn_probs(t)
                if not final:
                    grp_v(t + 1, 1 - b)
                grp_group(t)
                if not first:
                    grp_turn_rows(t - 1)
                grp_turn_weights(t)
                if not first:
                    grp_logits(t - 1)
                grp_values(t, b)
                grp_rows(t, b)

            pe.wait_ge(ffs[1]["out"].sem, ffs[1]["out"].done(last))
            pe.wait_ge(ffs[1]["gelu"].sem, ffs[1]["gelu"].done(FC * NT - 1))
            grp_qk(0, 0)
            grp_v(0, 0)
            grp_tile(0, 0, first=True)
            with pe.Fori(0, NT // 2 - 1) as i:
                grp_tile(2 * i + 1, 1)
                grp_tile(2 * i + 2, 0)
            grp_tile(last, 1, final=True)
            def sh_turn(t, b):
                pe.wait_ge(s_x.sem, s_x.done(t))
                pe.wait_ge(s_xt.sem, s_xt.done(t - 1))
                for j in range(BPT):
                    pe.transpose(PS[:, 0, P * j:P * j + P], shx[:, j, 0:DM], ident)
                    tr = pe.transpose(PS[0:DT, 1, P * j:P * j + P], shx[:, j, DM:D], ident)
                tr.then_inc(s_tr.sem, 1)

            sh_turn(0, 0)
            grp_turn_rows(last)
            grp_logits(last)

            def route_counts():
                pe.wait_ge(r_mask, 1)
                chosen, earlier = R[7].rearrange("p b n -> p (b n)"), R[5].rearrange("p b n -> p (b n)")
                pe.matmul(PS[:, 0, :], c("before"), chosen, start=True, stop=False)
                pe.matmul(PS[:, 0, :], c("ones"), earlier, start=False, stop=True)
                pe.matmul(PS[:, 1, 0:NE], c("ones"), R[4][:, NB - 1, :], start=True, stop=True).then_inc(r_pos, 1)

            def sh_up(t, b, m):
                n = SC * t + m
                if m == 0:
                    pe.wait_ge(s_xt.sem, s_xt.done(t))
                pe.wait_ge(s_gg.sem, s_gg.recycled(n))
                for g in range(2):
                    for i, (w, x) in enumerate(((0, 0), (0, 1), (1, 0), (2, 2), (3, 2))):
                        mm = pe.matmul(PS[:, 2 + 2 * (m % 2) + g, :], shs[:, w, g, P * m:P * m + P],
                                       sx[:, b, x, :], start=i == 0, stop=i == 4)
                    mm.then_inc(s_up.sem, 1)

            def sh_down(t, m):
                n = SC * t + m
                pe.wait_ge(s_gg.sem, s_gg.done(n))
                if m == 0:
                    pe.wait_ge(s_z.sem, s_z.done(t - 1))
                for j in range(BPT):
                    mm = pe.matmul(PS[:, 6 + j // 2, D * (j % 2):D * (j % 2) + D], gg[:, m % 2, P * j:P * j + P],
                                   shw2[:, m, :], start=m == 0 and j % 2 == 0, stop=m == SC - 1,
                                   skip_group_check=True)
                mm.then_inc(s_dn.sem, 1)

            def sh_tile(t, b, more):
                sh_up(t, b, 0)
                for m in range(1, SC):
                    sh_up(t, b, m)
                    sh_down(t, m - 1)
                    if t is FIRST and m == SC // 2:
                        route_counts()
                    if t is FIRST and m == SC - 1:
                        pe.wait_ge(r_read, 1)
                    if more and m == (SC - 1 if t is FIRST else SC // 2):
                        sh_turn(t + 1, 1 - b)
                sh_down(t, SC - 1)

            pe.wait_ge(shared_in, 96)
            pe.wait_ge(sh_split, 8)
            pe.wait_ge(g_lgc.sem, g_lgc.done(last))
            sh_tile(FIRST, 0, True)
            with pe.Fori(0, NT // 2 - 1) as i:
                sh_tile(2 * i + 1, 1, True)
                sh_tile(2 * i + 2, 0, True)
            sh_tile(last, 1, False)

            def ex_turn(j, b, i):
                pe.wait_ge(e_in[b], 16 * (i + 1))
                pe.wait_ge(e_xt.sem, e_xt.recycled(j))
                pe.transpose(PS[:, 4 + b, 0:P], xg[:, b, 0:DM], ident)
                pe.transpose(PS[0:DT, 4 + b, P:2 * P], xg[:, b, DM:D], ident).then_inc(e_tr.sem, 1)

            def ex_up(j, b, g):
                if g == 0:
                    pe.wait_ge(e_xt.sem, e_xt.done(j))
                    pe.wait_ge(e_w.sem, e_w.done(j))
                    pe.wait_ge(e_silu.sem, e_silu.recycled(j))
                else:
                    pe.wait_ge(e_g.sem, e_g.recycled(j))
                tail = slice(DT * g, DT * g + DT)
                for q in range(MI // P):
                    o, a = PS[:, 2 * g + b, P * q:P * q + P], slice(P * q, P * q + P)
                    pe.matmul(o, ew[:, b, MI * g:MI * g + MI][:, a], exT[:, b, 0, :], start=True, stop=False)
                    mm = pe.matmul(o, ew[tail, b, 2 * MI:3 * MI][:, a], exT[tail, b, 1, :], start=False, stop=True)
                mm.then_inc((e_h1, e_h3)[g].sem, 1)

            def ex_down(j, b):
                w = weights_at(pe, j, met_pe)
                pe.wait_ge(e_g.sem, e_g.done(j))
                pe.wait_ge(e_ys.sem, e_ys.recycled(j))
                for q in range(MI // P):
                    mm = pe.matmul(PS[:, 6 + b, 0:D], eg[:, b, P * q:P * q + P],
                                   mem[:, bass.ds(w + 3 * MI + D * q, D)], start=q == 0, stop=q == MI // P - 1)
                mm.then_inc(e_y.sem, 1)

            def ex_step(j, b, i_next, first=False, final=False):
                ex_up(j, b, 0)
                if not final:
                    ex_turn(j + 1, 1 - b, i_next)
                ex_up(j, b, 1)
                if not first:
                    ex_down(j - 1, 1 - b)

            pe.wait_ge(experts_in, 16 * (NE - LATE))
            pe.wait_ge(s_z.sem, s_z.done(last))
            pe.wait_ge(s_gg.sem, s_gg.done(SC * NT - 1))
            ex_turn(0, 0, 0)
            ex_step(0, 0, 0, first=True)
            with pe.Fori(0, (ET - 3) // 2) as i:
                ex_step(2 * i + 1, 1, i + 1)
                ex_step(2 * i + 2, 0, i + 1)
            ex_step(ET - 2, 1, (ET - 1) // 2)
            ex_step(ET - 1, 0, 0, final=True)
            ex_down(ET - 1, 0)

        @block.scalar
        def _(act):
            act.wait_ge(patch_in[0], 16)
            for dst, name in ((wff1, "ff1_w"), (wff2, "ff2_w"), (wqkv, "qkv_w"), (wproj, "proj_w"),
                              (wqkv2, "qkv2_w"), (wproj2, "proj2_w"), (wgp, "gp_w"), (wgate, "gate_w")):
                if name == "ff2_w":
                    act.dma_start(dst, d[name]).then_inc(early_in, 16)
                    continue
                src = d[name]
                if name in ("ff1_w", "qkv_w", "qkv2_w"):
                    act.dma_start(dst[:, 0, :], src[0:DM, :]).then_inc(early_in, 16)
                    act.dma_start(dst[0:DT, 1, :], src[DM:D, :]).then_inc(early_in, 16)
                    if name == "ff1_w":
                        act.dma_start(dst[DT:P, 1, :], src[DM:D, :]).then_inc(early_in, 16)
                else:
                    act.dma_start(dst[:, 0, :], src[0:DM, :]).then_inc(early_in, 16)
                    act.dma_start(dst[0:DT, 1, :], src[DM:D, :]).then_inc(early_in, 16)
            act.wait_ge(late_in, 64)
            act.activation(mix[:, 0:1], alpha, ACT.Exp, scale=-1.0).then_inc(exp_alpha, 1)
            act.wait_ge(early_in, 16 * EARLY)
            act.copy(ff1s[:, 0:4:2, :], wff1).then_inc(ff1_high, 1)
            for s in (em_xt, ffs[0]["gelu"], ffs[1]["gelu"], w_exp, w_et, w_o, g_exp, g_gtc, g_wtc, g_oc, g_ht,
                      s_x, s_xt, s_silu, e_xt, e_silu, e_w):
                s.start(act)

            with act.Fori(0, NT // 2) as i:
                for b in range(2):
                    t = 2 * i + b
                    act.wait_ge(em_tr.sem, em_tr.done(t))
                    for k in range(2):
                        act.copy(XT[0:KROWS[k], k, bass.ds(t * TT, TT)], PS[0:KROWS[k], 4 + 2 * k + b, :])\
                            .then_inc(em_xt.sem, 1)

            def gelus(s):
                with act.Fori(0, NT // 2) as i:
                    for q in range(2 * FC):
                        m, n = q % FC, 2 * FC * i + q
                        act.wait_ge(s["up"].sem, s["up"].done(n))
                        act.wait_ge(s["down"].sem, s["down"].recycled(n))
                        act.activation(s["hid"][:, q % 4, :], PS[:, 4 + m % 3, :], ACT.Gelu_apprx_tanh,
                                       bias=bcols[:, _B["ff1"]][:, m:m + 1]).then_inc(s["gelu"].sem, 1)

            gelus(ffs[0])

            def win_exp(pair, p):
                act.wait_ge(w_sub.sem, w_sub.done(pair))
                act.activation(E[:, p % 2, :], E[:, p % 2, :], ACT.Exp).then_inc(w_exp.sem, 1)

            def win_turned(pair, p):
                act.wait_ge(w_tr.sem, w_tr.done(pair))
                act.wait_ge(w_pv.sem, w_pv.recycled(pair))
                act.copy(ETb[:, p % 2, 0:512], PS[:, 2, :]).then_inc(w_et.sem, 1)
                act.copy(ETb[:, p % 2, 512:], PS[:, 3, 0:NH * WIN - 512]).then_inc(w_et.sem, 1)

            def win_heads(i, b):
                t = 2 * i + b
                act.wait_ge(w_pv.sem, w_pv.done(4 * t + 3))
                for k in range(2):
                    act.activation(oT[0:KROWS[k], k, :], PS[0:KROWS[k], 4 + k, :], ACT.Identity,
                                   bias=bc("v", k, KROWS[k])).then_inc(w_o.sem, 1)

            def win_q_main(i, b):
                item = win_item(i, b, WQ)
                act.wait_ge(*item.filled())
                act.activation(qT[:, b, 0, :], PS[:, item.bank, :], ACT.Identity, bias=qbias[:, 0:1],
                               scale=float(DH) ** -0.5).then_inc(item.drain.sem, 1)

            def win_k_main(i, b, heads):
                item = win_item(i, b, WK)
                act.wait_ge(*item.filled())
                for h in heads:
                    ins = act.activation(kbd[:, b, :, h, :], PS[:, item.bank, :].rearrange("p (i n) -> p i n", i=IPT),
                                         ACT.Identity, bias=kbias[:, h:h + 1], scale=kmask[:, h:h + 1])
                if heads[-1] == HM - 1:
                    ins.then_inc(item.drain.sem, 1)

            def win_tile_act(i, b, first=False, more=True):
                t = 2 * i + b
                before, behind = win_neighbours(i, b)
                if not first:
                    win_turned(4 * t - 1, 3)
                win_exp(4 * t, 0)
                if more:
                    win_q_main(*behind)
                if not first:
                    win_heads(*before)
                if more:
                    win_k_main(*behind, range(0, HM // 2))
                win_turned(4 * t, 0)
                win_exp(4 * t + 1, 1)
                if more:
                    win_k_main(*behind, range(HM // 2, HM))
                if first:
                    win_skip(act, *behind, WK)
                win_turned(4 * t + 1, 1)
                win_exp(4 * t + 2, 2)
                win_turned(4 * t + 2, 2)
                win_exp(4 * t + 3, 3)

            act.wait_ge(consts_ready, 5)
            act.wait_ge(ffs[0]["down"].sem, ffs[0]["down"].done(FC * NT - 1))
            win_q_main(0, 0)
            win_k_main(0, 0, range(HM))
            win_skip(act, 0, 0, WK)
            win_tile_act(0, 0, first=True)
            win_tile_act(0, 1)
            with act.Fori(1, NT // 2 - 1) as i:
                for b in range(2):
                    win_tile_act(i, b)
            win_tile_act(NT // 2 - 1, 0)
            win_tile_act(NT // 2 - 1, 1, more=False)
            win_turned(4 * last + 3, 3)
            win_heads(NT // 2 - 1, 1)
            for u in range(2):
                act.wait_ge(*win_item_proj(NT // 2 - 1, 1, u, True).drained())
            gelus(ffs[1])

            SCALE = float(D) ** -0.5

            def grp_exps(t):
                act.wait_ge(g_dif.sem, g_dif.done(t, 0))
                act.activation(sE, sE, ACT.Exp, scale=SCALE).then_inc(g_exp.sem, 1)
                act.wait_ge(g_dif.sem, g_dif.done(t, 1))
                act.activation(lE, lE, ACT.Exp).then_inc(g_exp.sem, 1)

            def grp_copies(t, k0, signal_in, signal_out, dst):
                act.wait_ge(signal_in.sem, signal_in.done(t))
                for k in range(2):
                    act.copy(dst[0:KROWS[k], k, :], PS[0:KROWS[k], k0 + k, :]).then_inc(signal_out.sem, 1)

            def grp_tile_act(t, first=False):
                grp_exps(t)
                act.wait_ge(g_gt.sem, g_gt.done(t))
                act.copy(gT[0:GP, :], PS[0:GP, 4, :]).then_inc(g_gtc.sem, 1)
                if not first:
                    grp_copies(t - 1, 2, g_tr, g_ht, hT2)
                act.wait_ge(g_wt.sem, g_wt.done(t))
                act.copy(wT, PS[:, 3, :]).then_inc(g_wtc.sem, 1)
                grp_copies(t, 4, g_pv, g_oc, oT2)

            grp_tile_act(0, first=True)
            with act.Fori(1, NT) as t:
                grp_tile_act(t)
            def sh_rows(t):
                act.wait_ge(s_tr.sem, s_tr.done(t - 1))
                act.copy(shx, H2X[:, bass.ds(t * BPT, BPT), 0:D]).then_inc(s_x.sem, 1)

            def sh_turned(t, b):
                act.wait_ge(s_tr.sem, s_tr.done(t))
                act.copy(sx[:, b, 0, :], PS[:, 0, :]).then_inc(s_xt.sem, 1)
                for a in (slice(0, DT), slice(DT, P)):
                    act.copy(sx[a, b, 2, :], PS[0:DT, 1, :]).then_inc(s_xt.sem, 1)

            act.wait_ge(g_h2.sem, g_h2.done(0))
            sh_rows(0)
            sh_turned(0, 0)
            grp_copies(last, 2, g_tr, g_ht, hT2)

            act.wait_ge(r_chain, 2)
            act.activation(R[1], R[0], ACT.Exp).then_inc(r_exp, 1)

            def sh_tile_act(t, b, more):
                for m in range(SC):
                    n = SC * t + m
                    act.wait_ge(s_up.sem, s_up.done(n, 0))
                    if t is FIRST:
                        act.wait_ge(s_up.sem, s_up.done(n))
                        act.wait_ge(s_gg.sem, s_gg.done(n - 1))
                        act.copy(up3, PS[:, 3 + 2 * (m % 2), :])
                    act.wait_ge(s_gg.sem, s_gg.recycled(n))
                    act.activation(sil[:, m % 2, :], PS[:, 2 + 2 * (m % 2), :], ACT.Silu).then_inc(s_silu.sem, 1)
                    if m == SC // 2 - 1 and more:
                        sh_rows(t + 1)
                    if more and m == (SC - 1 if t is FIRST else SC // 2):
                        sh_turned(t + 1, 1 - b)
                if t is FIRST:
                    act.wait_ge(s_dn.sem, s_dn.done(SC - 1))
                    act.copy(zo[:, 0:2, :], two(6))
                    act.copy(zo[:, 2:4, :], two(7)).then_inc(first_down, 1)

            act.wait_ge(g_h2.sem, g_h2.done(last))
            sh_tile_act(FIRST, 0, True)
            with act.Fori(0, NT // 2 - 1) as i:
                sh_tile_act(2 * i + 1, 1, True)
                sh_tile_act(2 * i + 2, 0, True)
            sh_tile_act(last, 1, False)

            def ex_weights(j, b):
                w = weights_at(act, j, met_act)
                act.wait_ge(e_h3.sem, e_h3.recycled(j))
                act.copy(ew[:, b, :], mem[:, bass.ds(w, 3 * MI)]).then_inc(e_w.sem, 1)

            def ex_turned(j, b):
                act.wait_ge(e_tr.sem, e_tr.done(j))
                act.wait_ge(e_h3.sem, e_h3.recycled(j))
                act.copy(exT[:, b, 0, :], PS[:, 4 + b, 0:P])
                act.copy(exT[0:64, b, 1, :], PS[0:DT, 4 + b, P:2 * P])
                act.copy(exT[64:128, b, 1, :], PS[0:DT, 4 + b, P:2 * P]).then_inc(e_xt.sem, 1)

            def ex_silu(j, b):
                act.wait_ge(e_h1.sem, e_h1.done(j))
                act.wait_ge(e_g.sem, e_g.recycled(j))
                act.activation(esil[:, b, :], PS[:, b, :], ACT.Silu).then_inc(e_silu.sem, 1)

            def ex_step_act(j, b, final=False):
                if not final:
                    ex_weights(j + 1, 1 - b)
                ex_silu(j, b)
                if not final:
                    ex_turned(j + 1, 1 - b)

            act.wait_ge(s_z.sem, s_z.done(last))
            act.wait_ge(e_in[0], 16)
            act.wait_ge(e_in[1], 16)
            for e in range(NE - LATE, NE):
                act.dma_start(mem[:, e * EW:(e + 1) * EW], d["experts"][e]).then_inc(lastw_in, 16)
            act.wait_ge(scattered, NT)
            act.wait_ge(experts_in, 16 * (NE - LATE))
            ex_weights(0, 0)
            ex_turned(0, 0)
            with act.Fori(0, (ET - 1) // 2) as i:
                ex_step_act(2 * i, 0)
                ex_step_act(2 * i + 1, 1)
            ex_step_act(ET - 1, 0, final=True)

            for t in range(NT):
                if t % FG == 0:
                    act.wait_ge(f_norm, t // FG + 1)
                if t == NT - FG:
                    continue
                for j in range(BPT):
                    n = BPT * (t % FG) + j
                    act.activation(fout[:, t, j, :], fin[:, t, j, :], ACT.Identity,
                                   bias=fshift[t // FG][:, n:n + 1], scale=frstd[t // FG][:, n:n + 1])\
                        .then_inc(f_out[t % 2], 1)

        @block.vector
        def _(dve):
            for s in (em_raw, em_norm, ffs[0]["out"], ffs[1]["out"], ffs[0]["half"], ffs[1]["half"], *w_drain, w_mx, w_sub, w_sum, w_rs, g_drain, g_mx,
                      g_dif, g_sum, g_gw, g_t1, g_wb, g_raw, g_norm, g_lgc, s_gg, s_z, e_g, e_ys, e_gate):
                s.start(dve)
            dve.wait_ge(late_in, 64)

            def rows(r, n):
                return rows5[:, r, :].unsqueeze(1).broadcast_to([P, n, D])

            dve.wait_ge(exp_alpha, 1)
            dve.tensor_scalar(mix[:, 1:2], mix[:, 0:1], 1.0, None, ALU.add).then_inc(consts_ready, 1)
            dve.wait_ge(consts_ready, 1)
            dve.reciprocal(mix[:, 2:3], mix[:, 1:2]).then_inc(consts_ready, 1)
            dve.wait_ge(consts_ready, 2)
            dve.tensor_scalar(mix[:, 3:4], mix[:, 2:3], -1.0, 1.0, ALU.mult, ALU.add).then_inc(consts_ready, 1)
            qk = bcols[:, _B["qk"]]
            dve.tensor_scalar(qbias, qk[:, 0:1], float(DH) ** -0.5, None, ALU.mult).then_inc(consts_ready, 1)
            dve.tensor_tensor(kbias, kmask, qk[:, 1:2].broadcast_to([P, HM]), ALU.mult).then_inc(consts_ready, 1)

            with dve.Fori(0, NT // 2) as i:
                for b in range(2):
                    t = 2 * i + b
                    dve.wait_ge(em_mm.sem, em_mm.done(t))
                    dve.wait_ge(em_tr.sem, em_tr.recycled(t))
                    for g in range(2):
                        dve.tensor_tensor(xw[:, b, 2 * g:2 * g + 2, :], two(2 * b + g), rows(0, 2), ALU.add)\
                            .then_inc(em_raw.sem, 1)
                    dve.wait_ge(em_raw.sem, em_raw.done(t))
                    chain = Chain(dve, em_chain, N_EMBED * t)
                    norm_stats(dve, chain, [xw[:, b, j, :] for j in range(BPT)], stats, mv, rstd, tmp4, met_dve)
                    assert chain.n == N_EMBED
                    for j in range(BPT):
                        dve.tensor_scalar(xw[:, b, j, :], xw[:, b, j, :], mv[:, j, 0:1], rstd[:, j:j + 1],
                                          ALU.subtract, ALU.mult).then_inc(em_norm.sem, 1)
            dve.wait_ge(em_xt.sem, em_xt.done(0))
            split_x(dve, ffs[0], 0, 0, first=True)
            dve.wait_ge(ff1_high, 1)
            dve.tensor_tensor(ff1s[:, 1:4:2, :], wff1, plain(ff1s[:, 0:4:2, :]), ALU.subtract).then_inc(ff1_low, 1)

            def ff_banks(s, residual):
                with dve.Fori(0, NT // 2) as i:
                    for b in range(2):
                        t = 2 * i + b
                        dve.wait_ge(s["down"].sem, s["down"].done(FC * t + FC - 1))
                        lo, n = slice(0, DT), s["half"]
                        dst = XT if residual else YT
                        main, tail = dst[:, 0, bass.ds(t * TT, TT)], dst[lo, 1, bass.ds(t * TT, TT)]
                        if residual:
                            dve.scalar_tensor_tensor(out=tail, in0=PS[lo, 2 * b + 1, :], scalar=bc("ff2", 1, DT),
                                                     in1=tail, op0=ALU.add, op1=ALU.add).then_inc(n.sem, 1)
                            dve.scalar_tensor_tensor(out=main, in0=PS[:, 2 * b, :], scalar=bc("ff2", 0), in1=main,
                                                     op0=ALU.add, op1=ALU.add).then_inc(s["out"].sem, 1)
                        else:
                            dve.tensor_scalar(tail, PS[lo, 2 * b + 1, :], bc("ff2", 1, DT), None, ALU.add)\
                                .then_inc(n.sem, 1)
                            dve.tensor_scalar(main, PS[:, 2 * b, :], bc("ff2", 0), None, ALU.add)\
                                .then_inc(s["out"].sem, 1)
                        dve.wait_ge(n.sem, n.done(t))
                        dve.tensor_tensor(tail, PS[DT:P, 2 * b + 1, :], tail, ALU.add).then_inc(s["out"].sem, 1)

            ff_banks(ffs[0], False)

            def win_tails(i, b, ops):
                item, qk = win_item(i, b, WQK), bcols[:, _B["qk"]]
                dve.wait_ge(*item.filled())
                for op in ops:
                    if op == 0:
                        ins = dve.tensor_scalar(qT[DT:P, b, 1, :], PS[0:DT, item.bank, :], qk[0:DT, 2:3],
                                                float(DH) ** -0.5, ALU.add, ALU.mult)
                    else:
                        mine = DT // DH + op - 1
                        ins = dve.tensor_scalar(kbd[DT:P, b, :, HM + op - 1, :],
                                                PS[DT:P, item.bank, :].rearrange("p (i n) -> p i n", i=IPT),
                                                qk[DT:P, 2:3], kmask[DT:P, mine:mine + 1], ALU.add, ALU.mult)
                if ops[-1] == NH - HM:
                    ins.then_inc(item.drain.sem, 1)

            def win_v(i, b, g):
                item = win_item(i, b, WV + g)
                dve.wait_ge(*item.filled())
                for image in range(2):
                    for odd in range(2):
                        src = two(item.bank)[WIN * image:WIN * image + WIN]
                        dst = vbd[WIN * odd:WIN * odd + WIN, b, 4 * g + image:4 * g + 4:2, :]
                        src, dst = (x.rearrange("p j (g h n) -> p j g h n", h=2, n=DH)[:, :, :, odd, :] for x in (src, dst))
                        ins = dve.tensor_copy(dst, src)
                ins.then_inc(item.drain.sem, 1)

            def heads(x):
                return x.rearrange("p (h n) -> p h n", h=NH)

            def win_shift(pair, p):
                s = heads(PS[:, 0:2, :].rearrange("p b n -> p (b n)")[:, 0:NH * WIN])
                dve.wait_ge(w_s.sem, w_s.done(pair))
                dve.tensor_reduce(mx12[:, p % 2, :], s, AX, ALU.max).then_inc(w_mx.sem, 1)
                dve.wait_ge(w_mx.sem, w_mx.done(pair))
                dve.wait_ge(w_tr.sem, w_tr.recycled(pair))
                dve.tensor_tensor(heads(E[:, p % 2, :]), s,
                                  mx12[:, p % 2, :].unsqueeze(2).broadcast_to([P, NH, WIN]), ALU.subtract)\
                    .then_inc(w_sub.sem, 1)

            def win_sum(pair, p):
                dve.wait_ge(w_exp.sem, w_exp.done(pair))
                dve.tensor_reduce(sm12[:, p % 2, :], heads(E[:, p % 2, :]), AX, ALU.add).then_inc(w_sum.sem, 1)
                dve.wait_ge(w_sum.sem, w_sum.done(pair))
                dve.reciprocal(sm12[:, p % 2, :], sm12[:, p % 2, :]).then_inc(w_rs.sem, 1)

            def win_drain_proj(i, b, k, ending=False):
                rr, item = slice(0, KROWS[k]), win_item_proj(i, b, k, ending)
                dve.wait_ge(*item.filled())
                x = XT[rr, k, bass.ds((2 * i + b) * TT, TT)]
                dve.scalar_tensor_tensor(out=x, in0=PS[rr, item.bank, :], scalar=bc("proj", k, KROWS[k]), in1=x,
                                         op0=ALU.add, op1=ALU.add).then_inc(item.drain.sem, 1)

            def win_tile_dve(i, b, first=False, more=True):
                t = 2 * i + b
                before, behind = win_neighbours(i, b)
                win_shift(4 * t, 0)
                win_sum(4 * t, 0)
                win_shift(4 * t + 1, 1)
                win_sum(4 * t + 1, 1)
                if more:
                    win_tails(*behind, range(0, 3))
                win_shift(4 * t + 2, 2)
                if more:
                    win_tails(*behind, range(3, NH - HM + 1))
                if first:
                    win_skip(dve, *behind, WQK)
                win_sum(4 * t + 2, 2)
                if not first:
                    win_drain_proj(*before, 0, not more)
                win_shift(4 * t + 3, 3)
                if not first:
                    win_drain_proj(*before, 1, not more)
                win_sum(4 * t + 3, 3)
                if more:
                    win_v(*behind, 0)
                    win_v(*behind, 1)

            dve.wait_ge(ffs[0]["down"].sem, ffs[0]["down"].done(FC * NT - 1))
            dve.wait_ge(w_zero, 1)
            win_tails(0, 0, range(NH - HM + 1))
            win_skip(dve, 0, 0, WQK)
            win_v(0, 0, 0)
            win_v(0, 0, 1)
            win_tile_dve(0, 0, first=True)
            win_tile_dve(0, 1)
            with dve.Fori(1, NT // 2 - 1) as i:
                for b in range(2):
                    win_tile_dve(i, b)
            win_tile_dve(NT // 2 - 1, 0)
            win_tile_dve(NT // 2 - 1, 1, more=False)
            dve.wait_ge(w_y.sem, w_y.done(last))
            for k in range(2):
                dve.wait_ge(*win_item_proj(0, 0, k).drained())
            split_x(dve, ffs[1], 0, 0, first=True)
            for k in range(2):
                win_drain_proj(NT // 2 - 1, 1, k, True)
            dve.wait_ge(shared_in, 96)
            for part in range(2):
                for g in range(2):
                    dve.tensor_copy(shs[:, 2 * part, g, :], raw_shared[:, part, SI * g:SI * g + SI]).then_inc(sh_split, 1)
            for part in range(2):
                for g in range(2):
                    dve.wait_ge(sh_split, 2 * part + g + 1)
                    dve.scalar_tensor_tensor(out=shs[:, 2 * part + 1, g, :], in0=raw_shared[:, part, SI * g:SI * g + SI],
                                             scalar=1.0, in1=plain(shs[:, 2 * part, g, :]), op0=ALU.mult,
                                             op1=ALU.subtract).then_inc(sh_split, 1)
            ff_banks(ffs[1], True)

            def grp_shift(t):
                sS = PS[:, 2, 0:BPT * WIN].rearrange("p (j n) -> p j n", j=BPT)
                sL = PS[:, 3, 0:BPT * GP].rearrange("p (j n) -> p j n", j=BPT)
                for part, (s, m, dst, n) in enumerate(((sS, mxS, sE, WIN), (sL, mxL, lE, GP))):
                    dve.wait_ge(g_a.sem, g_a.done(t, part))
                    dve.tensor_reduce(m, s, AX, ALU.max).then_inc(g_mx.sem, 1)
                    dve.wait_ge(g_mx.sem, g_mx.done(t, part))
                    dve.tensor_tensor(dst, s, m.unsqueeze(2).broadcast_to([P, BPT, n]), ALU.subtract)\
                        .then_inc(g_dif.sem, 1)

            def grp_probs(t):
                dve.wait_ge(g_exp.sem, g_exp.done(t, 0))
                dve.tensor_reduce(smS, sE, AX, ALU.add).then_inc(g_sum.sem, 1)
                dve.wait_ge(g_exp.sem, g_exp.done(t, 1))
                dve.tensor_reduce(smL, lE, AX, ALU.add).then_inc(g_sum.sem, 1)
                dve.wait_ge(g_sum.sem, g_sum.done(t, 1))
                dve.reciprocal(smL, smL).then_inc(g_sum.sem, 1)
                dve.reciprocal(smS, smS).then_inc(g_sum.sem, 1)
                dve.wait_ge(g_sum.sem, g_sum.done(t))
                dve.tensor_tensor(lE, lE, smL.unsqueeze(2).broadcast_to([P, BPT, GP]), ALU.mult).then_inc(g_gw.sem, 1)
                dve.tensor_tensor(sE, sE, smS.unsqueeze(2).broadcast_to([P, BPT, WIN]), ALU.mult).then_inc(g_gw.sem, 1)

            def grp_drain(t, b, us):
                qk, lo = bcols[:, _B["qk2"]], slice(0, DT)
                for u in us:
                    bank = grp_bank(b, u)
                    dve.wait_ge(g_fill.sem, g_fill.done(GU * t + u))
                    if u < 2:
                        ins = dve.tensor_scalar((q2, k2)[u][:, 0, :], PS[:, bank, :], qk[:, u:u + 1], None, ALU.add)
                    elif u == 2:
                        dve.tensor_scalar(q2[lo, 1, :], PS[lo, bank, :], qk[lo, 2:3], None, ALU.add)
                        ins = dve.tensor_scalar(k2[lo, 1, :], PS[DT:P, bank, :], qk[DT:P, 2:3], None, ALU.add)
                    else:
                        ins = dve.tensor_tensor(v2[:, b, 2 * (u - 3):2 * (u - 3) + 2, :], two(bank), rows(3, 2), ALU.add)
                    ins.then_inc(g_drain.sem, 1)

            def grp_weights(t):
                dve.wait_ge(g_grp.sem, g_grp.done(t))
                dve.tensor_scalar(t1, PS[:, 5, 0:BPT * WIN].rearrange("p (j n) -> p j n", j=BPT), mix[:, 3:4],
                                  mix[:, 2:3], ALU.mult, ALU.add).then_inc(g_t1.sem, 1)
                dve.wait_ge(g_t1.sem, g_t1.done(t))
                dve.wait_ge(g_gw.sem, g_gw.done(t))
                for r in range(2):
                    a = slice(WIN * r, WIN * r + WIN)
                    dve.tensor_tensor(wb[a, :, a], t1[a], sE[a], ALU.mult).then_inc(g_wb.sem, 1)

            def grp_keep_logits(t):
                dve.wait_ge(g_lg.sem, g_lg.done(t))
                dve.tensor_copy(LG[:, bass.ds(t * BPT, BPT), :],
                                PS[:, 6, 0:BPT * NE].rearrange("p (j n) -> p j n", j=BPT)).then_inc(g_lgc.sem, 1)

            def grp_norm(t):
                dve.wait_ge(g_z.sem, g_z.done(t))
                dve.wait_ge(g_h2.sem, g_h2.done(t - 1))
                for g in range(2):
                    dve.tensor_tensor(zw[:, 2 * g:2 * g + 2, :], two(6 + g), rows(4, 2), ALU.add).then_inc(g_raw.sem, 1)
                dve.wait_ge(g_raw.sem, g_raw.done(t))
                chain = Chain(dve, g_chain, N_GROUP * t)
                norm_stats(dve, chain, [zw[:, j, :] for j in range(BPT)], stats, mv, rstd, tmp4, met_dve)
                for j in range(BPT):
                    dve.tensor_scalar(zw[:, j, :], zw[:, j, :], mv[:, j, 0:1], rstd[:, j:j + 1],
                                      ALU.subtract, ALU.mult).then_inc(g_norm.sem, 1)

            def grp_tile_dve(t, b, first=False, final=False):
                grp_shift(t)
                if not final:
                    grp_drain(t + 1, 1 - b, (0, 1))
                grp_probs(t)
                if not final:
                    grp_drain(t + 1, 1 - b, (2, 3, 4))
                grp_weights(t)
                if not first:
                    grp_keep_logits(t - 1)
                grp_norm(t)

            dve.wait_ge(wb_zero, 1)
            dve.wait_ge(consts_ready, 3)
            grp_drain(0, 0, range(GU))
            grp_tile_dve(0, 0, first=True)
            with dve.Fori(0, NT // 2 - 1) as i:
                grp_tile_dve(2 * i + 1, 1)
                grp_tile_dve(2 * i + 2, 0)
            grp_tile_dve(last, 1, final=True)
            sh_low(dve, FIRST, 0)
            grp_keep_logits(last)

            ch = Chain(dve, r_chain, 0)

            def step(ins):
                ch(ins)
                ch.join()

            def over_e(x):
                return x.unsqueeze(2).broadcast_to([P, NB, NE])

            def over_b(x):
                return x.unsqueeze(1).broadcast_to([P, NB, NE])

            top, total, m1, i1, m2, i2, p1, p2 = r1
            dve.wait_ge(g_lgc.sem, g_lgc.done(last))
            dve.wait_ge(g_h2.sem, g_h2.done(last))
            step(dve.tensor_reduce(top, LG, AX, ALU.max))
            step(dve.tensor_tensor(R[0], LG, over_e(top), ALU.subtract))
            dve.wait_ge(r_exp, 1)
            step(dve.tensor_reduce(total, R[1], AX, ALU.add))
            step(dve.reciprocal(total, total))
            step(dve.tensor_tensor(R[1], R[1], over_e(total), ALU.mult))
            scores, one1, one2 = R[1], R[2], R[3]
            for src, m, index, one in ((scores, m1, i1, one1), (R[6], m2, i2, one2)):
                if one is one2:
                    step(dve.scalar_tensor_tensor(out=R[6], in0=one1, scalar=-2.0, in1=scores, op0=ALU.mult, op1=ALU.add))
                step(dve.tensor_reduce(m, src, AX, ALU.max))
                step(dve.tensor_tensor(R[5], src, over_e(m), ALU.is_equal))
                step(dve.scalar_tensor_tensor(out=R[0], in0=R[5], scalar=-float(NE), in1=over_b(c("experts")),
                                              op0=ALU.mult, op1=ALU.add))
                step(dve.tensor_reduce(index, R[0], AX, ALU.min))
                step(dve.tensor_tensor(one, R[0], over_e(index), ALU.is_equal))
            step(dve.tensor_tensor(R[7], one1, one2, ALU.add))
            src, dst, s = R[7], R[4], 1
            while s < NB:
                ch(dve.tensor_copy(dst[:, 0:s, :], src[:, 0:s, :]))
                step(dve.tensor_tensor(dst[:, s:NB, :], src[:, s:NB, :], src[:, 0:NB - s, :], ALU.add))
                src, dst, s = dst, (R[6] if dst is R[4] else R[4]), 2 * s
            assert src is R[4]
            dve.tensor_tensor(R[5], R[4], R[7], ALU.subtract).then_inc(r_mask, 1)
            dve.wait_ge(r_pos, 1)
            ch(dve.tensor_copy(R[0], PS[:, 0, :].rearrange("p (b n) -> p b n", b=NB)))
            step(dve.tensor_scalar(re[0].bitcast(I32), PS[:, 1, 0:NE], float(P - 1), None, ALU.add))
            dve.sem_inc(r_read, 1)
            step(dve.tensor_scalar(re[1].bitcast(I32), re[0].bitcast(I32), 7, None, ALU.arith_shift_right))
            step(dve.tensor_copy(re[2], re[1].bitcast(I32)))
            src, dst, s = re[2], re[3], 1
            while s < NE:
                ch(dve.tensor_copy(dst[:, 0:s], src[:, 0:s]))
                step(dve.tensor_tensor(dst[:, s:NE], src[:, s:NE], src[:, 0:NE - s], ALU.add))
                src, dst, s = dst, (re[4] if dst is re[3] else re[3]), 2 * s
            ends = src
            step(dve.tensor_tensor(re[5], ends, re[2], ALU.subtract))
            step(dve.tensor_scalar(re[6], re[5], float(P), None, ALU.mult))
            step(dve.tensor_tensor(R[0], R[0], over_b(re[6]), ALU.add))
            for s, (one, place) in enumerate(((one1, p1), (one2, p2))):
                step(dve.tensor_tensor(R[6], one, R[0], ALU.mult))
                step(dve.tensor_reduce(place, R[6], AX, ALU.add))
                step(dve.tensor_copy(posi[:, s, :], place))
            ch(dve.tensor_copy(H2X[:, :, D], m1))
            ch(dve.tensor_copy(H2X[:, :, D + 1], m2))
            ch(dve.tensor_scalar(H2X[:, :, D + 2], i1, float(NE), None, ALU.add))
            ch(dve.tensor_copy(H2X[:, :, D + 3], c("token")))
            step(dve.tensor_tensor(tmap, ends.unsqueeze(1).broadcast_to([P, ET, NE]),
                                   c("tiles").unsqueeze(2).broadcast_to([P, ET, NE]), ALU.is_le))
            step(dve.tensor_reduce(emapf, tmap, AX, ALU.add))
            step(dve.tensor_scalar(emapf, emapf, float(NE - 1), None, ALU.min))
            step(dve.tensor_scalar(need_f, emapf, float(NE - LATE), float(16 * LATE), ALU.is_ge, ALU.mult))
            step(dve.tensor_scalar(need, need_f, 16.0, None, ALU.add))
            dve.tensor_copy(emap, emapf).then_inc(r_done, 1)

            def sh_hidden(t, m):
                n = SC * t + m
                dve.wait_ge(s_silu.sem, s_silu.done(n))
                dve.wait_ge(s_up.sem, s_up.done(n))
                dve.wait_ge(s_dn.sem, s_dn.recycled(n))
                dve.tensor_tensor(gg[:, m % 2, :], sil[:, m % 2, :], PS[:, 3 + 2 * (m % 2), :], ALU.mult)\
                    .then_inc(s_gg.sem, 1)

            def sh_sum(t):
                dve.wait_ge(s_dn.sem, s_dn.done(SC * t + SC - 1))
                dve.wait_ge(s_acc, 16 + 16 * t)
                for g in range(2):
                    dve.tensor_tensor(zo[:, 2 * g:2 * g + 2, :], two(6 + g), H2X[:, bass.ds(t * BPT + 2 * g, 2), 0:D],
                                      ALU.add).then_inc(s_z.sem, 1)

            def sh_tile_dve(t, b, more=True):
                for m in range(SC):
                    sh_hidden(t, m)
                    if m == SC // 2 and more:
                        sh_low(dve, t + 1, 1 - b)
                sh_sum(t)

            sh_low(dve, 1, 1)
            with dve.Fori(0, NT // 2 - 1) as i:
                sh_tile_dve(2 * i + 1, 1)
                sh_tile_dve(2 * i + 2, 0)
            sh_tile_dve(last, 1, False)

            ch = Chain(dve, gates_ready, 0)
            dve.wait_ge(behind_in, 16)
            ch(dve.tensor_tensor(gates, behind_rows[:, :, 2], emapf, ALU.is_equal))
            ch(dve.tensor_tensor(gates2, behind_rows[:, :, 2], emapf, ALU.not_equal))
            ch(dve.tensor_copy(tokens.bitcast(I32), behind_rows[:, :, 3]))
            ch.join()
            ch(dve.tensor_tensor(gates, gates, behind_rows[:, :, 0], ALU.mult))
            ch(dve.tensor_tensor(gates2, gates2, behind_rows[:, :, 1], ALU.mult))
            ch.join()
            ch(dve.tensor_tensor(gates, gates, gates2, ALU.add))
            ch.join()

            def ex_hidden(j, b):
                dve.wait_ge(e_silu.sem, e_silu.done(j))
                dve.wait_ge(e_h3.sem, e_h3.done(j))
                dve.wait_ge(e_y.sem, e_y.recycled(j))
                dve.tensor_tensor(eg[:, b, :], esil[:, b, :], PS[:, 2 + b, :], ALU.mult).then_inc(e_g.sem, 1)

            def ex_rows(j, b):
                dve.wait_ge(e_added.sem, e_added.recycled(j))
                dve.tensor_copy(egate[:, b:b + 1], gates[:, bass.ds(j, 1)]).then_inc(e_gate.sem, 1)
                dve.tensor_copy(tokidx[:, b:b + 1], tokens.bitcast(I32)[:, bass.ds(j, 1)]).then_inc(e_gate.sem, 1)
                dve.wait_ge(e_y.sem, e_y.done(j))
                dve.wait_ge(e_gate.sem, e_gate.done(j))
                dve.tensor_scalar(ey[:, b, :], PS[:, 6 + b, 0:D], egate[:, b:b + 1], None, ALU.mult)\
                    .then_inc(e_ys.sem, 1)

            ex_hidden(0, 0)
            with dve.Fori(0, (ET - 1) // 2) as i:
                ex_hidden(2 * i + 1, 1)
                ex_rows(2 * i, 0)
                ex_hidden(2 * i + 2, 0)
                ex_rows(2 * i + 1, 1)
            ex_rows(ET - 1, 0)

            for g in range(NT // FG):
                chain = Chain(dve, f_chain, N_FIN * g)
                dve.wait_ge(f_sum, FG * g + FG)
                norm_stats(dve, chain, [fin[:, FG * g + j // BPT, j % BPT, :] for j in range(FG * BPT)], fstats, fmv[g],
                           frstd[g], ftmp, met_dve)
                chain(dve.scalar_tensor_tensor(out=fshift[g], in0=fmv[g][:, :, 0], scalar=-1.0, in1=frstd[g],
                                               op0=ALU.mult, op1=ALU.mult))
                chain.join()
                dve.sem_inc(f_norm, 1)
                if g == NT // FG - 1:
                    for j in range(BPT):
                        dve.tensor_scalar(fout[:, FG * g, j, :], fin[:, FG * g, j, :], fmv[g][:, j, 0:1],
                                          frstd[g][:, j:j + 1], ALU.subtract, ALU.mult).then_inc(f_out[2], 1)

        @block.gpsimd
        def _(pool):
            for s in (em_mul, em_tok, ffs[0]["x"], ffs[1]["x"], w_y, w_norm, g_hs, g_h2, e_added):
                s.start(pool)
            pool.wait_ge(late_in, 64)
            pool.tensor_tensor(bias_pe, rows5[:, 2, :], c("pe"), ALU.add).then_inc(bias_ready, 1)
            pool.wait_ge(bias_ready, 1)

            def over_j(x):
                return x.unsqueeze(1).broadcast_to([P, BPT, D])

            with pool.Fori(0, NT // 2) as i:
                for b in range(2):
                    t = 2 * i + b
                    pool.wait_ge(em_norm.sem, em_norm.done(t))
                    pool.tensor_tensor(xw[:, b, :, :], xw[:, b, :, :], over_j(rows5[:, 1, :]), ALU.mult)\
                        .then_inc(em_mul.sem, 1)
                    pool.wait_ge(em_mul.sem, em_mul.done(t))
                    pool.tensor_tensor(xw[:, b, :, :], xw[:, b, :, :], over_j(bias_pe), ALU.add)\
                        .then_inc(em_tok.sem, 1)
            def split_all(s):
                pool.wait_ge(s["x"].sem, s["x"].done(0))
                split_x(pool, s, 1, 1, first=True)
                with pool.Fori(1, NT // 2) as i:
                    for b in range(2):
                        split_x(pool, s, 2 * i + b, b)

            pool.wait_ge(em_xt.sem, em_xt.done(last))
            split_all(ffs[0])

            def win_copy_y(t, b, k):
                pool.tensor_copy(ys[0:KROWS[k], b, k, :], YT[0:KROWS[k], k, bass.ds(t * TT, TT)]).then_inc(w_y.sem, 1)

            def win_normalise(pair, p):
                pool.wait_ge(w_rs.sem, w_rs.done(pair))
                e = E[:, p % 2, :].rearrange("p (h n) -> p h n", h=NH)
                pool.tensor_tensor(e, e, sm12[:, p % 2, :].unsqueeze(2).broadcast_to([P, NH, WIN]), ALU.mult)\
                    .then_inc(w_norm.sem, 1)

            def win_tile_steps(t, b, more=True):
                win_normalise(4 * t, 0)
                if more:
                    win_copy_y(t + 2, b, 0)
                win_normalise(4 * t + 1, 1)
                if more:
                    win_copy_y(t + 2, b, 1)
                win_normalise(4 * t + 2, 2)
                win_normalise(4 * t + 3, 3)

            for b in range(2):
                pool.wait_ge(ffs[0]["out"].sem, ffs[0]["out"].done(b))
                for k in range(2):
                    win_copy_y(b, b, k)
            pool.wait_ge(ffs[0]["out"].sem, ffs[0]["out"].done(last))
            pool.memset(vbd, 0.0).then_inc(w_zero, 1)
            with pool.Fori(0, NT // 2 - 1) as i:
                for b in range(2):
                    win_tile_steps(2 * i + b, b)
            win_tile_steps(last - 1, 0, False)
            win_tile_steps(last, 1, False)
            for u in range(2):
                pool.wait_ge(*win_item_proj(NT // 2 - 1, 1, u, True).drained())
            split_all(ffs[1])

            def grp_copy_h(t, b, first=False):
                if not first:
                    pool.wait_ge(g_z.sem, g_z.done(t - 2))
                for k in range(2):
                    pool.tensor_copy(hs[0:KROWS[k], b, k, :], XT[0:KROWS[k], k, bass.ds(t * TT, TT)])\
                        .then_inc(g_hs.sem, 1)

            def grp_keep(t):
                pool.wait_ge(g_norm.sem, g_norm.done(t))
                pool.tensor_copy(H2X[:, bass.ds(t * BPT, BPT), 0:D], zw).then_inc(g_h2.sem, 1)

            for b in range(2):
                pool.wait_ge(ffs[1]["out"].sem, ffs[1]["out"].done(b))
                grp_copy_h(b, b, first=True)
            pool.wait_ge(ffs[1]["out"].sem, ffs[1]["out"].done(last))
            pool.memset(wb, 0.0).then_inc(wb_zero, 1)
            with pool.Fori(0, NT // 2 - 1) as i:
                for b in range(2):
                    grp_copy_h(2 * i + b + 2, b)
                    grp_keep(2 * i + b)
            grp_keep(last - 1)
            grp_keep(last)

            for m in range(SC):
                pool.wait_ge(s_silu.sem, s_silu.done(m))
                pool.wait_ge(s_dn.sem, s_dn.recycled(m))
                pool.tensor_tensor(gg[:, m % 2, :], sil[:, m % 2, :], up3, ALU.mult).then_inc(s_gg.sem, 1)
            pool.wait_ge(first_down, 1)
            for g in range(2):
                pool.tensor_tensor(zo[:, 2 * g:2 * g + 2, :], zo[:, 2 * g:2 * g + 2, :], H2X[:, 2 * g:2 * g + 2, 0:D],
                                   ALU.add).then_inc(s_z.sem, 1)

            pool.wait_ge(r_done, 1)
            pool.wait_ge(table_filled, 16)
            for t in range(NT):
                for blk in range(BPT * t, BPT * t + BPT):
                    for s in range(2):
                        pool.indirect_dma_start(XS, bass.IndirectOffsetOnAxis(ap=posi[:, s, blk:blk + 1], axis=0),
                                                H2X[:, blk, :], None).then_inc(scat[t % 2], 16)
                if t >= 1:
                    pool.wait_ge(scat[(t - 1) % 2], 32 * BPT * ((t - 1) // 2 + 1))
                    pool.sem_inc(scattered, 1)
            pool.wait_ge(scat[last % 2], 32 * BPT * (last // 2 + 1))
            pool.sem_inc(scattered, 1)
            pool.dma_start(behind_rows, XS.rearrange("(t p) n -> p t n", p=P)[:, :, D:ROW]).then_inc(behind_in, 16)

            pool.wait_ge(s_acc, 16 + 16 * NT)
            pool.wait_ge(dummies_filled, 32)

            def ex_add(j, b):
                pool.wait_ge(e_ys.sem, e_ys.done(j))
                pool.sem_inc(met_pool, 1)
                pool.indirect_dma_start((ACC, ACC1)[b], bass.IndirectOffsetOnAxis(ap=tokidx[:, b:b + 1], axis=0),
                                        ey[:, b, :], None, compute_op=ALU.add).then_inc(e_acc[b], 16)

            def ex_landed(b, i):
                pool.wait_ge(e_acc[b], 16 * (i + 1))
                pool.sem_inc(e_added.sem, 1)

            ex_add(0, 0)
            with pool.Fori(0, (ET - 1) // 2) as i:
                ex_add(2 * i + 1, 1)
                ex_landed(0, i)
                ex_add(2 * i + 2, 0)
                ex_landed(1, i)
            ex_landed(0, ET // 2)

            for t in range(NT):
                pool.wait_ge(f_in[t], 32)
                pool.tensor_tensor(fin[:, t, :, :], fin[:, t, :, :], fin1[:, t, :, :], ALU.add).then_inc(f_sum, 1)


def _constants():
    a = np.zeros((P, CONST), np.float32)
    p = np.arange(P)
    a[:, _C["ident"]] = np.eye(P)
    a[:, _C["before"]] = p[:, None] < p[None, :]
    a[:, _C["ones"]] = 1
    a[:, _C["kmask"]] = p[:, None] // DH == np.arange(HM)[None, :]
    pos = np.arange(WIN, dtype=np.float32)[:, None]
    i = np.arange(D // 2, dtype=np.float32)[None, :]
    angle = pos / np.power(np.float32(10000.0), np.float32(2.0) * i / np.float32(D))
    pe = np.zeros((WIN, D), np.float32)
    pe[:, 0::2], pe[:, 1::2] = np.sin(angle), np.cos(angle)
    a[:, _C["pe"]] = np.concatenate([pe, pe])
    a[:, _C["experts"]] = np.arange(NE)
    a[:, _C["tiles"]] = np.arange(ET)
    a[:, _C["padrow"]][:, D + 2] = -1
    a[:, _C["padrow"]][:, D + 3] = TOK + p
    a[:, _C["token"]] = np.arange(NB)[None, :] * P + p[:, None]
    return a


def _split(v):
    out = np.zeros((P, 2), v.dtype)
    out[:, 0], out[:DT, 1] = v[:DM], v[DM:]
    return out


def _arrays(x, L0_tok_patch_w, L0_tok_patch_b, L0_tok_ln_g, L0_tok_ln_b, L0_tok_qkv_w, L0_tok_qkv_b, L0_tok_proj_w,
            L0_tok_proj_b, L0_tok_ff1_w, L0_tok_ff1_b, L0_tok_ff2_w, L0_tok_ff2_b, L0_attn_W_qkv, L0_attn_b_qkv,
            L0_attn_W_proj, L0_attn_b_proj, L0_attn_W_gp, L0_attn_alpha, L0_ffn_gate_w, L0_ffn_w1, L0_ffn_w2,
            L0_ffn_w3, L0_ffn_sw1, L0_ffn_sw2, L0_ffn_sw3):
    d = {"const": _constants()}
    a = x.reshape(IMAGES, CH, GRID, PATCH, GRID, PATCH).transpose(1, 3, 5, 0, 2, 4)
    d["patches"] = a.reshape(PK, P, NT, TT).transpose(2, 1, 0, 3)
    d["patch_w"] = L0_tok_patch_w.reshape(D, PK, P).transpose(2, 1, 0)
    d["rows5"] = np.concatenate([L0_tok_patch_b, L0_tok_ln_g, L0_tok_ln_b, L0_attn_b_qkv[2 * D:], L0_attn_b_proj])[None]
    d["alpha"] = L0_attn_alpha[None]
    def qk_columns(b):
        q, k = b[0:D], b[D:2 * D]
        return np.stack([q[:DM], k[:DM], np.concatenate([q[DM:], k[DM:]])], axis=1)

    d["bcols"] = np.concatenate(
        [L0_tok_ff1_b.reshape(FC, P).T, _split(L0_tok_ff2_b), qk_columns(L0_tok_qkv_b), _split(L0_tok_qkv_b[2 * D:]),
         _split(L0_tok_proj_b), qk_columns(L0_attn_b_qkv)], axis=1)
    d["ff1_w"], d["ff2_w"] = L0_tok_ff1_w, L0_tok_ff2_w.reshape(FC, P, D).transpose(1, 0, 2)
    d["proj_w"], d["proj2_w"] = L0_tok_proj_w, L0_attn_W_proj
    for name, w in (("qkv_w", L0_tok_qkv_w), ("qkv2_w", L0_attn_W_qkv)):
        q, k, v = w[:, 0:D], w[:, D:2 * D], w[:, 2 * D:]
        d[name] = np.concatenate([q[:, :DM], k[:, :DM], q[:, DM:], k[:, DM:], v], axis=1)
    d["gp_w"], d["gate_w"] = L0_attn_W_gp, L0_ffn_gate_w.T
    def up(w1, w3):
        w1, w3 = np.swapaxes(w1, -1, -2), np.swapaxes(w3, -1, -2)
        return [w1[..., :DM, :], w3[..., :DM, :], np.concatenate([w1[..., DM:, :], w3[..., DM:, :]], axis=-2)]

    def down(w2):
        w2 = np.swapaxes(w2, -1, -2)
        n = w2.shape[-2] // P
        w2 = np.swapaxes(w2.reshape(*w2.shape[:-2], n, P, D), -2, -3)
        return [w2.reshape(*w2.shape[:-2], n * D)]

    d["shared"] = np.concatenate(up(L0_ffn_sw1, L0_ffn_sw3) + down(L0_ffn_sw2), axis=-1)
    d["experts"] = np.concatenate(up(L0_ffn_w1, L0_ffn_w3) + down(L0_ffn_w2), axis=-1)
    return {n: np.ascontiguousarray(v) for n, v in d.items()}


def kernel(**inputs):
    import concourse.bacc as _bacc
    from concourse.bass_utils import run_bass_kernel_spmd as _run

    arrays = {f"in_{n}": a for n, a in _arrays(**{n: np.asarray(a) for n, a in inputs.items()}).items()}
    nc = _bacc.Bacc("TRN2", target_bir_lowering=False, num_devices=1)
    d = {n[3:]: nc.dram_tensor(n, a.shape, mybir.dt.from_np(a.dtype), kind="ExternalInput").ap()
         for n, a in arrays.items()}
    out = nc.dram_tensor("out_dram", (TOK, D), F32, kind="ExternalOutput").ap()
    build(nc, d, out)
    r = _run(nc, [arrays], core_ids=[0])
    return r.results[0]["out_dram"].reshape(IMAGES, WIN, D)
```
